# Optimizing a Trainium2 kernel written in Bass

```python
import numpy as np
import jax
import jax.numpy as jnp

def _softmax(x, axis=-1):
    return jax.nn.softmax(x, axis=axis)

def _gelu(x):
    return jax.nn.gelu(x, approximate=True)

def _silu(x):
    return jax.nn.silu(x)

def _sigmoid(x):
    return jax.nn.sigmoid(x)

def _layernorm(x, axis=-1, eps=1e-05):
    m = jnp.mean(x, axis=axis, keepdims=True)
    v = jnp.var(x, axis=axis, keepdims=True)
    return (x - m) / jnp.sqrt(v + eps)

def _scatter_add(tgt, idx, src, axis=0):
    return tgt.at[idx].add(src)

def _segment_sum(src, seg, n):
    return jax.ops.segment_sum(src, seg, n)
kernel_name = 'mk_gnn_ffn_d2_gnn_r32_c00cdd'

def setup_inputs(seed: int=0):
    np.random.seed(seed)
    _w = jnp.asarray

    def _rec_inputs():
        import jax
        import jax.numpy as jnp
        _gk = jax.random.key(seed)
        x = -0.0002117 + 1 * jax.random.normal(jax.random.fold_in(_gk, 1), (3125, 256), jnp.float32)
        src = jax.random.randint(jax.random.fold_in(_gk, 2), (50000,), 0, 3125, jnp.int32)
        dst = jax.random.randint(jax.random.fold_in(_gk, 3), (50000,), 0, 3125, jnp.int32)
        _o = jnp.argsort(dst, stable=True)
        src = src[_o]
        dst = dst[_o]
        return (x, src, dst)
    x, src, dst = _rec_inputs()

    def _L0_gnn_setup():
        import jax, jax.numpy as jnp
        import numpy as np
        N_NODES = 3125
        N_EDGES = 50000
        D_IN = 256
        HEADS = 8
        D_HEAD = 32
        NEG_SLOPE = 0.2
        BN_EPS = 1e-05
        key = jax.random.key(seed)
        ks = jax.random.split(key, 8)
        x = jax.random.normal(ks[0], (N_NODES, D_IN), dtype=jnp.float32)
        edge_index = jax.random.randint(ks[1], (2, N_EDGES), 0, N_NODES, dtype=jnp.int32)
        W = jax.random.normal(ks[2], (D_IN, HEADS * D_HEAD), dtype=jnp.float32) / np.sqrt(D_IN)
        att_src = jax.random.normal(ks[3], (HEADS, D_HEAD), dtype=jnp.float32) / np.sqrt(D_HEAD)
        att_dst = jax.random.normal(ks[4], (HEADS, D_HEAD), dtype=jnp.float32) / np.sqrt(D_HEAD)
        bias = jax.random.normal(ks[5], (HEADS * D_HEAD,), dtype=jnp.float32) * 0.01
        gamma = jnp.ones((HEADS * D_HEAD,), dtype=jnp.float32)
        beta = jnp.zeros((HEADS * D_HEAD,), dtype=jnp.float32)
        return {'x': x, 'edge_index': edge_index, 'W': W, 'att_src': att_src, 'att_dst': att_dst, 'bias': bias, 'gamma': gamma, 'beta': beta}
    _L0_gnn_all = _L0_gnn_setup()
    _L0_gnn_in = {k: v for k, v in _L0_gnn_all.items() if k in ('W', 'att_src', 'att_dst', 'bias', 'gamma', 'beta')}
    del _L0_gnn_all

    def _L0_ffn_setup():
        import jax, jax.numpy as jnp
        import numpy as np
        N_EXPERTS = 8
        TOP_K = 2
        key = jax.random.key(seed)
        ks = jax.random.split(key, 5)
        B, T, C, E, H = (8, 64, 256, 8, 682)
        scale = 1.0 / np.sqrt(C)
        return {'x': jax.random.normal(ks[0], (B, T, C), dtype=jnp.float32), 'router_w': jax.random.normal(ks[1], (E, C), dtype=jnp.float32) * scale, 'w1': jax.random.normal(ks[2], (E, H, C), dtype=jnp.float32) * scale, 'w2': jax.random.normal(ks[3], (E, C, H), dtype=jnp.float32) * (1.0 / np.sqrt(H)), 'w3': jax.random.normal(ks[4], (E, H, C), dtype=jnp.float32) * scale}
    _L0_ffn_all = _L0_ffn_setup()
    _L0_ffn_in = {k: v for k, v in _L0_ffn_all.items() if k in ('router_w', 'w1', 'w2', 'w3')}
    del _L0_ffn_all

    def _L1_gnn_setup():
        import jax, jax.numpy as jnp
        import numpy as np
        N_NODES = 3125
        N_EDGES = 50000
        IN_DIM = 256
        OUT_DIM = 256
        key = jax.random.key(seed)
        k1, k2, k3 = jax.random.split(key, 3)
        x = jax.random.normal(k1, (N_NODES, IN_DIM), dtype=jnp.float32)
        limit = 0.1 * np.sqrt(6.0 / (IN_DIM + OUT_DIM))
        W = jax.random.uniform(k2, (OUT_DIM, IN_DIM), dtype=jnp.float32, minval=-limit, maxval=limit)
        b = jnp.zeros((OUT_DIM,), dtype=jnp.float32)
        edge_index = jax.random.randint(k3, (2, N_EDGES), 0, N_NODES, dtype=jnp.int64)
        return {'x': x, 'W': W, 'b': b, 'edge_index': edge_index}
    _L1_gnn_all = _L1_gnn_setup()
    _L1_gnn_in = {k: v for k, v in _L1_gnn_all.items() if k in ('W', 'b')}
    del _L1_gnn_all

    def _L1_ffn_setup():
        import jax, jax.numpy as jnp
        import numpy as np
        DIM = 256
        H = 8
        D = 64
        G = 64
        INNER = H * D
        SCALE = D ** (-0.5)
        key = jax.random.key(seed)
        ks = jax.random.split(key, 12)
        B, N = (4, 512)
        x = jax.random.normal(ks[0], (B, N, DIM), dtype=jnp.float32)
        s = lambda fan_in: 1.0 / np.sqrt(fan_in)
        W_fx = jax.random.normal(ks[1], (DIM, INNER), dtype=jnp.float32) * s(DIM)
        b_fx = jnp.zeros((INNER,), dtype=jnp.float32)
        W_x = jax.random.normal(ks[2], (DIM, INNER), dtype=jnp.float32) * s(DIM)
        b_x = jnp.zeros((INNER,), dtype=jnp.float32)
        A = jax.random.normal(ks[3], (G, D), dtype=jnp.float32)
        Q, _ = jnp.linalg.qr(A.T)
        W_slice = Q[:, :G].astype(jnp.float32)
        b_slice = jnp.zeros((G,), dtype=jnp.float32)
        W_q = jax.random.normal(ks[4], (D, D), dtype=jnp.float32) * s(D)
        W_k = jax.random.normal(ks[5], (D, D), dtype=jnp.float32) * s(D)
        W_v = jax.random.normal(ks[6], (D, D), dtype=jnp.float32) * s(D)
        W_out = jax.random.normal(ks[7], (INNER, DIM), dtype=jnp.float32) * s(INNER)
        b_out = jnp.zeros((DIM,), dtype=jnp.float32)
        temperature = jnp.ones((1, H, 1, 1), dtype=jnp.float32) * 0.5
        return {'x': x, 'W_fx': W_fx, 'b_fx': b_fx, 'W_x': W_x, 'b_x': b_x, 'W_slice': W_slice, 'b_slice': b_slice, 'W_q': W_q, 'W_k': W_k, 'W_v': W_v, 'W_out': W_out, 'b_out': b_out, 'temperature': temperature}
    _L1_ffn_all = _L1_ffn_setup()
    _L1_ffn_in = {k: v for k, v in _L1_ffn_all.items() if k in ('W_fx', 'b_fx', 'W_x', 'b_x', 'W_slice', 'b_slice', 'W_q', 'W_k', 'W_v', 'W_out', 'b_out', 'temperature')}
    del _L1_ffn_all
    return {'x': x, 'src': src, 'dst': dst, 'L0_gnn_W': _L0_gnn_in['W'], 'L0_gnn_att_src': _L0_gnn_in['att_src'], 'L0_gnn_att_dst': _L0_gnn_in['att_dst'], 'L0_gnn_bias': _L0_gnn_in['bias'], 'L0_gnn_gamma': _L0_gnn_in['gamma'], 'L0_gnn_beta': _L0_gnn_in['beta'], 'L0_ffn_router_w': _L0_ffn_in['router_w'], 'L0_ffn_w1': _L0_ffn_in['w1'], 'L0_ffn_w2': _L0_ffn_in['w2'], 'L0_ffn_w3': _L0_ffn_in['w3'], 'L1_gnn_W': _L1_gnn_in['W'], 'L1_gnn_b': _L1_gnn_in['b'], 'L1_ffn_W_fx': _L1_ffn_in['W_fx'], 'L1_ffn_b_fx': _L1_ffn_in['b_fx'], 'L1_ffn_W_x': _L1_ffn_in['W_x'], 'L1_ffn_b_x': _L1_ffn_in['b_x'], 'L1_ffn_W_slice': _L1_ffn_in['W_slice'], 'L1_ffn_b_slice': _L1_ffn_in['b_slice'], 'L1_ffn_W_q': _L1_ffn_in['W_q'], 'L1_ffn_W_k': _L1_ffn_in['W_k'], 'L1_ffn_W_v': _L1_ffn_in['W_v'], 'L1_ffn_W_out': _L1_ffn_in['W_out'], 'L1_ffn_b_out': _L1_ffn_in['b_out'], 'L1_ffn_temperature': _L1_ffn_in['temperature']}

def reference(x, src, dst, L0_gnn_W, L0_gnn_att_src, L0_gnn_att_dst, L0_gnn_bias, L0_gnn_gamma, L0_gnn_beta, L0_ffn_router_w, L0_ffn_w1, L0_ffn_w2, L0_ffn_w3, L1_gnn_W, L1_gnn_b, L1_ffn_W_fx, L1_ffn_b_fx, L1_ffn_W_x, L1_ffn_b_x, L1_ffn_W_slice, L1_ffn_b_slice, L1_ffn_W_q, L1_ffn_W_k, L1_ffn_W_v, L1_ffn_W_out, L1_ffn_b_out, L1_ffn_temperature):
    import jax
    import jax.numpy as jnp

    def _L0_gnn_ref(x, edge_index, W, att_src, att_dst, bias, gamma, beta):
        import jax, jax.numpy as jnp
        import numpy as np
        N_NODES = 3125
        N_EDGES = 50000
        D_IN = 256
        HEADS = 8
        D_HEAD = 32
        NEG_SLOPE = 0.2
        BN_EPS = 1e-05
        N = x.shape[0]
        H, D = att_src.shape
        xh = (x @ W).reshape(N, H, D)
        a_src = jnp.einsum('nhd,hd->nh', xh, att_src)
        a_dst = jnp.einsum('nhd,hd->nh', xh, att_dst)
        loops = jnp.arange(N, dtype=edge_index.dtype)
        src = jnp.concatenate([edge_index[0], loops])
        dst = jnp.concatenate([edge_index[1], loops])
        e = jax.nn.leaky_relu(a_src[src] + a_dst[dst], NEG_SLOPE)
        m = jax.ops.segment_max(e, dst, num_segments=N)
        e = jnp.exp(e - m[dst])
        denom = jax.ops.segment_sum(e, dst, num_segments=N)
        alpha = e / denom[dst]
        msg = xh[src] * alpha[:, :, None]
        out = jax.ops.segment_sum(msg, dst, num_segments=N).reshape(N, H * D) + bias
        mean = jnp.mean(out, axis=0)
        var = jnp.var(out, axis=0)
        out = (out - mean) * jax.lax.rsqrt(var + BN_EPS) * gamma + beta
        return out + x

    def _L0_ffn_ref(x, router_w, w1, w2, w3):
        import jax, jax.numpy as jnp
        import numpy as np
        N_EXPERTS = 8
        TOP_K = 2
        B, T, C = x.shape
        flat = x.reshape(-1, C)
        logits = flat @ router_w.T
        probs = jax.nn.softmax(logits, axis=-1)
        topk_probs, topk_idx = jax.lax.top_k(probs, TOP_K)
        topk_probs = topk_probs / (jnp.sum(topk_probs, axis=-1, keepdims=True) + 1e-09)
        onehot = jax.nn.one_hot(topk_idx, N_EXPERTS, dtype=flat.dtype)
        gates = jnp.einsum('nk,nke->ne', topk_probs, onehot)
        h1 = jnp.einsum('nc,ehc->neh', flat, w1)
        h3 = jnp.einsum('nc,ehc->neh', flat, w3)
        h = jax.nn.silu(h1) * h3
        y = jnp.einsum('neh,ech->nec', h, w2)
        out = jnp.einsum('ne,nec->nc', gates, y)
        return out.reshape(B, T, C)

    def _L1_gnn_ref(x, W, b, edge_index):
        import jax, jax.numpy as jnp
        import numpy as np
        N_NODES = 3125
        N_EDGES = 50000
        IN_DIM = 256
        OUT_DIM = 256
        num_nodes = x.shape[0]
        src, tgt = (edge_index[0], edge_index[1])
        xt = jnp.einsum('ni,oi->no', x, W) + b
        out = jax.ops.segment_sum(xt[src], tgt, num_segments=num_nodes)
        deg = jax.ops.segment_sum(jnp.ones_like(tgt, dtype=x.dtype), tgt, num_segments=num_nodes)
        out = out / (deg + 1.0)[:, None]
        return out

    def _L1_ffn_ref(x, W_fx, b_fx, W_x, b_x, W_slice, b_slice, W_q, W_k, W_v, W_out, b_out, temperature):
        import jax, jax.numpy as jnp
        import numpy as np
        DIM = 256
        H = 8
        D = 64
        G = 64
        INNER = H * D
        SCALE = D ** (-0.5)
        B, N, _ = x.shape
        fx_mid = (x @ W_fx + b_fx).reshape(B, N, H, D).transpose(0, 2, 1, 3)
        x_mid = (x @ W_x + b_x).reshape(B, N, H, D).transpose(0, 2, 1, 3)
        temp = jnp.clip(temperature, 0.1, 5.0)
        slice_weights = jax.nn.softmax((x_mid @ W_slice + b_slice) / temp, axis=-1)
        slice_norm = slice_weights.sum(axis=2)
        slice_token = jnp.einsum('bhnc,bhng->bhgc', fx_mid, slice_weights)
        slice_token = slice_token / (slice_norm[..., None] + 1e-05)
        q = slice_token @ W_q
        k = slice_token @ W_k
        v = slice_token @ W_v
        attn = jax.nn.softmax(jnp.einsum('bhgc,bhkc->bhgk', q, k) * SCALE, axis=-1)
        out_slice = jnp.einsum('bhgk,bhkc->bhgc', attn, v)
        out_x = jnp.einsum('bhgc,bhng->bhnc', out_slice, slice_weights)
        out_x = out_x.transpose(0, 2, 1, 3).reshape(B, N, INNER)
        return out_x @ W_out + b_out
    edge_index = jnp.stack([src, dst])
    x = x + _L0_gnn_ref(_layernorm(x, axis=-1), edge_index, L0_gnn_W, L0_gnn_att_src, L0_gnn_att_dst, L0_gnn_bias, L0_gnn_gamma, L0_gnn_beta)
    x = x + _L0_ffn_ref(_layernorm(x, axis=-1)[None], L0_ffn_router_w, L0_ffn_w1, L0_ffn_w2, L0_ffn_w3)[0]
    x = x + _L1_gnn_ref(_layernorm(x, axis=-1), L1_gnn_W, L1_gnn_b, edge_index)
    x = x + _L1_ffn_ref(_layernorm(x, axis=-1)[None], L1_ffn_W_fx, L1_ffn_b_fx, L1_ffn_W_x, L1_ffn_b_x, L1_ffn_W_slice, L1_ffn_b_slice, L1_ffn_W_q, L1_ffn_W_k, L1_ffn_W_v, L1_ffn_W_out, L1_ffn_b_out, L1_ffn_temperature)[0]
    return x

_drawn_inputs = setup_inputs


def setup_inputs(seed=0):
    import zlib

    import numpy as np

    out = dict(_drawn_inputs(seed))
    spreads = {'L0_gnn_gamma': (1.0, 0.2),
     'L0_gnn_beta': (0.0, 0.1),
     'L1_gnn_b': (0.0, 0.1),
     'L1_ffn_b_fx': (0.0, 0.1),
     'L1_ffn_b_x': (0.0, 0.8),
     'L1_ffn_b_slice': (0.0, 0.8),
     'L1_ffn_b_out': (0.0, 0.1),
     'L1_ffn_temperature': (0.5, 0.6)}
    factors = {'L0_gnn_bias': 8.0,
     'L1_gnn_W': 5.22,
     'L1_ffn_W_x': 8.0,
     'L1_ffn_W_slice': 8.0,
     'L1_ffn_W_q': 8.0,
     'L1_ffn_W_k': 8.0}
    for name, (base, spread) in spreads.items():
        noise = np.random.default_rng([zlib.crc32(name.encode()), seed]).standard_normal(out[name].shape)
        drawn = base * np.exp(spread * noise) if base else spread * noise
        out[name] = jnp.asarray(drawn.astype(out[name].dtype))
    for name, factor in factors.items():
        out[name] = (out[name] * factor).astype(out[name].dtype)
    return out
```

```python
from contextlib import ExitStack

import numpy as np
import concourse.bass as bass
from concourse import mybir

F32 = mybir.dt.float32
I32 = mybir.dt.int32
U32 = mybir.dt.uint32
ALU = mybir.AluOpType
ACT = mybir.ActivationFunctionType
AX = mybir.AxisListType.X

N, C, E = 3125, 256, 50000
P, NT = 125, 25
TB = 5
H, D = 8, 32
EP = 128
ET = 392
SB = 14
NB = ET // SB
Q, J = 98, 4
XW = C + H
RW = C + 2 * H
NO_ROW = ET * EP
NO_CHAIN = ET
BIG = 3e38
EPS = 1e-5


class Steps:

    def __init__(self, sem):
        self.sem, self.n, self.turn = sem, 0, None

    def __call__(self, eng, ins):
        ins.then_inc(self.sem, 1)
        self.n += 1
        eng.wait_ge(self.sem, self.n if self.turn is None else self.turn * self.k + self.n)

    def loop(self, turn, k):
        self.turn, self.k, self.first = turn, k, self.n

    def end(self, turns):
        assert self.n - self.first == self.k, (self.n - self.first, self.k)
        self.n, self.turn = self.first + self.k * turns, None


class Kernel:

    def __init__(self, nc, ctx, out, arrays):
        self.nc, self.ctx, self.out, self.a = nc, ctx, out, arrays
        self.opened = None
        self.steps = {e: Steps(self.sem(f"{e}_steps")) for e in ("pe", "act", "dve", "pool")}

    def sb(self, name, shape, dt=F32, ctx=None):
        return (ctx or self.ctx).enter_context(self.nc.sbuf_tensor(name, shape, dt))

    def sem(self, name):
        s = self.nc.semaphore(name)
        if self.opened is None:
            return self.ctx.enter_context(s)
        self.opened.append(self.layer.enter_context(s))
        return self.opened[-1]

    def gather_sem(self, name):
        return self.ctx.enter_context(self.nc.semaphore(name))

    def open_layer(self):
        self.opened, self.layer = [], ExitStack()

    def close_layer(self):
        with self.nc.Block() as block:

            @block.gpsimd
            def _(pool):
                for s in self.opened:
                    pool.sem_clear(s)
        self.layer.close()
        self.opened = None

    def dram(self, name, shape, dt=F32):
        return self.nc.dram_tensor(name, shape, dt, kind=SCRATCH).ap()


SCRATCH = "Internal"


def setup(k):
    k.ps = [k.ctx.enter_context(k.nc.psum_tensor(f"bank{i}", [128, 512], F32)) for i in range(8)]
    k.ident = k.sb("ident", [128, 128])
    k.ones = k.sb("ones", [128, 128])
    k.res = k.sb("res", [P, NT, C])
    k.stats = k.sb("stats", [P, NT, 6])
    k.mv = k.sb("mv", [P, NT, 2])
    k.rstd = k.sb("rstd", [P, NT])
    k.node = k.sb("node", [P, NT])
    k.deg = k.sb("deg", [P, NT])
    k.main_row = k.sb("main_row", [P, NT], I32)
    k.chain_row = k.sb("chain_row", [P, NT], I32)
    k.start_row = k.sb("start_row", [P, NT], I32)
    k.src_e = k.sb("src_e", [EP, ET], I32)
    k.dst_e = k.sb("dst_e", [EP, ET])
    k.fwd_e = k.sb("fwd_e", [EP, ET])
    k.bwd_e = k.sb("bwd_e", [EP, ET])
    k.joins = k.sb("joins", [128, ET])
    k.cont_q = k.sb("cont_q", [Q, J * EP])
    k.tile_dst = k.sb("tile_dst", [Q, J], I32)
    k.xh_tab = k.dram("xh_tab", [N, XW])
    k.adst_tab = k.dram("adst_tab", [N, H])
    k.adst_edge = k.dram("adst_edge", [ET * EP, H])
    k.gate = k.sb("gate", [P, 2, NT])
    k.place = k.sb("place", [P, 2, NT], I32)
    k.item_expert = k.sb("item_expert", [1, NI], I32)
    k.slot_token = k.sb("slot_token", [M, NI], I32)
    k.x1_tab, k.xn_tab, k.y_tab = k.dram("x1_tab", [N, C]), k.dram("xn_tab", [N, C]), k.dram("y_tab", [NI * M, C])
    k.dst_pad = k.dram("dst_pad", [ET * EP])
    k.start_tab = k.dram("start_tab", [N + 1])
    k.parts = k.dram("parts", [ET * EP + 1, RW])
    k.chains = k.dram("chains", [ET + 1, RW])


def index_phase(k):
    nc, st = k.nc, k.steps
    ctx = ExitStack()
    with ctx:
        sb = lambda n, s, d=F32: k.sb(n, s, d, ctx)
        srcq_i, dstq_i = sb("srcq_i", [Q, J * EP], I32), sb("dstq_i", [Q, J * EP], I32)
        srcq, dstq = sb("srcq", [Q, J * EP]), sb("dstq", [Q, J * EP])
        same = sb("same", [Q, J * EP + 1])
        first_b = sb("first_b", [128, ET])
        last_b = sb("last_b", [128, ET])
        trash = sb("trash", [P, ET])
        before = sb("before", [P, NT])
        tile = sb("tile", [P, NT])
        tile_i = sb("tile_i", [P, NT], I32)
        window = sb("window", [P, NT, EP])
        start, end, last = sb("start", [P, NT]), sb("end", [P, NT]), sb("last", [P, NT])
        last_i, has, t0, t1 = sb("last_i", [P, NT], I32), sb("has", [P, NT]), sb("t0", [P, NT]), sb("t1", [P, NT])
        total = sb("total", [1, 1])
        padded = k.sem("padded")
        edges_in = k.sem("edges_in")
        x_in = k.sem("x_in")
        consts = k.sem("consts")
        edges_f = k.sem("edges_f")
        pad_out = k.sem("pad_out")
        turned = k.sem("turned")
        ends_b = k.sem("ends_b")
        tiles_found = k.sem("tiles_found")
        windows_in = k.gather_sem("windows_in")
        starts_found = k.sem("starts_found")
        starts_out = k.sem("starts_out")
        ends_in = k.sem("ends_in")
        ready = k.sem("index_ready")
        k.x_in, k.consts = x_in, consts
        full = E // (J * EP)
        rest = E - full * J * EP

        block = ctx.enter_context(nc.Block())

        @block.sync
        def _(sp):
            sp.wait_ge(padded, 2)
            for a, t in ((k.a["dst"], dstq_i), (k.a["src"], srcq_i)):
                sp.dma_start(t[0:full, :], a[0:full * J * EP].rearrange("(q e) -> q e", e=J * EP)).then_inc(edges_in, 16)
                sp.dma_start(t[full:full + 1, 0:rest], a[full * J * EP:E].rearrange("(q e) -> q e", q=1)).then_inc(edges_in, 16)
            sp.dma_start(k.res[:, :, :], k.a["x"].rearrange("(p t) c -> p t c", p=P)).then_inc(x_in, 16)
            sp.wait_ge(edges_f, 1)
            sp.dma_start(k.dst_pad.rearrange("(q e) -> q e", q=Q), dstq[:, :]).then_inc(pad_out, 16)
            sp.wait_ge(starts_found, 1)
            sp.dma_start(k.start_tab[0:N].rearrange("(p t) -> p t", p=P), start[:, :]).then_inc(starts_out, 16)
            sp.dma_start(k.start_tab[N:N + 1].rearrange("(a b) -> a b", a=1), total[:, :]).then_inc(starts_out, 16)
            sp.wait_ge(starts_out, 32)
            sp.dma_start(end[:, :], k.start_tab[1:N + 1].rearrange("(p t) -> p t", p=P)).then_inc(ends_in, 16)

        @block.gpsimd
        def _(pool):
            me = st["pool"]
            nc.gpsimd.memset(srcq_i[:, :], 0).then_inc(padded, 1)
            nc.gpsimd.memset(dstq_i[:, :], N).then_inc(padded, 1)
            nc.gpsimd.memset(k.ones[:, :], 1.0)
            nc.gpsimd.memset(total[:, :], float(E))
            me(pool, nc.gpsimd.memset(k.ident[:, :], 0.0))
            nc.gpsimd.affine_select(out=k.ident[:, :], in_=k.ident[:, :], compare_op=ALU.not_equal, fill=1.0, base=0,
                                    pattern=[[-1, 128]], channel_multiplier=1)
            nc.gpsimd.iota(k.node[:, :], pattern=[[1, NT]], base=0, channel_multiplier=NT,
                           allow_small_or_imprecise_dtypes=True).then_inc(consts, 1)
            pool.wait_ge(tiles_found, 1)
            pool.wait_ge(pad_out, 16)
            for t in range(NT):
                pool.indirect_dma_start(out=window[:, t, :], out_offset=None, in_=k.dst_pad.rearrange("(a b) -> a b", b=EP),
                                        in_offset=bass.IndirectOffsetOnAxis(ap=tile_i[:, t:t + 1], axis=0)).then_inc(windows_in, 16)

        @block.tensor
        def _(pe):
            pe.wait_ge(edges_f, 4)
            pe.wait_ge(consts, 1)
            for b, t in enumerate((dstq, srcq, same, same)):
                for j in range(J):
                    at = j * EP + (b == 3)
                    last_mm = nc.tensor.transpose(k.ps[b][:, j * Q:(j + 1) * Q], t[:, at:at + EP], k.ident[0:Q, 0:Q])
                last_mm.then_inc(turned, 1)
            pe.wait_ge(ends_b, 1)
            nc.tensor.matmul(k.ps[4][:, 0:ET], k.ident[:, 0:1].to_broadcast([128, 128]), k.dst_e[:, :], start=True, stop=True).then_inc(turned, 1)
            nc.tensor.matmul(k.ps[5][:, 0:ET], k.ident[:, EP - 1:EP].to_broadcast([128, 128]), k.dst_e[:, :], start=True, stop=True).then_inc(turned, 1)

        @block.vector
        def _(dve):
            me = st["dve"]
            v = nc.vector
            dve.wait_ge(edges_in, 64)
            v.tensor_copy(dstq[:, :], dstq_i[:, :]).then_inc(edges_f, 1)
            dve.wait_ge(edges_f, 1)
            v.tensor_copy(srcq[:, :], srcq_i[:, :]).then_inc(edges_f, 1)
            me(dve, v.tensor_tensor(same[:, 1:J * EP], dstq[:, 1:J * EP], dstq[:, 0:J * EP - 1], ALU.is_equal))
            me(dve, v.memset(same[:, 0:J * EP + 1:EP], 0.0))
            v.tensor_copy(k.cont_q[:, :], same[:, 0:J * EP])
            me(dve, v.tensor_scalar(k.tile_dst[:, :], dstq[:, 0:J * EP:EP], float(N - 1), None, ALU.min))
            v.tensor_scalar(same[:, :], same[:, :], -1.0, BIG, ALU.add, ALU.mult).then_inc(edges_f, 2)
            for b, t in enumerate((k.dst_e, k.src_e, k.fwd_e, k.bwd_e)):
                dve.wait_ge(turned, b + 1)
                me(dve, v.tensor_copy(t[:, :].rearrange("p (q j) -> p j q", j=J),
                                      k.ps[b][:, 0:ET].rearrange("p (j q) -> p j q", j=J)))
                if b == 0:
                    dve.sem_inc(ends_b, 1)
            dve.wait_ge(turned, 6)
            v.tensor_copy(first_b[:, :], k.ps[4][:, 0:ET])
            me(dve, v.tensor_copy(last_b[:, :], k.ps[5][:, 0:ET]))
            me(dve, v.memset(k.joins[:, 0:1], 0.0))
            me(dve, v.tensor_tensor(k.joins[:, 1:ET], last_b[:, 1:ET], last_b[:, 0:ET - 1], ALU.is_equal))
            dve.wait_ge(consts, 1)
            with dve.Fori(0, NT) as t:
                me.loop(t, 1)
                me(dve, v.tensor_scalar(trash[:, :], first_b[0:P, :], k.node[:, bass.ds(t, 1)], None, ALU.is_lt, ALU.add,
                                        accum_out=before[:, bass.ds(t, 1)]))
                me.end(NT)
            me(dve, v.tensor_scalar(tile[:, :], before[:, :], -1.0, 0.0, ALU.add, ALU.max))
            v.tensor_copy(tile_i[:, :], tile[:, :]).then_inc(tiles_found, 1)
            dve.wait_ge(windows_in, 16 * NT)
            with dve.Fori(0, NT) as t:
                me.loop(t, 1)
                me(dve, v.tensor_scalar(trash[:, 0:EP], window[:, bass.ds(t, 1), :].rearrange("p a e -> p (a e)"), k.node[:, bass.ds(t, 1)], None,
                                        ALU.is_lt, ALU.add, accum_out=before[:, bass.ds(t, 1)]))
                me.end(NT)
            v.scalar_tensor_tensor(out=start[:, :], in0=tile[:, :], scalar=float(EP), in1=before[:, :], op0=ALU.mult,
                                   op1=ALU.add).then_inc(starts_found, 1)
            dve.wait_ge(starts_found, 1)
            dve.wait_ge(ends_in, 16)
            me(dve, v.tensor_tensor(k.deg[:, :], end[:, :], start[:, :], ALU.subtract))
            v.tensor_scalar(has[:, :], k.deg[:, :], 0.0, None, ALU.is_gt)
            me(dve, v.tensor_scalar(last[:, :], end[:, :], -1.0, 0.0, ALU.add, ALU.max))
            me(dve, v.tensor_copy(last_i[:, :], last[:, :]))
            me(dve, v.tensor_single_scalar(tile_i[:, :], last_i[:, :], 7, ALU.logical_shift_right))
            me(dve, v.tensor_copy(tile[:, :], tile_i[:, :]))
            v.tensor_scalar(t0[:, :], last[:, :], -float(NO_ROW), None, ALU.add)
            me(dve, v.scalar_tensor_tensor(out=t1[:, :], in0=tile[:, :], scalar=float(EP), in1=start[:, :],
                                           op0=ALU.mult, op1=ALU.is_gt))
            v.tensor_tensor(t0[:, :], t0[:, :], has[:, :], ALU.mult)
            me(dve, v.tensor_tensor(t1[:, :], t1[:, :], has[:, :], ALU.mult))
            v.tensor_scalar(k.main_row[:, :], t0[:, :], float(NO_ROW), None, ALU.add)
            me(dve, v.tensor_scalar(tile[:, :], tile[:, :], -1.0 - NO_CHAIN, None, ALU.add))
            me(dve, v.tensor_tensor(t1[:, :], t1[:, :], tile[:, :], ALU.mult))
            v.tensor_scalar(k.chain_row[:, :], t1[:, :], float(NO_CHAIN), None, ALU.add)
            me(dve, v.tensor_scalar(t0[:, :], start[:, :], -float(NO_ROW + 1), None, ALU.add))
            me(dve, v.tensor_tensor(t0[:, :], t0[:, :], has[:, :], ALU.mult))
            me(dve, v.tensor_scalar(k.start_row[:, :], t0[:, :], float(NO_ROW + 1), None, ALU.add))


def norm_stats(k, dve, src, ready, deviations, roots):
    v, me = k.nc.vector, k.steps["dve"]
    with dve.Fori(0, NT) as t:
        v.bn_stats(k.stats[:, bass.ds(t, 1), :].rearrange("p a s -> p (a s)"),
                   src[:, bass.ds(t, 1), :].rearrange("p a c -> p (a c)"))
    me(dve, v.memset(k.rstd[:, :], 0.0))
    even, odd, mean, var = k.stats[:, :, 1], k.stats[:, :, 4], k.mv[:, :, 0], k.mv[:, :, 1]
    v.tensor_tensor(mean, even, odd, ALU.add)
    v.tensor_tensor(var, even, odd, ALU.subtract)
    me(dve, v.tensor_tensor(k.rstd[:, :], k.stats[:, :, 2], k.stats[:, :, 5], ALU.add))
    v.tensor_scalar(mean, mean, 0.5, None, ALU.mult)
    v.tensor_scalar(k.rstd[:, :], k.rstd[:, :], 1.0 / C, EPS, ALU.mult, ALU.add)
    me(dve, v.tensor_tensor(var, var, var, ALU.mult))
    v.scalar_tensor_tensor(out=k.rstd[:, :], in0=var, scalar=0.25, in1=k.rstd[:, :], op0=ALU.mult, op1=ALU.add).then_inc(deviations, 1)
    dve.wait_ge(roots, 1)
    me(dve, v.reciprocal(k.rstd[:, :], k.rstd[:, :]))


def norm_roots(k, act, deviations, roots):
    act.wait_ge(deviations, 1)
    k.nc.scalar.activation(k.rstd[:, :], k.rstd[:, :], ACT.Sqrt).then_inc(roots, 1)


def project_phase(k):
    nc, st = k.nc, k.steps
    ctx = ExitStack()
    with ctx:
        sb = lambda n, s, d=F32: k.sb(n, s, d, ctx)
        w = sb("w", [128, 2, RW])
        att = sb("att", [128, 2, C])
        prod = sb("prod", [128, 2, C])
        xn = sb("xn", [P, TB, C])
        xt = sb("xt", [128, TB, 2, P])
        w_in, att_in = k.sem("w_in"), k.sem("att_in")
        deviations, roots = k.sem("p_deviations"), k.sem("p_roots")
        w_ready = k.sem("w_ready")
        xn_made, xt_turned, xt_made = k.sem("p_xn_made"), k.sem("p_xt_turned"), k.sem("p_xt_made")
        projected, taken, out_done = k.sem("projected"), k.sem("p_taken"), k.sem("p_out_done")
        block = ctx.enter_context(nc.Block())

        @block.sync
        def _(sp):
            sp.dma_start(w[:, :, 0:C], k.a["L0_gnn_W"].rearrange("(a p) c -> p a c", p=128)).then_inc(w_in, 16)
            for i, name in enumerate(("L0_gnn_att_src", "L0_gnn_att_dst")):
                sp.dma_start(att[:, i, :], k.a[name].rearrange("(a h) d -> a (h d)", a=1).to_broadcast([128, C])).then_inc(att_in, 16)
            sp.wait_ge(taken, NT + TB)
            sp.dma_start(k.xh_tab.rearrange("(p t) c -> p t c", p=P), k.xh[:, :, 0:XW]).then_inc(out_done, 16)
            sp.dma_start(k.adst_tab.rearrange("(p t) c -> p t c", p=P), k.xh[:, :, XW:RW]).then_inc(out_done, 16)
            sp.wait_ge(out_done, 32)

        @block.tensor
        def _(pe):
            pe.sem_inc(xt_turned, TB)
            pe.sem_inc(projected, TB)
            pe.wait_ge(k.consts, 1)
            pe.wait_ge(w_ready, 1)
            with pe.Fori(0, NT // TB) as i:
                for s in range(TB):
                    pe.wait_ge(xn_made, i * TB + s + 1)
                    pe.wait_ge(xt_made, i * TB + TB if s < 3 else i * TB + s - 2 + TB)
                    for c in range(2):
                        last_mm = nc.tensor.transpose(k.ps[s % 3][:, c * P:(c + 1) * P],
                                                      xn[:, s, c * 128:(c + 1) * 128], k.ident[0:P, 0:P])
                    last_mm.then_inc(xt_turned, 1)
                for s in range(TB):
                    pe.wait_ge(xt_made, i * TB + s + 1 + TB)
                    pe.wait_ge(taken, i * TB + s + 1)
                    for c in range(2):
                        last_mm = nc.tensor.matmul(k.ps[3 + s][0:P, 0:RW], xt[:, s, c, :], w[:, c, :], start=(c == 0), stop=(c == 1))
                    last_mm.then_inc(projected, 1)

        @block.scalar
        def _(act):
            norm_roots(k, act, deviations, roots)
            act.sem_inc(xt_made, TB)
            with act.Fori(0, NT // TB) as i:
                for s in range(TB):
                    act.wait_ge(xt_turned, i * TB + s + 1 + TB)
                    act.wait_ge(projected, i * TB + s + 1)
                    nc.scalar.copy(xt[:, s, :, :].rearrange("p a n -> p (a n)"), k.ps[s % 3][:, 0:2 * P]).then_inc(xt_made, 1)

        @block.vector
        def _(dve):
            v, me = nc.vector, st["dve"]
            dve.sem_inc(taken, TB)
            dve.wait_ge(w_in, 16)
            dve.wait_ge(att_in, 32)
            for i in range(2):
                me(dve, v.tensor_tensor(prod[:, :, :], w[:, :, 0:C], att[:, i:i + 1, :].to_broadcast([128, 2, C]), ALU.mult))
                me(dve, v.tensor_reduce(w[:, :, C + H * i:C + H * (i + 1)], prod[:, :, :].rearrange("p a (h d) -> p a h d", h=H), AX, ALU.add))
            dve.sem_inc(w_ready, 1)
            dve.wait_ge(k.x_in, 16)
            norm_stats(k, dve, k.res, None, deviations, roots)
            with dve.Fori(0, NT // TB) as i:
                me.loop(i, TB)
                for s in range(TB):
                    t = i * TB + s
                    dve.wait_ge(xt_turned, i * TB + s + 1)
                    me(dve, v.tensor_scalar(xn[:, s, :], k.res[:, bass.ds(t, 1), :].rearrange("p a c -> p (a c)"), k.mv[:, bass.ds(t, 1), 0:1].rearrange("p a c -> p (a c)"),
                                    k.rstd[:, bass.ds(t, 1)], ALU.subtract, ALU.mult))
                    r = k.res[:, bass.ds(t, 1), :].rearrange("p a c -> p (a c)")
                    v.tensor_tensor(r, r, xn[:, s, :], ALU.add).then_inc(xn_made, 1)
                for s in range(TB):
                    t = i * TB + s
                    dve.wait_ge(projected, i * TB + s + 1 + TB)
                    v.tensor_scalar(k.xh[:, bass.ds(t, 1), :].rearrange("p a c -> p (a c)"), k.ps[3 + s][0:P, 0:RW], 1.0, None, ALU.mult).then_inc(taken, 1)
                me.end(NT // TB)


def spread_phase(k):
    nc, st = k.nc, k.steps
    ctx = ExitStack()
    with ctx:
        sb = lambda n, s, d=F32: k.sb(n, s, d, ctx)
        sparse = sb("sparse", [Q, J * EP * H])
        filled = sb("filled", [Q, J * EP * H])
        firsts = sb("firsts", [Q, J, H])
        zeroed, cleared, firsts_in = k.sem("zeroed"), k.sem("cleared"), k.gather_sem("firsts_in")
        firsts_out, starts_out, sparse_in = k.sem("firsts_out"), k.gather_sem("node_starts_out"), k.sem("sparse_in")
        spread, turned, taken = k.sem("spread"), k.sem("s_turned"), k.sem("s_taken")
        block = ctx.enter_context(nc.Block())
        edge_rows = k.adst_edge.rearrange("(q m) h -> q (m h)", q=Q)

        @block.sync
        def _(sp):
            sp.wait_ge(zeroed, 1)
            sp.dma_start(edge_rows, sparse[:, :]).then_inc(cleared, 16)
            sp.wait_ge(cleared, 16)
            sp.wait_ge(firsts_in, 16 * J)
            sp.dma_start(k.adst_edge.rearrange("(q j e) h -> q j e h", q=Q, j=J)[:, :, 0, :], firsts[:, :, :]).then_inc(firsts_out, 16)
            sp.wait_ge(starts_out, 16 * NT)
            sp.dma_start(sparse[:, :], edge_rows).then_inc(sparse_in, 16)

        @block.gpsimd
        def _(pool):
            for j in range(J):
                pool.indirect_dma_start(out=firsts[:, j, :], out_offset=None, in_=k.adst_tab,
                                        in_offset=bass.IndirectOffsetOnAxis(ap=k.tile_dst[:, j:j + 1], axis=0)).then_inc(firsts_in, 16)
            pool.wait_ge(firsts_out, 16)
            for t in range(NT):
                pool.indirect_dma_start(out=k.adst_edge, out_offset=bass.IndirectOffsetOnAxis(ap=k.start_row[:, t:t + 1], axis=0),
                                        in_=k.xh[:, t, XW:RW], in_offset=None, bounds_check=NO_ROW - 1, oob_is_err=False).then_inc(starts_out, 16)

        @block.tensor
        def _(pe):
            pe.wait_ge(spread, H)
            for h in range(H):
                if h >= 4:
                    pe.wait_ge(taken, h - 3)
                for j in range(J):
                    m = nc.tensor.transpose(k.ps[h % 4][:, j * Q:(j + 1) * Q], filled[:, j * EP * H + h:(j + 1) * EP * H:H], k.ident[0:Q, 0:Q])
                m.then_inc(turned, 1)

        @block.scalar
        def _(act):
            for h in range(H):
                act.wait_ge(turned, h + 1)
                nc.scalar.copy(k.adst_e[:, :, h].rearrange("p (q j) -> p j q", j=J), k.ps[h % 4][:, 0:ET].rearrange("p (j q) -> p j q", j=J)).then_inc(taken, 1)

        @block.vector
        def _(dve):
            v = nc.vector
            v.memset(sparse[:, :], 0.0).then_inc(zeroed, 1)
            dve.wait_ge(sparse_in, 16)
            for h in range(H):
                for j in range(J):
                    m = v.tensor_tensor_scan(filled[:, j * EP * H + h:(j + 1) * EP * H:H], k.cont_q[:, j * EP:(j + 1) * EP],
                                             sparse[:, j * EP * H + h:(j + 1) * EP * H:H], 0.0, ALU.mult, ALU.add)
                m.then_inc(spread, 1)


def edge_phase(k, name, table, width, weighted):
    nc, st = k.nc, k.steps
    ctx = ExitStack()
    sums_w = C + H if weighted else C
    out_w = RW if weighted else C
    BK = 7
    with ctx:
        sb = lambda n, s, d=F32: k.sb(f"{name}_{n}", s, d, ctx)
        sem = lambda n: k.sem(f"{name}_{n}")
        ix = [sb(f"ix{s}", [EP, SB], I32) for s in range(2)]
        rows = [sb(f"rows{s}", [EP, SB, width]) for s in range(2)]
        dstb = [sb(f"dstb{s}", [EP, SB * EP]) for s in range(2)]
        same = [sb(f"same{s}", [EP, SB, EP]) for s in range(2)]
        outs = [sb(f"outs{s}", [EP, SB, out_w]) for s in range(2)]
        if weighted:
            logit0, logit, shifted = (sb(n, [EP, SB, H]) for n in ("logit0", "logit", "shifted"))
            mask8 = sb("mask8", [EP, 2, SB, H])
            masks = sb("masks", [SB * H, 2 * EP])
            running, maxima = sb("running", [SB * H, EP]), sb("maxima", [SB * H, EP])
        outs_free = sem("outs_free")
        ix_made, issuing = sem("ix_made"), sem("issuing")
        rows_in = [k.gather_sem(f"{name}_rows_in{s}") for s in range(2)]
        dstb_in = [sem(f"dstb_in{s}") for s in range(2)]
        outs_out = [sem(f"outs_out{s}") for s in range(2)]
        same_made, logits_made, logits_turned, masks_in = sem("same_made"), sem("logits_made"), sem("logits_turned"), sem("masks_in")
        maxima_made, maxima_turned, maxima_in, less_max = sem("maxima_made"), sem("maxima_turned"), sem("maxima_in"), sem("less_max")
        weights_made, messages, sums, taken = sem("weights_made"), sem("messages"), sem("sums"), sem("taken")
        block = ctx.enter_context(nc.Block())

        @block.sync
        def _(sp):
            out_rows = k.parts[0:ET * EP, 0:out_w].rearrange("(b t e) c -> e b t c", t=SB, e=EP)
            dst_rows = k.dst_pad.rearrange("(b e) -> b e", b=NB)
            sp.sem_inc(outs_free, 2)

            def load(b, s, guarded=True):
                if guarded:
                    sp.wait_ge(same_made, b)
                sp.dma_start(dstb[s][:, :], dst_rows[bass.ds(b, 1), :].to_broadcast([EP, SB * EP])).then_inc(dstb_in[s], 16)

            def store(b, s, turn):
                sp.wait_ge(taken, b * SB + SB + BK)
                if weighted:
                    sp.wait_ge(maxima_in, b + 1)
                sp.dma_start(out_rows[:, bass.ds(b, 1), :, :].rearrange("e b t c -> e (b t) c"), outs[s][:, :, :]).then_inc(outs_out[s], 16)
                sp.wait_ge(outs_out[s], 16 * turn + 16)
                sp.sem_inc(outs_free, 1)

            load(0, 0, guarded=False)
            with sp.Fori(0, NB // 2 - 1) as i:
                load(i * 2 + 1, 1)
                store(i * 2, 0, i)
                load(i * 2 + 2, 0)
                store(i * 2 + 1, 1, i)
            load(NB - 1, 1)
            store(NB - 2, 0, NB // 2 - 1)
            store(NB - 1, 1, NB // 2 - 1)

        @block.gpsimd
        def _(pool):
            with pool.Fori(0, NB // 2) as i:
                for s in range(2):
                    b = i * 2 + s
                    pool.wait_ge(sums, b * SB + SB)
                    nc.gpsimd.tensor_copy(ix[s][:, :], k.src_e[:, bass.ds(b * SB, SB)]).then_inc(ix_made, 1)
                    pool.wait_ge(ix_made, b + 1)
                    pool.sem_inc(issuing, 1)
                    for t in range(SB):
                        pool.indirect_dma_start(out=rows[s][:, t, :], out_offset=None, in_=table,
                                                in_offset=bass.IndirectOffsetOnAxis(ap=ix[s][:, t:t + 1], axis=0)).then_inc(rows_in[s], 16)

        @block.vector
        def _(dve):
            v, me = nc.vector, st["dve"]
            dve.sem_inc(same_made, 1)
            with dve.Fori(0, NB // 2) as i:
                if weighted:
                    me.loop(i, 4)
                for s in range(2):
                    b = i * 2 + s
                    dve.wait_ge(dstb_in[s], 16 * i + 16)
                    dve.wait_ge(sums, b * SB + SB)
                    v.tensor_tensor(same[s][:, :, :], dstb[s][:, :].rearrange("p (t e) -> p t e", t=SB),
                                    k.dst_e[:, bass.ds(b * SB, SB)].rearrange("p (t a) -> p t a", a=1).to_broadcast([EP, SB, EP]),
                                    ALU.is_equal).then_inc(same_made, 1)
                    if not weighted:
                        continue
                    for m, mask in enumerate((k.fwd_e, k.bwd_e)):
                        v.tensor_scalar(mask8[:, m, :, :], mask[:, bass.ds(b * SB, SB)].rearrange("p (t a) -> p t a", a=1).to_broadcast([EP, SB, H]),
                                        1.0, None, ALU.mult)
                    dve.wait_ge(rows_in[s], 16 * SB * i + 16 * SB)
                    me(dve, v.tensor_tensor(logit0[:, :, :], rows[s][:, :, C:C + H], k.adst_e[:, bass.ds(b * SB, SB), :], ALU.add))
                    v.scalar_tensor_tensor(out=logit[:, :, :], in0=logit0[:, :, :], scalar=0.2, in1=logit0[:, :, :], op0=ALU.mult, op1=ALU.max).then_inc(logits_made, 1)
                    dve.wait_ge(masks_in, b + 1)
                    me(dve, v.tensor_tensor_scan(running[:, :], masks[:, 0:EP], k.ps[0][0:SB * H, 0:EP], -BIG, ALU.add, ALU.max))
                    v.tensor_tensor_scan(maxima[:, ::-1], masks[:, EP:2 * EP][:, ::-1], running[:, ::-1], -BIG, ALU.add, ALU.max).then_inc(maxima_made, 1)
                    dve.wait_ge(maxima_in, b + 1)
                    v.tensor_tensor(shifted[:, :, :], logit[:, :, :], outs[s][:, :, C + H:RW], ALU.subtract).then_inc(less_max, 1)
                    dve.wait_ge(weights_made, b + 2)
                    for half in range(2):
                        t0, t1 = half * SB // 2, (half + 1) * SB // 2
                        f = rows[s][:, t0:t1, 0:C].rearrange("p t (h d) -> p t h d", h=H)
                        v.tensor_tensor(f, f, rows[s][:, t0:t1, C:C + H].rearrange("p t (h a) -> p t h a", a=1).to_broadcast([EP, SB // 2, H, D]),
                                        ALU.mult).then_inc(messages, 1)
                if weighted:
                    me.end(NB // 2)

        @block.tensor
        def _(pe):
            pe.sem_inc(sums, 2 * SB)
            with pe.Fori(0, NB // 2) as i:
                for s in range(2):
                    b = i * 2 + s
                    if weighted:
                        pe.wait_ge(logits_made, b + 1)
                        pe.wait_ge(weights_made, b + 1)
                        nc.tensor.transpose(k.ps[0][0:SB * H, 0:EP], logit[:, :, :].rearrange("p t h -> p (t h)"), k.ident[:, :])
                        for m in range(2):
                            mm = nc.tensor.transpose(k.ps[0][0:SB * H, EP * (m + 1):EP * (m + 2)], mask8[:, m, :, :].rearrange("p t h -> p (t h)"), k.ident[:, :])
                        mm.then_inc(logits_turned, 1)
                        pe.wait_ge(maxima_made, b + 1)
                        nc.tensor.transpose(k.ps[0][:, 384:384 + SB * H], maxima[:, :], k.ident[0:SB * H, 0:SB * H]).then_inc(maxima_turned, 1)
                    pe.wait_ge(same_made, b + 2)
                    if not weighted:
                        pe.wait_ge(rows_in[s], 16 * SB * i + 16 * SB)
                    for t in range(SB):
                        if weighted and t % (SB // 2) == 0:
                            pe.wait_ge(messages, 2 * b + 1 + 2 * t // SB)
                        pe.wait_ge(taken, b * SB + t + 1)
                        nc.tensor.matmul(k.ps[1 + t % BK][:, 0:sums_w], same[s][:, t, :], rows[s][:, t, 0:sums_w],
                                         start=True, stop=True).then_inc(sums, 1)

        @block.scalar
        def _(act):
            act.sem_inc(taken, BK)
            act.sem_inc(weights_made, 1)
            with act.Fori(0, NB // 2) as i:
                for s in range(2):
                    b = i * 2 + s
                    act.wait_ge(outs_free, b + 1)
                    if weighted:
                        act.wait_ge(logits_turned, b + 1)
                        nc.scalar.copy(masks[:, :], k.ps[0][0:SB * H, EP:3 * EP]).then_inc(masks_in, 1)
                        act.wait_ge(maxima_turned, b + 1)
                        nc.scalar.copy(outs[s][:, :, C + H:RW], k.ps[0][:, 384:384 + SB * H].rearrange("p (t h) -> p t h", h=H)).then_inc(maxima_in, 1)
                        act.wait_ge(less_max, b + 1)
                        nc.scalar.activation(rows[s][:, :, C:C + H], shifted[:, :, :], ACT.Exp).then_inc(weights_made, 1)
                    for t in range(SB):
                        act.wait_ge(sums, b * SB + t + 1 + 2 * SB)
                        nc.scalar.copy(outs[s][:, t, 0:sums_w], k.ps[1 + t % BK][:, 0:sums_w]).then_inc(taken, 1)


def chain_phase(k, name, weighted):
    nc, st = k.nc, k.steps
    ctx = ExitStack()
    w = RW if weighted else C
    with ctx:
        sb = lambda n, s, d=F32: k.sb(f"{name}c_{n}", s, d, ctx)
        sem = lambda n: k.sem(f"{name}c_{n}")
        lasts, carried = sb("lasts", [Q, J, w]), sb("carried", [Q, J, w])
        last_t = [sb(f"last_t{c}", [128, ET]) for c in range(2)]
        sum_t = [sb(f"sum_t{c}", [128, ET]) for c in range(2)]
        dummy = sb("dummy", [1, RW])
        if weighted:
            den_t, max_t, den_c, max_c, neg, keep, scale = (sb(n, [H, ET]) for n in ("den_t", "max_t", "den_c", "max_c", "neg", "keep", "scale"))
            sel = sb("sel", [H, C])
        lasts_in, dummies, sel_made, turned = sem("lasts_in"), sem("dummies"), sem("sel_made"), sem("turned")
        drops, factors, spread, scanned, back, rows_made, stored = (sem(n) for n in ("drops", "factors", "spread", "scanned", "back", "rows_made", "stored"))
        block = ctx.enter_context(nc.Block())

        @block.sync
        def _(sp):
            sp.dma_start(lasts[:, :, :], k.parts[0:ET * EP, :].rearrange("(q j e) c -> q j e c", q=Q, j=J)[:, :, EP - 1, 0:w]).then_inc(lasts_in, 16)
            if weighted:
                sp.wait_ge(dummies, 1)
                sp.dma_start(k.parts[NO_ROW:NO_ROW + 1, :], dummy[:, :]).then_inc(stored, 16)
                sp.dma_start(k.chains[NO_CHAIN:NO_CHAIN + 1, :], dummy[:, :]).then_inc(stored, 16)
            sp.wait_ge(rows_made, 1)
            sp.dma_start(k.chains[0:ET, 0:w].rearrange("(q j) c -> q j c", j=J), carried[:, :, :]).then_inc(stored, 16)
            sp.wait_ge(stored, 48 if weighted else 16)

        @block.gpsimd
        def _(pool):
            if weighted:
                me = st["pool"]
                nc.gpsimd.memset(dummy[:, 0:C + H], 0.0)
                me(pool, nc.gpsimd.memset(dummy[:, C + H:RW], -BIG))
                pool.sem_inc(dummies, 1)
                me(pool, nc.gpsimd.memset(sel[:, :], 1.0))
                me(pool, nc.gpsimd.affine_select(out=sel[:, :], in_=sel[:, :], compare_op=ALU.is_ge, fill=0.0, base=0,
                                                 pattern=[[1, C]], channel_multiplier=-D))
                nc.gpsimd.affine_select(out=sel[:, :], in_=sel[:, :], compare_op=ALU.is_ge, fill=0.0, base=D - 1,
                                        pattern=[[-1, C]], channel_multiplier=D).then_inc(sel_made, 1)

        @block.tensor
        def _(pe):
            pe.wait_ge(lasts_in, 16)
            for c in range(2):
                for j in range(J):
                    m = nc.tensor.transpose(k.ps[c][:, j * Q:(j + 1) * Q], lasts[:, j, c * 128:(c + 1) * 128], k.ident[0:Q, 0:Q])
                m.then_inc(turned, 1)
            if weighted:
                for c in range(2):
                    for j in range(J):
                        m = nc.tensor.transpose(k.ps[2 + c][0:H, j * Q:(j + 1) * Q], lasts[:, j, C + c * H:C + (c + 1) * H], k.ident[0:Q, 0:Q])
                    m.then_inc(turned, 1)
                pe.wait_ge(sel_made, 1)
                pe.wait_ge(factors, 3)
                for c in range(2):
                    nc.tensor.matmul(k.ps[4 + c][:, 0:ET], sel[:, c * 128:(c + 1) * 128], keep[:, :], start=True, stop=True)
                    nc.tensor.matmul(k.ps[6 + c][:, 0:ET], sel[:, c * 128:(c + 1) * 128], scale[:, :], start=True, stop=True).then_inc(spread, 1)
            pe.wait_ge(scanned, 3 if weighted else 2)
            for c in range(2):
                for j in range(J):
                    m = nc.tensor.transpose(k.ps[c][0:Q, j * 128:(j + 1) * 128], sum_t[c][:, j:ET:J], k.ident[:, :])
                m.then_inc(back, 1)
            if weighted:
                for c, t in enumerate((den_c, max_c)):
                    for j in range(J):
                        m = nc.tensor.transpose(k.ps[2 + c][0:Q, j * H:(j + 1) * H], t[:, j:ET:J], k.ident[0:H, 0:H])
                    m.then_inc(back, 1)

        @block.scalar
        def _(act):
            if weighted:
                act.wait_ge(drops, 1)
                nc.scalar.activation(keep[:, :], keep[:, :], ACT.Exp).then_inc(factors, 1)
                nc.scalar.activation(scale[:, :], scale[:, :], ACT.Exp).then_inc(factors, 1)

        @block.vector
        def _(dve):
            v, me = nc.vector, st["dve"]

            def lay(dst, bank, parts):
                me(dve, v.tensor_copy(dst[:, :].rearrange("p (q j) -> p j q", j=J), k.ps[bank][0:parts, 0:ET].rearrange("p (j q) -> p j q", j=J)))

            for c in range(2):
                dve.wait_ge(turned, c + 1)
                lay(last_t[c], c, 128)
            if weighted:
                dve.wait_ge(turned, 4)
                lay(den_t, 2, H)
                lay(max_t, 3, H)
                me(dve, v.tensor_scalar(neg[:, :], k.joins[0:H, :], -1.0, BIG, ALU.add, ALU.mult))
                me(dve, v.tensor_tensor_scan(max_c[:, :], neg[:, :], max_t[:, :], -BIG, ALU.add, ALU.max))
                v.memset(keep[:, 0:1], 0.0)
                me(dve, v.tensor_tensor(keep[:, 1:ET], max_c[:, 0:ET - 1], max_c[:, 1:ET], ALU.subtract))
                me(dve, v.tensor_tensor(keep[:, :], keep[:, :], k.joins[0:H, :], ALU.mult))
                v.tensor_tensor(scale[:, :], max_t[:, :], max_c[:, :], ALU.subtract).then_inc(drops, 1)
                dve.wait_ge(factors, 2)
                v.tensor_tensor(keep[:, :], keep[:, :], k.joins[0:H, :], ALU.mult).then_inc(factors, 1)
                me(dve, v.tensor_tensor(den_t[:, :], den_t[:, :], scale[:, :], ALU.mult))
                v.tensor_tensor_scan(den_c[:, :], keep[:, :], den_t[:, :], 0.0, ALU.mult, ALU.add).then_inc(scanned, 1)
                for c in range(2):
                    dve.wait_ge(spread, c + 1)
                    me(dve, v.tensor_tensor(last_t[c][:, :], last_t[c][:, :], k.ps[6 + c][:, 0:ET], ALU.mult))
                    v.tensor_tensor_scan(sum_t[c][:, :], k.ps[4 + c][:, 0:ET], last_t[c][:, :], 0.0, ALU.mult, ALU.add).then_inc(scanned, 1)
            else:
                for c in range(2):
                    v.tensor_tensor_scan(sum_t[c][:, :], k.joins[:, :], last_t[c][:, :], 0.0, ALU.mult, ALU.add).then_inc(scanned, 1)
            for c in range(2):
                dve.wait_ge(back, c + 1)
                me(dve, v.tensor_copy(carried[:, :, c * 128:(c + 1) * 128], k.ps[c][0:Q, :].rearrange("p (j c) -> p j c", j=J)))
            if weighted:
                for c in range(2):
                    dve.wait_ge(back, c + 3)
                    me(dve, v.tensor_copy(carried[:, :, C + c * H:C + (c + 1) * H], k.ps[2 + c][0:Q, 0:J * H].rearrange("p (j h) -> p j h", j=J)))
            dve.sem_inc(rows_made, 1)


def gather_nodes(k, pool, width, main, chain, ix, sems):
    nc = k.nc
    ix_made, issuing, rows_in, rows_used = sems
    with pool.Fori(0, NT // TB) as i:
        pool.wait_ge(rows_used, i + 1)
        nc.gpsimd.tensor_copy(ix[:, 0, :], k.main_row[:, bass.ds(i * TB, TB)])
        nc.gpsimd.tensor_copy(ix[:, 1, :], k.chain_row[:, bass.ds(i * TB, TB)]).then_inc(ix_made, 1)
        pool.wait_ge(ix_made, i + 1)
        pool.sem_inc(issuing, 1)
        for s in range(TB):
            pool.indirect_dma_start(out=main[:, s, :], out_offset=None, in_=k.parts[:, :],
                                    in_offset=bass.IndirectOffsetOnAxis(ap=ix[:, 0, s:s + 1], axis=0)).then_inc(rows_in, 16)
            pool.indirect_dma_start(out=chain[:, s, :], out_offset=None, in_=k.chains[:, :],
                                    in_offset=bass.IndirectOffsetOnAxis(ap=ix[:, 1, s:s + 1], axis=0)).then_inc(rows_in, 16)


def gat_node_phase(k):
    nc, st = k.nc, k.steps
    ctx = ExitStack()
    with ctx:
        sb = lambda n, s, d=F32: k.sb(f"gn_{n}", s, d, ctx)
        sem = lambda n: k.sem(f"gn_{n}")
        main, chain = sb("main", [P, TB, RW]), sb("chain", [P, TB, RW])
        ix = sb("ix", [P, 2, TB], I32)
        own0, own = sb("own0", [P, NT, H]), sb("own", [P, NT, H])
        top, den, tmp = sb("top", [P, TB, H]), sb("den", [P, TB, H]), sb("tmp", [P, TB, H])
        wt = sb("wt", [P, 3, TB, H])
        rowv = sb("rowv", [P, 3, C])
        mean, var = sb("mean", [P, C]), sb("var", [P, C])
        sq = sb("sq", [P, NT, C])
        rows_in = k.gather_sem("gn_rows_in")
        ix_made, issuing, rows_used, vecs_in, gaps, weights = (sem(n) for n in ("ix_made", "issuing", "rows_used", "vecs_in", "gaps", "weights"))
        all_made, summed, centred, squared, spread_s, dev, root, beta_in = (sem(n) for n in ("all_made", "summed", "centred", "squared", "spread", "dev", "root", "beta_in"))
        block = ctx.enter_context(nc.Block())
        feat = k.xh[:, :, 0:C]

        @block.sync
        def _(sp):
            for i, name in enumerate(("L0_gnn_bias", "L0_gnn_gamma", "L0_gnn_beta")):
                sp.dma_start(rowv[:, i, :], k.a[name].rearrange("(a c) -> a c", a=1).to_broadcast([P, C])).then_inc(vecs_in, 16)

        @block.gpsimd
        def _(pool):
            pool.sem_inc(rows_used, 1)
            gather_nodes(k, pool, RW, main, chain, ix, (ix_made, issuing, rows_in, rows_used))
            pool.wait_ge(vecs_in, 48)
            nc.gpsimd.tensor_tensor(k.res[:, :, :], k.res[:, :, :], rowv[:, 2:3, :].to_broadcast([P, NT, C]), ALU.add).then_inc(beta_in, 1)

        @block.scalar
        def _(act):
            with act.Fori(0, NT // TB) as i:
                act.wait_ge(gaps, i + 1)
                nc.scalar.activation(wt[:, :, :, :], wt[:, :, :, :], ACT.Exp).then_inc(weights, 1)
            act.wait_ge(centred, 1)
            nc.scalar.activation(sq[:, :, :], feat, ACT.Square).then_inc(squared, 1)
            act.wait_ge(dev, 1)
            nc.scalar.activation(var[:, :], var[:, :], ACT.Sqrt).then_inc(root, 1)

        def over_nodes(bank, tile):
            ones = k.ones[0:P, 0:P]
            nc.tensor.matmul(bank, ones, tile[:, 0, 0:C], start=True, stop=False)
            with nc.tensor.Fori(1, NT - 1) as t:
                nc.tensor.matmul(bank, ones, tile[:, bass.ds(t, 1), 0:C].rearrange("p a c -> p (a c)"), start=False, stop=False)
            nc.tensor.matmul(bank, ones, tile[:, NT - 1, 0:C], start=False, stop=True).then_inc(summed, 1)

        @block.tensor
        def _(pe):
            pe.wait_ge(all_made, 1)
            over_nodes(k.ps[0][0:P, 0:C], k.xh)
            pe.wait_ge(squared, 1)
            over_nodes(k.ps[1][0:P, 0:C], sq)

        @block.vector
        def _(dve):
            v, me = nc.vector, st["dve"]
            me(dve, v.tensor_tensor(own0[:, :, :], k.xh[:, :, C:C + H], k.xh[:, :, C + H:RW], ALU.add))
            me(dve, v.scalar_tensor_tensor(out=own[:, :, :], in0=own0[:, :, :], scalar=0.2, in1=own0[:, :, :], op0=ALU.mult, op1=ALU.max))
            dve.wait_ge(vecs_in, 48)
            with dve.Fori(0, NT // TB) as i:
                me.loop(i, 11)
                dve.wait_ge(rows_in, 32 * TB * i + 32 * TB)
                mine = own[:, bass.ds(i * TB, TB), :]
                m1, m2 = main[:, :, C + H:RW], chain[:, :, C + H:RW]
                me(dve, v.tensor_tensor(top[:, :, :], m1, m2, ALU.max))
                me(dve, v.tensor_tensor(top[:, :, :], top[:, :, :], mine, ALU.max))
                v.tensor_tensor(wt[:, 0, :, :], m1, top[:, :, :], ALU.subtract)
                v.tensor_tensor(wt[:, 1, :, :], m2, top[:, :, :], ALU.subtract)
                v.tensor_tensor(wt[:, 2, :, :], mine, top[:, :, :], ALU.subtract).then_inc(gaps, 1)
                dve.wait_ge(weights, i + 1)
                v.tensor_tensor(den[:, :, :], wt[:, 0, :, :], main[:, :, C:C + H], ALU.mult)
                me(dve, v.tensor_tensor(tmp[:, :, :], wt[:, 1, :, :], chain[:, :, C:C + H], ALU.mult))
                me(dve, v.tensor_tensor(den[:, :, :], den[:, :, :], tmp[:, :, :], ALU.add))
                me(dve, v.tensor_tensor(den[:, :, :], den[:, :, :], wt[:, 2, :, :], ALU.add))
                me(dve, v.reciprocal(den[:, :, :], den[:, :, :]))
                me(dve, v.tensor_tensor(wt[:, :, :, :], wt[:, :, :, :], den[:, :, :].rearrange("p (a t) h -> p a t h", a=1).to_broadcast([P, 3, TB, H]), ALU.mult))
                node = k.xh[:, bass.ds(i * TB, TB), 0:C]
                for j, t in enumerate((main[:, :, 0:C], chain[:, :, 0:C], node)):
                    t = t.rearrange("p t (h d) -> p t h d", h=H)
                    m = v.tensor_tensor(t, t, wt[:, j, :, :].rearrange("p t (h a) -> p t h a", a=1).to_broadcast([P, TB, H, D]), ALU.mult)
                me(dve, m)
                me(dve, v.tensor_tensor(node, node, main[:, :, 0:C], ALU.add))
                me(dve, v.tensor_tensor(node, node, chain[:, :, 0:C], ALU.add))
                me(dve, v.tensor_tensor(node, node, rowv[:, 0:1, :].to_broadcast([P, TB, C]), ALU.add))
                dve.sem_inc(rows_used, 1)
                me.end(NT // TB)
            dve.sem_inc(all_made, 1)
            dve.wait_ge(summed, 1)
            me(dve, v.tensor_scalar(mean[:, :], k.ps[0][0:P, 0:C], 1.0 / N, None, ALU.mult))
            v.tensor_tensor(feat, feat, mean[:, :].rearrange("p (a c) -> p a c", a=1).to_broadcast([P, NT, C]), ALU.subtract).then_inc(centred, 1)
            dve.wait_ge(summed, 2)
            v.tensor_scalar(var[:, :], k.ps[1][0:P, 0:C], 1.0 / N, EPS, ALU.mult, ALU.add).then_inc(dev, 1)
            dve.wait_ge(root, 1)
            me(dve, v.reciprocal(var[:, :], var[:, :]))
            me(dve, v.tensor_tensor(var[:, :], var[:, :], rowv[:, 1, :], ALU.mult))
            me(dve, v.tensor_tensor(feat, feat, var[:, :].rearrange("p (a c) -> p a c", a=1).to_broadcast([P, NT, C]), ALU.mult))
            dve.wait_ge(beta_in, 1)
            me(dve, v.tensor_tensor(k.res[:, :, :], k.res[:, :, :], feat, ALU.add))


class Turning:

    def __init__(self, k, name, ctx):
        self.k = k
        self.xn = k.sb(f"{name}_xn", [P, TB, C], F32, ctx)
        self.xt = k.sb(f"{name}_xt", [128, TB, 2, P], F32, ctx)
        self.made, self.turned, self.kept, self.multiplied, self.taken = (
            k.sem(f"{name}_{n}") for n in ("made", "turned", "kept", "multiplied", "taken"))

    def on_tensor(self, pe, multiply):
        pe.sem_inc(self.turned, TB)
        pe.sem_inc(self.multiplied, TB)
        with pe.Fori(0, NT // TB) as i:
            for s in range(TB):
                pe.wait_ge(self.made, i * TB + s + 1)
                pe.wait_ge(self.kept, i * TB + TB if s < 3 else i * TB + s - 2 + TB)
                for c in range(2):
                    m = self.k.nc.tensor.transpose(self.k.ps[s % 3][:, c * P:(c + 1) * P], self.xn[:, s, c * 128:(c + 1) * 128], self.k.ident[0:P, 0:P])
                m.then_inc(self.turned, 1)
            for s in range(TB):
                pe.wait_ge(self.kept, i * TB + s + 1 + TB)
                pe.wait_ge(self.taken, i * TB + s + 1)
                multiply(s).then_inc(self.multiplied, 1)

    def on_scalar(self, act):
        act.sem_inc(self.kept, TB)
        with act.Fori(0, NT // TB) as i:
            for s in range(TB):
                act.wait_ge(self.turned, i * TB + s + 1 + TB)
                act.wait_ge(self.multiplied, i * TB + s + 1)
                self.k.nc.scalar.copy(self.xt[:, s, :, :].rearrange("p a n -> p (a n)"), self.k.ps[s % 3][:, 0:2 * P]).then_inc(self.kept, 1)

    def on_vector(self, dve, fill, take, steps=0, rows_free=None):
        me = self.k.steps["dve"]
        dve.sem_inc(self.taken, TB)
        with dve.Fori(0, NT // TB) as i:
            me.loop(i, steps)
            for s in range(TB):
                dve.wait_ge(self.turned, i * TB + s + 1)
                fill(i * TB + s, s).then_inc(self.made, 1)
            if rows_free is not None:
                dve.wait_ge(self.made, i * TB + TB)
                dve.sem_inc(rows_free, 1)
            for s in range(TB):
                dve.wait_ge(self.multiplied, i * TB + s + 1 + TB)
                take(i * TB + s, s).then_inc(self.taken, 1)
            me.end(NT // TB)


def tile_of(a, t):
    return a[:, bass.ds(t, 1), :].rearrange("p a c -> p (a c)")


def normed(k, out, t):
    return k.nc.vector.tensor_scalar(out, tile_of(k.res, t), k.mv[:, bass.ds(t, 1), 0:1].rearrange("p a c -> p (a c)"),
                                     k.rstd[:, bass.ds(t, 1)], ALU.subtract, ALU.mult)


NE, HID = 8, 682
M = 128
NI = (2 * N + NE * (M - 1)) // M
HH = HID // 2
HB = [(a, b, min(128, HH - 128 * b)) for a in range(2) for b in range(3)]


def router_phase(k):
    nc, st = k.nc, k.steps
    ctx = ExitStack()
    with ctx:
        sb = lambda n, s, d=F32: k.sb(f"r_{n}", s, d, ctx)
        sem = lambda n: k.sem(f"r_{n}")
        q = Turning(k, "r", ctx)
        rw, rwt = sb("rw", [NE, C]), sb("rwt", [128, 2, NE])
        xn1 = sb("xn1", [P, NT, C])
        prob, rest, hit, cand = (sb(n, [P, NT, NE]) for n in ("prob", "rest", "hit", "cand"))
        oh = sb("oh", [P, 2, NT, NE])
        both, tot, inc, slot = (sb(n, [P, NT, NE]) for n in ("both", "tot", "inc", "slot"))
        expert, item, lane = sb("expert", [P, NE]), sb("item", [P, NI]), sb("lane", [P, M])
        peak, idx, den = sb("peak", [P, NT]), sb("idx", [P, NT]), sb("den", [P, NT])
        tiles, tiles_i, ends, begins = sb("tiles", [P, NE]), sb("tiles_i", [P, NE], I32), sb("ends", [P, NE]), sb("begins", [P, NE])
        pos, hi, lo = sb("pos", [P, 2, NT]), sb("hi", [P, 2, NT]), sb("lo", [P, 2, NT])
        hi_i = sb("hi_i", [P, 2, NT], I32)
        before = sb("before", [P, P])
        at_lane, at_item = sb("at_lane", [P, 2 * NT, M]), sb("at_item", [P, 2 * NT, NI])
        over = sb("over", [P, NI, NE])
        of_item = sb("of_item", [P, NI])
        rw_in, rw_turned, rw_ready, deviations, roots = (sem(n) for n in ("rw_in", "rw_turned", "rw_ready", "deviations", "roots"))
        logits_done, xn_out, less_peak, exped, chosen, counted, places, tokens = (sem(n) for n in ("logits_done", "xn_out", "less_peak", "exped", "chosen", "counted", "places", "tokens"))
        iotas = sem("iotas")
        block = ctx.enter_context(nc.Block())

        @block.sync
        def _(sp):
            sp.dma_start(rw[:, :], k.a["L0_ffn_router_w"]).then_inc(rw_in, 16)
            sp.dma_start(k.x1_tab.rearrange("(p t) c -> p t c", p=P), k.res[:, :, :]).then_inc(xn_out, 16)
            sp.wait_ge(logits_done, 1)
            sp.dma_start(k.xn_tab.rearrange("(p t) c -> p t c", p=P), xn1[:, :, :]).then_inc(xn_out, 16)
            sp.wait_ge(xn_out, 32)

        @block.gpsimd
        def _(pool):
            me = st["pool"]
            nc.gpsimd.iota(expert[:, :], pattern=[[1, NE]], base=0, channel_multiplier=0, allow_small_or_imprecise_dtypes=True)
            nc.gpsimd.iota(item[:, :], pattern=[[1, NI]], base=0, channel_multiplier=0, allow_small_or_imprecise_dtypes=True)
            nc.gpsimd.iota(lane[:, :], pattern=[[1, M]], base=0, channel_multiplier=0, allow_small_or_imprecise_dtypes=True)
            me(pool, nc.gpsimd.memset(before[:, :], 1.0))
            nc.gpsimd.affine_select(out=before[:, :], in_=before[:, :], compare_op=ALU.is_ge, fill=0.0, base=-1,
                                    pattern=[[1, P]], channel_multiplier=-1).then_inc(iotas, 1)

        @block.tensor
        def _(pe):
            pe.wait_ge(rw_in, 16)
            for c in range(2):
                m = nc.tensor.transpose(k.ps[0][:, c * NE:(c + 1) * NE], rw[:, c * 128:(c + 1) * 128], k.ident[0:NE, 0:NE])
            m.then_inc(rw_turned, 1)
            pe.wait_ge(rw_ready, 1)

            def multiply(s):
                for c in range(2):
                    m = nc.tensor.matmul(k.ps[3 + s][0:P, 0:NE], q.xt[:, s, c, :], rwt[:, c, :], start=(c == 0), stop=(c == 1))
                return m

            q.on_tensor(pe, multiply)
            pe.wait_ge(iotas, 1)
            pe.wait_ge(chosen, 1)
            flat = both[:, :, :].rearrange("p t e -> p (t e)")
            nc.tensor.matmul(k.ps[0][0:P, 0:NT * NE], before[:, :], flat, start=True, stop=True)
            nc.tensor.matmul(k.ps[1][0:P, 0:NT * NE], k.ones[0:P, 0:P], flat, start=True, stop=True).then_inc(counted, 1)
            pe.wait_ge(places, 1)
            for j in range(2 * NT):
                m = nc.tensor.matmul(k.ps[2][:, 0:NI], at_lane[:, j, :], at_item[:, j, :], start=(j == 0), stop=(j == 2 * NT - 1))
            m.then_inc(tokens, 1)

        @block.scalar
        def _(act):
            norm_roots(k, act, deviations, roots)
            q.on_scalar(act)
            act.wait_ge(less_peak, 1)
            nc.scalar.activation(prob[:, :, :], prob[:, :, :], ACT.Exp).then_inc(exped, 1)

        @block.vector
        def _(dve):
            v, me = nc.vector, st["dve"]

            def wide(a):
                return a[:, :].rearrange("p (t a) -> p t a", a=1).to_broadcast([P, NT, NE])

            def long(a):
                return a[:, :].rearrange("p (a e) -> p a e", a=1).to_broadcast([P, NT, NE])

            dve.wait_ge(rw_turned, 1)
            v.tensor_copy(rwt[:, :, :], k.ps[0][:, 0:2 * NE].rearrange("p (a e) -> p a e", a=2)).then_inc(rw_ready, 1)
            norm_stats(k, dve, k.res, None, deviations, roots)

            def fill(t, s):
                me(dve, normed(k, q.xn[:, s, :], t))
                return v.tensor_scalar(tile_of(xn1, t), q.xn[:, s, :], 1.0, None, ALU.mult)

            def take(t, s):
                return v.tensor_scalar(tile_of(prob, t), k.ps[3 + s][0:P, 0:NE], 1.0, None, ALU.mult)

            q.on_vector(dve, fill, take, TB)
            me(dve, v.tensor_copy(den[:, :], k.rstd[:, :]))
            dve.sem_inc(logits_done, 1)
            me(dve, v.tensor_reduce(peak[:, :], prob[:, :, :], AX, ALU.max))
            v.tensor_tensor(prob[:, :, :], prob[:, :, :], wide(peak), ALU.subtract).then_inc(less_peak, 1)
            dve.wait_ge(exped, 1)
            me(dve, v.tensor_reduce(den[:, :], prob[:, :, :], AX, ALU.add))
            me(dve, v.reciprocal(den[:, :], den[:, :]))
            me(dve, v.tensor_tensor(prob[:, :, :], prob[:, :, :], wide(den), ALU.mult))
            dve.wait_ge(iotas, 1)
            v.tensor_copy(rest[:, :, :], prob[:, :, :])
            me(dve, v.tensor_scalar(tiles[:, :], expert[:, :], -float(NE), None, ALU.add))
            for j in range(2):
                me(dve, v.tensor_reduce(k.gate[:, j, :], rest[:, :, :], AX, ALU.max))
                me(dve, v.tensor_tensor(hit[:, :, :], rest[:, :, :], wide(k.gate[:, j, :]), ALU.is_equal))
                me(dve, v.tensor_tensor(cand[:, :, :], hit[:, :, :], long(tiles), ALU.mult))
                me(dve, v.tensor_reduce(idx[:, :], cand[:, :, :], AX, ALU.min))
                me(dve, v.tensor_scalar(idx[:, :], idx[:, :], float(NE), None, ALU.add))
                me(dve, v.tensor_tensor(oh[:, j, :, :], wide(idx), long(expert), ALU.is_equal))
                if j == 0:
                    me(dve, v.scalar_tensor_tensor(out=rest[:, :, :], in0=oh[:, 0, :, :], scalar=-2.0, in1=rest[:, :, :], op0=ALU.mult, op1=ALU.add))
            me(dve, v.tensor_tensor(both[:, :, :], oh[:, 0, :, :], oh[:, 1, :, :], ALU.add))
            dve.sem_inc(chosen, 1)
            me(dve, v.scalar_tensor_tensor(out=den[:, :], in0=k.gate[:, 0, :], scalar=1e-9, in1=k.gate[:, 1, :], op0=ALU.add, op1=ALU.add))
            me(dve, v.reciprocal(den[:, :], den[:, :]))
            for j in range(2):
                v.tensor_tensor(k.gate[:, j, :], k.gate[:, j, :], den[:, :], ALU.mult)
            dve.wait_ge(counted, 1)
            me(dve, v.tensor_copy(tot[:, :, :], k.ps[1][0:P, 0:NT * NE].rearrange("p (t e) -> p t e", e=NE)))
            for e in range(NE):
                m = v.tensor_tensor_scan(inc[:, :, e], k.ones[0:P, 0:NT], tot[:, :, e], 0.0, ALU.mult, ALU.add)
            me(dve, m)
            me(dve, v.tensor_scalar(tiles[:, :], inc[:, NT - 1, :], float(M - 1), None, ALU.add))
            me(dve, v.tensor_copy(tiles_i[:, :], tiles[:, :]))
            me(dve, v.tensor_single_scalar(tiles_i[:, :], tiles_i[:, :], 7, ALU.logical_shift_right))
            me(dve, v.tensor_copy(tiles[:, :], tiles_i[:, :]))
            me(dve, v.tensor_tensor_scan(ends[:, :], k.ones[0:P, 0:NE], tiles[:, :], 0.0, ALU.mult, ALU.add))
            me(dve, v.tensor_tensor(begins[:, :], ends[:, :], tiles[:, :], ALU.subtract))
            me(dve, v.tensor_scalar(begins[:, :], begins[:, :], float(M), None, ALU.mult))
            me(dve, v.tensor_tensor(slot[:, :, :], inc[:, :, :], tot[:, :, :], ALU.subtract))
            me(dve, v.tensor_tensor(slot[:, :, :], slot[:, :, :], k.ps[0][0:P, 0:NT * NE].rearrange("p (t e) -> p t e", e=NE), ALU.add))
            me(dve, v.tensor_tensor(slot[:, :, :], slot[:, :, :], long(begins), ALU.add))
            for j in range(2):
                me(dve, v.tensor_tensor(cand[:, :, :], oh[:, j, :, :], slot[:, :, :], ALU.mult))
                me(dve, v.tensor_reduce(pos[:, j, :], cand[:, :, :], AX, ALU.add))
            me(dve, v.tensor_copy(k.place[:, :, :], pos[:, :, :]))
            me(dve, v.tensor_single_scalar(hi_i[:, :, :], k.place[:, :, :], 7, ALU.logical_shift_right))
            me(dve, v.tensor_copy(hi[:, :, :], hi_i[:, :, :]))
            me(dve, v.scalar_tensor_tensor(out=lo[:, :, :], in0=hi[:, :, :], scalar=-float(M), in1=pos[:, :, :], op0=ALU.mult, op1=ALU.add))
            v.tensor_tensor(at_lane[:, :, :], lane[:, :].rearrange("p (a m) -> p a m", a=1).to_broadcast([P, 2 * NT, M]),
                            lo[:, :, :].rearrange("p j (t a) -> p (j t) a", a=1).to_broadcast([P, 2 * NT, M]), ALU.is_equal)
            me(dve, v.tensor_tensor(at_item[:, :, :], item[:, :].rearrange("p (a m) -> p a m", a=1).to_broadcast([P, 2 * NT, NI]),
                                    hi[:, :, :].rearrange("p j (t a) -> p (j t) a", a=1).to_broadcast([P, 2 * NT, NI]), ALU.is_equal))
            for j in range(2):
                m = v.tensor_tensor(at_item[:, j * NT:(j + 1) * NT, :], at_item[:, j * NT:(j + 1) * NT, :],
                                    k.node[:, :].rearrange("p (t a) -> p t a", a=1).to_broadcast([P, NT, NI]), ALU.mult)
            me(dve, m)
            dve.sem_inc(places, 1)
            me(dve, v.tensor_tensor(over[:, :, :], item[:, :].rearrange("p (i a) -> p i a", a=1).to_broadcast([P, NI, NE]),
                                    ends[:, :].rearrange("p (a e) -> p a e", a=1).to_broadcast([P, NI, NE]), ALU.is_ge))
            me(dve, v.tensor_reduce(of_item[:, :], over[:, :, :], AX, ALU.add))
            me(dve, v.tensor_scalar(k.item_expert[:, :], of_item[0:1, :], float(NE - 1), None, ALU.min))
            dve.wait_ge(tokens, 1)
            me(dve, v.tensor_copy(k.slot_token[:, :], k.ps[2][:, 0:NI]))


def weights_phase(k):
    nc = k.nc
    ctx = ExitStack()
    FB = HID // 128
    TAIL = HID - FB * 128
    with ctx:
        sb = lambda n, s, d=F32: k.sb(f"w_{n}", s, d, ctx)
        sem = lambda n: k.sem(f"w_{n}")
        raw = [[sb(f"raw{m}{s}", [128, FB + 1, C] if m < 2 else [128, 2, HID]) for s in range(2)] for m in range(3)]
        come = [[sem(f"come{m}{s}") for s in range(2)] for m in range(3)]
        turned, act_kept, dve_kept, used = sem("turned"), sem("act_kept"), sem("dve_kept"), sem("used")
        block = ctx.enter_context(nc.Block())
        names = ("L0_ffn_w1", "L0_ffn_w3", "L0_ffn_w2")

        def groups(e, s):
            for m in range(2):
                for c in range(2):
                    for b0, b1 in ((0, 4), (4, FB + 1)):
                        ins = [(raw[m][s][0:(128 if b < FB else TAIL), b, c * 128:(c + 1) * 128], (b - b0) * 128, 128 if b < FB else TAIL) for b in range(b0, b1)]
                        n = sum(x[2] for x in ins)
                        yield m, 128, ins, (k.w1t, k.w3t)[m][:, c, e, b0 * 128:b0 * 128 + n], n
            for a in range(2):
                for blocks in ((0, 1), (2,)):
                    rows = 128 if len(blocks) == 2 else HH - 256
                    ins = [(raw[2][s][:, c, a * HH + b * 128:a * HH + b * 128 + rows], (b - blocks[0]) * C + c * 128, 128) for b in blocks for c in range(2)]
                    yield 2, rows, ins, k.w2t[0:rows, 3 * a + blocks[0]:3 * a + blocks[-1] + 1, e, :], len(blocks) * C

        G = 12

        @block.sync
        def _(sp):
            for e in range(NE):
                s = e % 2
                if e >= 2:
                    sp.wait_ge(turned, G * (e - 1))
                for m, name in enumerate(names):
                    if m < 2:
                        sp.dma_start(raw[m][s][:, 0:FB, :], k.a[name][e, 0:FB * 128, :].rearrange("(b p) c -> p b c", p=128)).then_inc(come[m][s], 16)
                        sp.dma_start(raw[m][s][0:TAIL, FB, :], k.a[name][e, FB * 128:HID, :]).then_inc(come[m][s], 16)
                    else:
                        sp.dma_start(raw[m][s][:, :, :], k.a[name][e].rearrange("(a p) h -> p a h", p=128)).then_inc(come[m][s], 16)

        @block.tensor
        def _(pe):
            n = 0
            for e in range(NE):
                s = e % 2
                for m, rows, ins, dst, width in groups(e, s):
                    pe.wait_ge(come[m][s], (32 if m < 2 else 16) * (e // 2 + 1))
                    if n >= 8:
                        pe.wait_ge((act_kept, dve_kept)[n % 2], (n - 8) // 2 + 1)
                    for x, at, w in ins:
                        t = nc.tensor.transpose(k.ps[n % 8][0:rows, at:at + w], x, k.ident[0:x.shape[0], 0:x.shape[0]])
                    t.then_inc(turned, 1)
                    n += 1

        def keep(eng, odd, copy, kept):
            n = 0
            for e in range(NE):
                for m, rows, ins, dst, width in groups(e, e % 2):
                    if n % 2 == odd:
                        eng.wait_ge(turned, n + 1)
                        src = k.ps[n % 8][0:rows, 0:width]
                        copy(dst, src if m < 2 else src.rearrange("p (b c) -> p b c", c=C)).then_inc(kept, 1)
                    n += 1

        @block.scalar
        def _(act):
            keep(act, 0, nc.scalar.copy, act_kept)

        @block.vector
        def _(dve):
            keep(dve, 1, nc.vector.tensor_copy, dve_kept)


def experts_phase(k):
    nc = k.nc
    ctx = ExitStack()
    with ctx:
        sb = lambda n, s, d=F32: k.sb(f"e_{n}", s, d, ctx)
        sem = lambda n: k.sem(f"e_{n}")
        ix = [sb(f"ix{s}", [M, 1], I32) for s in range(2)]
        x = [sb(f"x{s}", [M, C]) for s in range(2)]
        xt = [sb(f"xt{s}", [128, 2, M]) for s in range(2)]
        gated = [sb(f"gated{a}", [M, HH]) for a in range(2)]
        h = [sb(f"h{a}", [M, HH]) for a in range(2)]
        ht = [sb(f"ht{s}", [128, 6, M]) for s in range(2)]
        y = [sb(f"y{s}", [M, C]) for s in range(2)]
        x_in = [k.gather_sem(f"e_x_in{s}") for s in range(2)]
        y_out = [sem(f"y_out{s}") for s in range(2)]
        ix_made, issuing, x_turned, x_kept = sem("ix_made"), sem("issuing"), sem("x_turned"), sem("x_kept")
        up, silued, h_made, h_turned, h_kept = sem("up"), sem("silued"), sem("h_made"), sem("h_turned"), sem("h_kept")
        down, y_kept, y_free = sem("down"), sem("y_kept"), sem("y_free")
        block = ctx.enter_context(nc.Block())
        TURN, UP, GATE, TH, DOWN = k.ps[0], (k.ps[1], k.ps[3]), (k.ps[2], k.ps[4]), (k.ps[5], k.ps[6]), k.ps[7]

        @block.gpsimd
        def _(pool):
            with pool.Fori(0, NI // 2) as i:
                for s in range(2):
                    pool.wait_ge(x_turned, i * 2 + s + 1)
                    nc.gpsimd.tensor_copy(ix[s][:, :], k.slot_token[:, bass.ds(i * 2 + s, 1)]).then_inc(ix_made, 1)
                    pool.wait_ge(ix_made, i * 2 + s + 1)
                    pool.sem_inc(issuing, 1)
                    pool.indirect_dma_start(out=x[s][:, :], out_offset=None, in_=k.xn_tab,
                                            in_offset=bass.IndirectOffsetOnAxis(ap=ix[s][:, 0:1], axis=0)).then_inc(x_in[s], 16)

        @block.sync
        def _(sp):
            rows = k.y_tab.rearrange("(i p) c -> i p c", p=M)
            sp.sem_inc(y_free, 2)
            with sp.Fori(0, NI // 2) as i:
                for s in range(2):
                    sp.wait_ge(y_kept, i * 2 + s + 2)
                    sp.dma_start(rows[bass.ds(i * 2 + s, 1), :, :].rearrange("a p c -> (a p) c"), y[s][:, :]).then_inc(y_out[s], 16)
                    sp.wait_ge(y_out[s], 16 * i + 16)
                    sp.sem_inc(y_free, 1)

        @block.tensor
        def _(pe):
            pe.sem_inc(x_turned, 2)
            pe.sem_inc(h_turned, 2)

            def turn_x(i, s):
                pe.wait_ge(x_in[s], 16 * ((i - s) // 2) + 16 if isinstance(i, int) else x_in_at[s] * 16 + 16)
                pe.wait_ge(x_kept, i + 1)
                for c in range(2):
                    m = nc.tensor.transpose(TURN[:, c * M:(c + 1) * M], x[s][:, c * 128:(c + 1) * 128], k.ident[:, :])
                m.then_inc(x_turned, 1)

            x_in_at = {}

            def go_up(i, s, a, e):
                if a == 0:
                    pe.wait_ge(x_kept, i + 2)
                pe.wait_ge(h_made, 2 * i + a + 1)
                for bank, w in ((UP[a], k.w1t), (GATE[a], k.w3t)):
                    for c in range(2):
                        m = nc.tensor.matmul(bank[:, 0:HH], xt[s][:, c, :], weights(w, c, e, a), start=(c == 0), stop=(c == 1))
                m.then_inc(up, 1)

            def weights(w, c, e, a):
                return w[:, c, bass.ds(e, 1), a * HH:(a + 1) * HH].rearrange("p a h -> p (a h)")

            def turn_h(i, s, a):
                pe.wait_ge(h_made, 2 * i + a + 3)
                pe.wait_ge(h_kept, 2 * i + a + 1)
                for (_, b, n) in HB[3 * a:3 * a + 3]:
                    m = nc.tensor.transpose(TH[a][0:n, b * M:(b + 1) * M], h[a][:, b * 128:b * 128 + n], k.ident[:, :])
                m.then_inc(h_turned, 1)

            def go_down(i, s, e):
                pe.wait_ge(h_kept, 2 * i + 4)
                pe.wait_ge(y_kept, i + 1)
                for j, (a, b, n) in enumerate(HB):
                    m = nc.tensor.matmul(DOWN[:, 0:C], ht[s][0:n, j, :], k.w2t[0:n, j, bass.ds(e, 1), :].rearrange("p a c -> p (a c)"),
                                         start=(j == 0), stop=(j == 5))
                m.then_inc(down, 1)

            def expert(i):
                return pe.value_load(k.item_expert[0:1, bass.ds(i, 1)], min_val=0, max_val=NE - 1)

            e0 = expert(0)
            turn_x(0, 0)
            go_up(0, 0, 0, e0)
            go_up(0, 0, 1, e0)
            turn_h(0, 0, 0)
            turn_x(1, 1)

            def item(i, s, more=True):
                e, e_before = expert(i), expert(i - 1)
                go_up(i, s, 0, e)
                turn_h(i - 1, 1 - s, 1)
                go_up(i, s, 1, e)
                go_down(i - 1, 1 - s, e_before)
                turn_h(i, s, 0)
                if more:
                    turn_x(i + 1, 1 - s)

            with pe.Fori(0, NI // 2 - 1) as i:
                x_in_at[0], x_in_at[1] = i + 1, i + 1
                item(i * 2 + 1, 1)
                item(i * 2 + 2, 0)
            item(NI - 1, 1, more=False)
            turn_h(NI - 1, 1, 1)
            go_down(NI - 1, 1, expert(NI - 1))

        @block.scalar
        def _(act):
            act.sem_inc(x_kept, 1)
            act.sem_inc(h_kept, 2)
            act.sem_inc(y_kept, 1)

            def keep_x(i, s):
                act.wait_ge(x_turned, i + 3)
                nc.scalar.copy(xt[s][:, :, :].rearrange("p a m -> p (a m)"), TURN[:, 0:2 * M]).then_inc(x_kept, 1)

            def silu(i, a):
                act.wait_ge(up, 2 * i + a + 1)
                nc.scalar.activation(gated[a][:, :], UP[a][:, 0:HH], ACT.Silu).then_inc(silued, 1)

            def keep_h(i, s, a):
                act.wait_ge(h_turned, 2 * i + a + 3)
                j = 3 * a
                nc.scalar.copy(ht[s][:, j:j + 2, :].rearrange("p b m -> p (b m)"), TH[a][:, 0:2 * M])
                n = HB[j + 2][2]
                nc.scalar.copy(ht[s][0:n, j + 2, :], TH[a][0:n, 2 * M:3 * M]).then_inc(h_kept, 1)

            def keep_y(i, s):
                act.wait_ge(down, i + 1)
                act.wait_ge(y_free, i + 1)
                nc.scalar.copy(y[s][:, :], DOWN[:, 0:C]).then_inc(y_kept, 1)

            keep_x(0, 0)
            silu(0, 0)
            silu(0, 1)
            keep_h(0, 0, 0)
            keep_x(1, 1)

            def item(i, s, more=True):
                silu(i, 0)
                keep_h(i - 1, 1 - s, 1)
                silu(i, 1)
                keep_y(i - 1, 1 - s)
                keep_h(i, s, 0)
                if more:
                    keep_x(i + 1, 1 - s)

            with act.Fori(0, NI // 2 - 1) as i:
                item(i * 2 + 1, 1)
                item(i * 2 + 2, 0)
            item(NI - 1, 1, more=False)
            keep_h(NI - 1, 1, 1)
            keep_y(NI - 1, 1)

        @block.vector
        def _(dve):
            dve.sem_inc(h_made, 2)
            with dve.Fori(0, NI) as i:
                for a in range(2):
                    dve.wait_ge(silued, i * 2 + a + 1)
                    dve.wait_ge(up, i * 2 + a + 1)
                    dve.wait_ge(h_turned, i * 2 + a + 1)
                    nc.vector.tensor_tensor(h[a][:, :], gated[a][:, :], GATE[a][:, 0:HH], ALU.mult).then_inc(h_made, 1)


def combine_phase(k):
    nc, st = k.nc, k.steps
    ctx = ExitStack()
    with ctx:
        sb = lambda n, s, d=F32: k.sb(f"c_{n}", s, d, ctx)
        sem = lambda n: k.sem(f"c_{n}")
        ys = sb("ys", [P, TB, 2, C])
        ix = sb("ix", [P, 2, TB], I32)
        x1_in, ix_made, issuing, rows_used = sem("x1_in"), sem("ix_made"), sem("issuing"), sem("rows_used")
        rows_in = k.gather_sem("c_rows_in")
        block = ctx.enter_context(nc.Block())

        @block.sync
        def _(sp):
            sp.dma_start(k.res[:, :, :], k.x1_tab.rearrange("(p t) c -> p t c", p=P)).then_inc(x1_in, 16)

        @block.gpsimd
        def _(pool):
            with pool.Fori(0, NT // TB) as i:
                pool.wait_ge(rows_used, i + 1)
                nc.gpsimd.tensor_copy(ix[:, 0, :], k.place[:, 0, bass.ds(i * TB, TB)])
                nc.gpsimd.tensor_copy(ix[:, 1, :], k.place[:, 1, bass.ds(i * TB, TB)]).then_inc(ix_made, 1)
                pool.wait_ge(ix_made, i + 1)
                pool.sem_inc(issuing, 1)
                for s in range(TB):
                    for j in range(2):
                        pool.indirect_dma_start(out=ys[:, s, j, :], out_offset=None, in_=k.y_tab,
                                                in_offset=bass.IndirectOffsetOnAxis(ap=ix[:, j, s:s + 1], axis=0)).then_inc(rows_in, 16)

        @block.vector
        def _(dve):
            v, me = nc.vector, st["dve"]
            dve.sem_inc(rows_used, 1)
            dve.wait_ge(x1_in, 16)
            with dve.Fori(0, NT // TB) as i:
                me.loop(i, 2)
                dve.wait_ge(rows_in, 32 * TB * i + 32 * TB)
                for j in range(2):
                    for s in range(TB):
                        r = tile_of(k.res, i * TB + s)
                        m = v.scalar_tensor_tensor(out=r, in0=ys[:, s, j, :], scalar=k.gate[:, j, bass.ds(i * TB + s, 1)], in1=r, op0=ALU.mult, op1=ALU.add)
                    me(dve, m)
                dve.sem_inc(rows_used, 1)
                me.end(NT // TB)


def gnn_table_phase(k):
    nc, st = k.nc, k.steps
    ctx = ExitStack()
    with ctx:
        xn = k.sb("g_xn", [P, NT, C], F32, ctx)
        deviations, roots, made, out_done = (k.sem(f"g_{n}") for n in ("deviations", "roots", "made", "out_done"))
        block = ctx.enter_context(nc.Block())

        @block.sync
        def _(sp):
            sp.wait_ge(made, NT)
            sp.dma_start(k.xn_tab.rearrange("(p t) c -> p t c", p=P), xn[:, :, :]).then_inc(out_done, 16)
            sp.wait_ge(out_done, 16)

        @block.scalar
        def _(act):
            norm_roots(k, act, deviations, roots)

        @block.vector
        def _(dve):
            norm_stats(k, dve, k.res, None, deviations, roots)
            with dve.Fori(0, NT) as t:
                normed(k, tile_of(xn, t), t).then_inc(made, 1)


def gnn_node_phase(k):
    nc, st = k.nc, k.steps
    ctx = ExitStack()
    with ctx:
        sb = lambda n, s, d=F32: k.sb(f"n_{n}", s, d, ctx)
        sem = lambda n: k.sem(f"n_{n}")
        q = Turning(k, "n", ctx)
        w, wt = sb("w", [128, 2, C]), sb("wt", [128, 2, C])
        bias = sb("bias", [P, C])
        inv, part = sb("inv", [P, NT]), sb("part", [P, NT])
        main, chain = sb("main", [P, TB, RW]), sb("chain", [P, TB, RW])
        ix = sb("ix", [P, 2, TB], I32)
        w_in, bias_in, w_turned, w_ready = sem("w_in"), sem("bias_in"), sem("w_turned"), sem("w_ready")
        gathering = sem("ix_made"), sem("issuing"), k.gather_sem("n_rows_in"), sem("rows_used")
        rows_in, rows_used = gathering[2:]
        block = ctx.enter_context(nc.Block())

        @block.sync
        def _(sp):
            sp.dma_start(w[:, :, :], k.a["L1_gnn_W"].rearrange("(a p) c -> p a c", p=128)).then_inc(w_in, 16)
            sp.dma_start(bias[:, :], k.a["L1_gnn_b"].rearrange("(a c) -> a c", a=1).to_broadcast([P, C])).then_inc(bias_in, 16)

        @block.gpsimd
        def _(pool):
            gather_nodes(k, pool, C, main, chain, ix, gathering)

        @block.tensor
        def _(pe):
            pe.wait_ge(w_in, 16)
            for c in range(2):
                for a in range(2):
                    m = nc.tensor.transpose(k.ps[c][:, a * 128:(a + 1) * 128], w[:, a, c * 128:(c + 1) * 128], k.ident[:, :])
                m.then_inc(w_turned, 1)
            pe.wait_ge(w_ready, 2)

            def multiply(s):
                for c in range(2):
                    m = nc.tensor.matmul(k.ps[3 + s][0:P, 0:C], q.xt[:, s, c, :], wt[:, c, :], start=(c == 0), stop=(c == 1))
                return m

            q.on_tensor(pe, multiply)

        @block.scalar
        def _(act):
            q.on_scalar(act)

        @block.vector
        def _(dve):
            v, me = nc.vector, st["dve"]
            dve.sem_inc(rows_used, 1)
            me(dve, v.tensor_scalar(inv[:, :], k.deg[:, :], 1.0, None, ALU.add))
            me(dve, v.reciprocal(inv[:, :], inv[:, :]))
            me(dve, v.tensor_tensor(part[:, :], inv[:, :], k.deg[:, :], ALU.mult))
            for c in range(2):
                dve.wait_ge(w_turned, c + 1)
                v.tensor_copy(wt[:, c, :], k.ps[c][:, 0:C]).then_inc(w_ready, 1)
            dve.wait_ge(bias_in, 16)
            with dve.Fori(0, NT) as t:
                me.loop(t, 1)
                me(dve, v.scalar_tensor_tensor(out=tile_of(k.res, t), in0=bias[:, :], scalar=part[:, bass.ds(t, 1)], in1=tile_of(k.res, t), op0=ALU.mult, op1=ALU.add))
                me.end(NT)

            def fill(t, s):
                if s == 0:
                    dve.wait_ge(rows_in, t * 32 + 32 * TB)
                return v.tensor_tensor(q.xn[:, s, :], main[:, s, 0:C], chain[:, s, 0:C], ALU.add)

            def take(t, s):
                return v.scalar_tensor_tensor(out=tile_of(k.res, t), in0=k.ps[3 + s][0:P, 0:C], scalar=inv[:, bass.ds(t, 1)], in1=tile_of(k.res, t), op0=ALU.mult, op1=ALU.add)

            q.on_vector(dve, fill, take, rows_free=rows_used)


HD = 64
NP = H * HD // 128
HG = H * HD


def attention_phase(k):
    nc, st = k.nc, k.steps
    ctx = ExitStack()
    with ctx:
        sb = lambda n, s, d=F32: k.sb(f"t_{n}", s, d, ctx)
        sem = lambda n: k.sem(f"t_{n}")
        w_x, w_fx = sb("w_x", [128, 2, HG]), sb("w_fx", [128, 2, HG])
        w_out = sb("w_out", [128, NP, C])
        w_xt = sb("w_xt", [128, NP, C])
        square = sb("square", [128, 4, 128])
        diag = sb("diag", [128, 128])
        w_comb = sb("w_comb", [128, 2, HG])
        b_x, b_fx, b_slice = sb("b_x", [128, NP]), sb("b_fx", [1, HG]), sb("b_slice", [1, H, HD])
        temp, temp_b = sb("temp", [1, H]), sb("temp_b", [128, H])
        bias_row, bias = sb("bias_row", [1, HG]), sb("bias", [P, HG])
        b_out = sb("b_out", [P, C])
        xn = sb("xn", [P, TB, C + 1])
        xt = sb("xt", [128, TB, 2, P])
        logit = sb("logit", [P, TB, H, HD])
        peak, total = sb("peak", [P, TB, H]), sb("total", [P, TB, H])
        wt = sb("wt", [128, NT, NP, P])
        u, inv = sb("u", [128, NP, C + 1]), sb("inv", [128, NP])
        ut, share = sb("ut", [128, 2, HG]), sb("share", [1, HG])
        token, qt, kt, val = (sb(n, [128, NP, 128]) for n in ("token", "qt", "kt", "val"))
        score, attn, attn_t, mixed = sb("score", [128, NP, HD]), sb("attn", [128, NP, 128]), sb("attn_t", [128, NP, 128]), sb("mixed", [128, NP, 128])
        apeak, asum = sb("apeak", [128, NP]), sb("asum", [128, NP])
        v2 = sb("v2", [128, NP, C])
        squares0, squares_in, w_in, small_in, xones, bout_in = (sem(n) for n in ("squares0", "squares_in", "w_in", "small_in", "xones", "bout_in"))
        deviations, roots, prep, prep_pe = (sem(n) for n in ("deviations", "roots", "prep", "prep_pe"))
        made, turned, kept, logits, biased, peaked, less, exped, summed, weighed, w_turned, w_kept, added = (
            sem(n) for n in ("made", "turned", "kept", "logits", "biased", "peaked", "less", "exped", "summed", "weighed", "w_turned", "w_kept", "added"))
        mid, mid_pe, mid_act = sem("mid"), sem("mid_pe"), sem("mid_act")
        result, joined, stored = sem("result"), sem("joined"), sem("stored")
        block = ctx.enter_context(nc.Block())
        T, L, X, U = k.ps[0], (k.ps[1], k.ps[2]), k.ps[3], k.ps[4:8]

        @block.sync
        def _(sp):
            for t, name in ((w_x, "L1_ffn_W_x"), (w_fx, "L1_ffn_W_fx"), (w_out, "L1_ffn_W_out")):
                sp.dma_start(t[:, :, :], k.a[name].rearrange("(a p) c -> p a c", p=128)).then_inc(w_in, 16)
            sp.dma_start(b_fx[:, :], k.a["L1_ffn_b_fx"].rearrange("(a c) -> a c", a=1)).then_inc(small_in, 16)
            with nc.allow_non_contiguous_dma(reason="512 single values"):
                sp.dma_start(b_x[:, :], k.a["L1_ffn_b_x"].rearrange("(a p) -> p a", p=128)).then_inc(small_in, 16)
            sp.dma_start(b_slice[:, :, :], k.a["L1_ffn_b_slice"].rearrange("(a b c) -> a b c", a=1, b=1).to_broadcast([1, H, HD])).then_inc(small_in, 16)
            sp.dma_start(temp[:, :], k.a["L1_ffn_temperature"].rearrange("a h b c -> a (h b c)")).then_inc(small_in, 16)
            sp.dma_start(temp_b[:, :], k.a["L1_ffn_temperature"].rearrange("a h b c -> a (h b c)").to_broadcast([128, H])).then_inc(small_in, 16)
            sp.dma_start(b_out[:, :], k.a["L1_ffn_b_out"].rearrange("(a c) -> a c", a=1).to_broadcast([P, C])).then_inc(bout_in, 16)
            sp.wait_ge(squares0, 1)
            for i, name in enumerate(("L1_ffn_W_slice", "L1_ffn_W_q", "L1_ffn_W_k", "L1_ffn_W_v")):
                for d in range(2):
                    sp.dma_start(square[64 * d:64 * d + 64, i, 64 * d:64 * d + 64], k.a[name]).then_inc(squares_in, 16)
            rows = k.out.rearrange("(p t) c -> p t c", p=P)
            with sp.Fori(0, NT // TB) as i:
                sp.wait_ge(joined, i * TB + TB)
                sp.dma_start(rows[:, bass.ds(i * TB, TB), :], k.res[:, bass.ds(i * TB, TB), :]).then_inc(stored, 16)
            sp.wait_ge(stored, 16 * (NT // TB))

        @block.gpsimd
        def _(pool):
            g, me = nc.gpsimd, st["pool"]
            g.memset(square[:, :, :], 0.0).then_inc(squares0, 1)
            g.memset(attn[:, :, :], 0.0)
            me(pool, g.memset(diag[:, :], 0.0))
            g.memset(diag[0:64, 0:64], 1.0)
            g.memset(diag[64:128, 64:128], 1.0).then_inc(xones, 1)
            pool.wait_ge(xones, 1)
            g.memset(xn[:, :, C:C + 1], 1.0).then_inc(xones, 1)

            def less_peak(t, s):
                pool.wait_ge(peaked, t + 1)
                g.tensor_tensor(logit[:, s, :, :], logit[:, s, :, :], peak[:, s, :].rearrange("p (h a) -> p h a", a=1).to_broadcast([P, H, HD]), ALU.subtract).then_inc(less, 1)

            def weigh(t, s):
                pool.wait_ge(summed, t + 1)
                g.tensor_tensor(logit[:, s, :, :], logit[:, s, :, :], total[:, s, :].rearrange("p (h a) -> p h a", a=1).to_broadcast([P, H, HD]), ALU.mult).then_inc(weighed, 1)

            def body(i):
                for s in range(TB):
                    less_peak(i * TB + s, s)
                    if s or not isinstance(i, int):
                        weigh(i * TB + s - 1, (s - 1) % TB)

            body(0)
            with pool.Fori(1, NT // TB) as i:
                body(i)
            weigh(NT - 1, TB - 1)

        @block.tensor
        def _(pe):
            t_ = nc.tensor
            pe.wait_ge(w_in, 48)
            for a in range(NP):
                for c in range(2):
                    m = t_.transpose(k.ps[a][:, c * 128:(c + 1) * 128], w_x[:, c, a * 128:(a + 1) * 128], k.ident[:, :])
                m.then_inc(prep_pe, 1)
            pe.wait_ge(squares_in, 128)
            pe.wait_ge(small_in, 80)
            pe.wait_ge(prep, NP)
            for c in range(2):
                for a in range(NP):
                    m = t_.matmul(k.ps[4 + c][:, a * 128:(a + 1) * 128], w_xt[:, a, c * 128:(c + 1) * 128], square[:, 0, :], start=True, stop=True)
                m.then_inc(prep_pe, 1)
            for a in range(NP):
                m = t_.matmul(k.ps[6][0:1, a * 128:(a + 1) * 128], b_x[:, a:a + 1], square[:, 0, :], start=True, stop=True)
            m.then_inc(prep_pe, 1)
            pe.wait_ge(prep, NP + 1)
            t_.matmul(k.ps[7][0:P, :], k.ones[0:1, 0:P], bias_row[:, :], start=True, stop=True).then_inc(prep_pe, 1)
            pe.wait_ge(prep, NP + 4)
            pe.wait_ge(xones, 2)

            def turn(t, s):
                pe.wait_ge(made, t + 1)
                pe.wait_ge(kept, t + 1)
                for c in range(2):
                    m = t_.transpose(T[:, c * P:(c + 1) * P], xn[:, s, c * 128:(c + 1) * 128], k.ident[0:P, 0:P])
                m.then_inc(turned, 1)

            def score_nodes(t, s, bank, biased_at):
                pe.wait_ge(kept, t + 2)
                pe.wait_ge(biased, biased_at)
                for c in range(2):
                    m = t_.matmul(bank[0:P, :], xt[:, s, c, :], w_comb[:, c, :], start=(c == 0), stop=(c == 1))
                m.then_inc(logits, 1)

            def slices(t, s, first=False, last=False):
                pe.wait_ge(weighed, t + 1)
                pe.wait_ge(w_kept, t + 1)
                w = logit[:, s, :, :].rearrange("p h g -> p (h g)")
                for a in range(NP):
                    m = t_.transpose(X[:, a * P:(a + 1) * P], w[:, a * 128:(a + 1) * 128], k.ident[0:P, 0:P])
                m.then_inc(w_turned, 1)
                for a in range(NP):
                    m = t_.matmul(U[a][:, 0:C + 1], w[:, a * 128:(a + 1) * 128], xn[:, s, :], start=first, stop=last, skip_group_check=True)
                m.then_inc(added, 1)

            def body(i):
                for s in range(TB):
                    t = i * TB + s
                    turn(t, s)
                    score_nodes(t, s, L[s % 2], t + 1 if s == 0 else t)
                    if s >= 2 or not isinstance(i, int):
                        slices(t - 2, (s - 2) % TB, first=isinstance(t, int) and t == 2)

            body(0)
            with pe.Fori(1, NT // TB) as i:
                body(i)
            slices(NT - 2, TB - 2)
            slices(NT - 1, TB - 1, last=True)

            pe.wait_ge(w_kept, NT + 1)
            pe.wait_ge(mid, 1)
            for c in range(2):
                for a in range(NP):
                    m = t_.transpose(k.ps[c][:, a * 128:(a + 1) * 128], u[:, a, c * 128:(c + 1) * 128], k.ident[:, :])
                m.then_inc(mid_pe, 1)
            for a in range(NP):
                m = t_.transpose(k.ps[2][0:1, a * 128:(a + 1) * 128], u[:, a, C:C + 1], k.ident[:, :])
            m.then_inc(mid_pe, 1)
            pe.wait_ge(mid, 4)
            for a in range(NP):
                cols = slice(a * 128, (a + 1) * 128)
                for c in range(2):
                    t_.matmul(k.ps[3][:, cols], w_fx[:, c, cols], ut[:, c, cols], start=(c == 0), stop=False)
                m = t_.matmul(k.ps[3][:, cols], b_fx[:, cols], share[:, cols], start=False, stop=True)
            m.then_inc(mid_pe, 1)
            pe.wait_ge(mid, 5)
            for a in range(NP):
                cols = slice(a * 128, (a + 1) * 128)
                t_.matmul(k.ps[4][:, cols], square[:, 1, :], token[:, a, :], start=True, stop=True)
                t_.matmul(k.ps[5][:, cols], square[:, 2, :], token[:, a, :], start=True, stop=True)
                m = t_.matmul(k.ps[6][:, cols], token[:, a, :], square[:, 3, :], start=True, stop=True)
            m.then_inc(mid_pe, 1)
            pe.wait_ge(mid, 8)
            for a in range(NP):
                m = t_.matmul(k.ps[7][:, a * 128:(a + 1) * 128], qt[:, a, :], kt[:, a, :], start=True, stop=True)
            m.then_inc(mid_pe, 1)
            pe.wait_ge(mid, 9)
            for a in range(NP):
                m = t_.transpose(k.ps[0][:, a * 128:(a + 1) * 128], attn[:, a, :], k.ident[:, :])
            m.then_inc(mid_pe, 1)
            pe.wait_ge(mid, 10)
            for a in range(NP):
                m = t_.matmul(k.ps[1][:, a * 128:(a + 1) * 128], val[:, a, :], attn_t[:, a, :], start=True, stop=True)
            m.then_inc(mid_pe, 1)
            pe.wait_ge(mid, 11)
            for a in range(NP):
                m = t_.matmul(k.ps[2 + a // 2][:, (a % 2) * C:(a % 2 + 1) * C], mixed[:, a, :], w_out[:, a, :], start=True, stop=True)
            m.then_inc(mid_pe, 1)
            pe.wait_ge(mid, 13)

            for t in range(NT):
                if t >= 8:
                    pe.wait_ge(joined, t - 7)
                for a in range(NP):
                    m = t_.matmul(k.ps[t % 8][0:P, 0:C], wt[:, t, a, :], v2[:, a, :], start=(a == 0), stop=(a == NP - 1))
                m.then_inc(result, 1)

        @block.scalar
        def _(act):
            a_ = nc.scalar
            norm_roots(k, act, deviations, roots)
            act.sem_inc(kept, 1)
            act.sem_inc(w_kept, 1)

            def keep(t, s):
                act.wait_ge(turned, t + 1)
                a_.copy(xt[:, s, :, :].rearrange("p a n -> p (a n)"), T[:, 0:2 * P]).then_inc(kept, 1)

            def exp(t, s):
                act.wait_ge(less, t + 1)
                a_.activation(logit[:, s, :, :], logit[:, s, :, :], ACT.Exp).then_inc(exped, 1)

            def keep_w(t, s):
                act.wait_ge(w_turned, t + 1)
                a_.copy(wt[:, bass.ds(t, 1), :, :].rearrange("p b a n -> p (b a n)"), X[:, 0:NP * P]).then_inc(w_kept, 1)

            def body(i):
                for s in range(TB):
                    t = i * TB + s
                    keep(t, s)
                    if s or not isinstance(i, int):
                        exp(t - 1, (s - 1) % TB)
                    if s >= 2 or not isinstance(i, int):
                        keep_w(t - 2, (s - 2) % TB)

            body(0)
            with act.Fori(1, NT // TB) as i:
                body(i)
            exp(NT - 1, TB - 1)
            keep_w(NT - 2, TB - 2)
            keep_w(NT - 1, TB - 1)
            act.wait_ge(mid_act, 1)
            a_.activation(score[:, :, :], score[:, :, :], ACT.Exp, scale=float(HD) ** -0.5).then_inc(mid_act, 1)

        @block.vector
        def _(dve):
            v, me = nc.vector, st["dve"]
            norm_stats(k, dve, k.res, None, deviations, roots)
            for a in range(NP):
                dve.wait_ge(prep_pe, a + 1)
                v.tensor_copy(w_xt[:, a, :], k.ps[a][:, 0:C]).then_inc(prep, 1)
            dve.wait_ge(small_in, 80)
            for t in (temp, temp_b):
                me(dve, v.tensor_scalar(t[:, :], t[:, :], 0.1, 5.0, ALU.max, ALU.min))
                me(dve, v.reciprocal(t[:, :], t[:, :]))
            dve.wait_ge(prep_pe, NP + 3)
            me(dve, v.tensor_tensor(bias_row[:, :], k.ps[6][0:1, :], b_slice[:, :, :].rearrange("p h g -> p (h g)"), ALU.add))
            r = bias_row[:, :].rearrange("p (h g) -> p h g", h=H)
            v.tensor_tensor(r, r, temp[:, :].rearrange("p (h a) -> p h a", a=1).to_broadcast([1, H, HD]), ALU.mult).then_inc(prep, 1)
            for c in range(2):
                v.tensor_tensor(w_comb[:, c, :].rearrange("p (h g) -> p h g", h=H), k.ps[4 + c][:, :].rearrange("p (h g) -> p h g", h=H),
                                temp_b[:, :].rearrange("p (h a) -> p h a", a=1).to_broadcast([128, H, HD]), ALU.mult).then_inc(prep, 1)
            dve.wait_ge(prep_pe, NP + 4)
            v.tensor_copy(bias[:, :], k.ps[7][0:P, :]).then_inc(prep, 1)
            dve.wait_ge(prep, NP + 4)
            dve.wait_ge(xones, 2)
            dve.sem_inc(biased, 1)

            def fill(t, s):
                normed(k, xn[:, s, 0:C], t).then_inc(made, 1)

            def add_bias(t, s):
                dve.wait_ge(logits, t + 1)
                v.tensor_tensor(logit[:, s, :, :].rearrange("p h g -> p (h g)"), L[s % 2][0:P, :], bias[:, :], ALU.add).then_inc(biased, 1)
                dve.wait_ge(biased, t + 2)
                v.tensor_reduce(peak[:, s, :], logit[:, s, :, :], AX, ALU.max).then_inc(peaked, 1)

            def add_up(t, s):
                dve.wait_ge(exped, t + 1)
                me(dve, v.tensor_reduce(total[:, s, :], logit[:, s, :, :], AX, ALU.add))
                v.reciprocal(total[:, s, :], total[:, s, :]).then_inc(summed, 1)

            def body(i):
                first = isinstance(i, int)
                if not first:
                    me.loop(i - 1, TB)
                for s in range(TB):
                    if not first:
                        dve.wait_ge(added, i * TB + s - TB + 1)
                    fill(i * TB + s, s)
                    add_bias(i * TB + s, s)
                    if s or not first:
                        add_up(i * TB + s - 1, (s - 1) % TB)
                if not first:
                    me.end(NT // TB - 1)

            body(0)
            with dve.Fori(1, NT // TB) as i:
                body(i)
            add_up(NT - 1, TB - 1)

            dve.wait_ge(added, NT)
            for a in range(NP):
                m = v.tensor_scalar(inv[:, a:a + 1], U[a][:, C:C + 1], 1e-5, None, ALU.add)
            me(dve, m)
            me(dve, v.reciprocal(inv[:, :], inv[:, :]))
            for a in range(NP):
                m = v.tensor_scalar(u[:, a, :], U[a][:, 0:C + 1], inv[:, a:a + 1], None, ALU.mult)
            m.then_inc(mid, 1)
            for c in range(2):
                dve.wait_ge(mid_pe, c + 1)
                v.tensor_copy(ut[:, c, :], k.ps[c][:, :]).then_inc(mid, 1)
            dve.wait_ge(mid_pe, 3)
            v.tensor_copy(share[:, :], k.ps[2][0:1, :]).then_inc(mid, 1)
            dve.wait_ge(mid_pe, 4)
            v.tensor_tensor(token[:, :, :], k.ps[3][:, :].rearrange("p (a g) -> p a g", a=NP),
                            diag[:, :].rearrange("p (b g) -> p b g", b=1).to_broadcast([128, NP, 128]), ALU.mult).then_inc(mid, 1)
            dve.wait_ge(mid_pe, 5)
            for t, b in ((qt, 4), (kt, 5), (val, 6)):
                v.tensor_copy(t[:, :, :].rearrange("p a g -> p (a g)"), k.ps[b][:, :]).then_inc(mid, 1)
            dve.wait_ge(mid_pe, 6)
            for d in range(2):
                rows = slice(64 * d, 64 * d + 64)
                m = v.tensor_copy(score[rows, :, :], k.ps[7][rows, :].rearrange("p (a g) -> p a g", a=NP)[:, :, 64 * d:64 * d + 64])
            me(dve, m)
            me(dve, v.tensor_reduce(apeak[:, :], score[:, :, :], AX, ALU.max))
            v.tensor_tensor(score[:, :, :], score[:, :, :], apeak[:, :].rearrange("p (a b) -> p a b", b=1).to_broadcast([128, NP, HD]), ALU.subtract).then_inc(mid_act, 1)
            dve.wait_ge(mid_act, 2)
            me(dve, v.tensor_reduce(asum[:, :], score[:, :, :], AX, ALU.add))
            me(dve, v.reciprocal(asum[:, :], asum[:, :]))
            for d in range(2):
                rows = slice(64 * d, 64 * d + 64)
                m = v.tensor_tensor(attn[rows, :, 64 * d:64 * d + 64], score[rows, :, :],
                                    asum[rows, :].rearrange("p (a b) -> p a b", b=1).to_broadcast([64, NP, HD]), ALU.mult)
            m.then_inc(mid, 1)
            dve.wait_ge(mid_pe, 7)
            v.tensor_copy(attn_t[:, :, :].rearrange("p a g -> p (a g)"), k.ps[0][:, :]).then_inc(mid, 1)
            dve.wait_ge(mid_pe, 8)
            v.tensor_copy(mixed[:, :, :].rearrange("p a g -> p (a g)"), k.ps[1][:, :]).then_inc(mid, 1)
            dve.wait_ge(mid_pe, 9)
            for a in range(2):
                v.tensor_copy(v2[:, 2 * a:2 * a + 2, :].rearrange("p a c -> p (a c)"), k.ps[2 + a][:, :]).then_inc(mid, 1)
            dve.wait_ge(bout_in, 16)
            me(dve, v.tensor_tensor(k.res[:, :, :], k.res[:, :, :], b_out[:, :].rearrange("p (a c) -> p a c", a=1).to_broadcast([P, NT, C]), ALU.add))
            for t in range(NT):
                dve.wait_ge(result, t + 1)
                v.tensor_tensor(k.res[:, t, :], k.res[:, t, :], k.ps[t % 8][0:P, 0:C], ALU.add).then_inc(joined, 1)


def build(nc, out, **arrays):
    ctx = ExitStack()
    with ctx:
        k = Kernel(nc, ctx, out, arrays)
        setup(k)
        k.open_layer()
        with ExitStack() as gat:
            k.xh = k.sb("xh", [P, NT, RW], F32, gat)
            index_phase(k)
            project_phase(k)
            k.adst_e = k.sb("adst_e", [EP, ET, H], F32, gat)
            spread_phase(k)
            edge_phase(k, "gat", k.xh_tab, XW, True)
            chain_phase(k, "gat", True)
            gat_node_phase(k)
        k.close_layer()
        k.open_layer()
        router_phase(k)
        with ExitStack() as moe:
            k.w1t, k.w3t = (k.sb(n, [128, 2, NE, HID], F32, moe) for n in ("w1t", "w3t"))
            k.w2t = k.sb("w2t", [128, 6, NE, C], F32, moe)
            weights_phase(k)
            experts_phase(k)
        combine_phase(k)
        k.close_layer()
        k.open_layer()
        gnn_table_phase(k)
        edge_phase(k, "gnn", k.xn_tab, C, False)
        chain_phase(k, "gnn", False)
        gnn_node_phase(k)
        attention_phase(k)
        k.close_layer()
_INS = ['x','src','dst','L0_gnn_W','L0_gnn_att_src','L0_gnn_att_dst','L0_gnn_bias','L0_gnn_gamma','L0_gnn_beta','L0_ffn_router_w','L0_ffn_w1','L0_ffn_w2','L0_ffn_w3','L1_gnn_W','L1_gnn_b','L1_ffn_W_fx','L1_ffn_b_fx','L1_ffn_W_x','L1_ffn_b_x','L1_ffn_W_slice','L1_ffn_b_slice','L1_ffn_W_q','L1_ffn_W_k','L1_ffn_W_v','L1_ffn_W_out','L1_ffn_b_out','L1_ffn_temperature']


def kernel(**inputs):
    import numpy as _np
    import concourse.bacc as _bacc
    from concourse import mybir as _mybir
    from concourse.bass_utils import run_bass_kernel_spmd as _run

    nc = _bacc.Bacc("TRN2", target_bir_lowering=False, num_devices=1)
    arrays, args = {}, {}
    for name in _INS:
        a = _np.ascontiguousarray(inputs[name])
        arrays[f"in_{name}_dram"] = a
        args[name] = nc.dram_tensor(f"in_{name}_dram", a.shape, _mybir.dt.from_np(a.dtype), kind="ExternalInput").ap()
    out = nc.dram_tensor("out_0_dram", (3125, 256), _mybir.dt.float32, kind="ExternalOutput").ap()
    build(nc, out, **args)
    r = _run(nc, [arrays], core_ids=[0])
    return r.results[0]["out_0_dram"]
```

```python
from contextlib import ExitStack

import numpy as np
import concourse.bass as bass
from concourse import mybir

F32 = mybir.dt.float32
I32 = mybir.dt.int32
U32 = mybir.dt.uint32
ALU = mybir.AluOpType
ACT = mybir.ActivationFunctionType
AX = mybir.AxisListType.X

N, C, E = 3125, 256, 50000
P, NT = 125, 25
TB = 5
H, D = 8, 32
EP = 128
ET = 392
SB = 14
NB = ET // SB
Q, J = 98, 4
XW = C + H
RW = C + 2 * H
NO_ROW = ET * EP
NO_CHAIN = ET
BIG = 3e38
EPS = 1e-5


class Steps:

    def __init__(self, sem):
        self.sem, self.n, self.turn = sem, 0, None

    def __call__(self, eng, ins):
        ins.then_inc(self.sem, 1)
        self.n += 1
        eng.wait_ge(self.sem, self.n if self.turn is None else self.turn * self.k + self.n)

    def loop(self, turn, k):
        self.turn, self.k, self.first = turn, k, self.n

    def end(self, turns):
        assert self.n - self.first == self.k, (self.n - self.first, self.k)
        self.n, self.turn = self.first + self.k * turns, None


class Kernel:

    def __init__(self, nc, ctx, out, arrays):
        self.nc, self.ctx, self.out, self.a = nc, ctx, out, arrays
        self.opened = None
        self.steps = {e: Steps(self.sem(f"{e}_steps")) for e in ("pe", "act", "dve", "pool")}

    def sb(self, name, shape, dt=F32, ctx=None):
        return (ctx or self.ctx).enter_context(self.nc.sbuf_tensor(name, shape, dt))

    def sem(self, name):
        s = self.nc.semaphore(name)
        if self.opened is None:
            return self.ctx.enter_context(s)
        self.opened.append(self.layer.enter_context(s))
        return self.opened[-1]

    def gather_sem(self, name):
        return self.ctx.enter_context(self.nc.semaphore(name))

    def open_layer(self):
        self.opened, self.layer = [], ExitStack()

    def close_layer(self):
        with self.nc.Block() as block:

            @block.gpsimd
            def _(pool):
                for s in self.opened:
                    pool.sem_clear(s)
        self.layer.close()
        self.opened = None

    def dram(self, name, shape, dt=F32):
        return self.nc.dram_tensor(name, shape, dt, kind=SCRATCH).ap()


SCRATCH = "Internal"


def setup(k):
    k.ps = [k.ctx.enter_context(k.nc.psum_tensor(f"bank{i}", [128, 512], F32)) for i in range(8)]
    k.ident = k.sb("ident", [128, 128])
    k.ones = k.sb("ones", [128, 128])
    k.res = k.sb("res", [P, NT, C])
    k.stats = k.sb("stats", [P, NT, 6])
    k.mv = k.sb("mv", [P, NT, 2])
    k.rstd = k.sb("rstd", [P, NT])
    k.node = k.sb("node", [P, NT])
    k.deg = k.sb("deg", [P, NT])
    k.main_row = k.sb("main_row", [P, NT], I32)
    k.chain_row = k.sb("chain_row", [P, NT], I32)
    k.start_row = k.sb("start_row", [P, NT], I32)
    k.src_e = k.sb("src_e", [EP, ET], I32)
    k.dst_e = k.sb("dst_e", [EP, ET])
    k.fwd_e = k.sb("fwd_e", [EP, ET])
    k.bwd_e = k.sb("bwd_e", [EP, ET])
    k.joins = k.sb("joins", [128, ET])
    k.cont_q = k.sb("cont_q", [Q, J * EP])
    k.tile_dst = k.sb("tile_dst", [Q, J], I32)
    k.xh_tab = k.dram("xh_tab", [N, XW])
    k.adst_tab = k.dram("adst_tab", [N, H])
    k.adst_edge = k.dram("adst_edge", [ET * EP, H])
    k.gate = k.sb("gate", [P, 2, NT])
    k.place = k.sb("place", [P, 2, NT], I32)
    k.item_expert = k.sb("item_expert", [1, NI], I32)
    k.slot_token = k.sb("slot_token", [M, NI], I32)
    k.x1_tab, k.xn_tab, k.y_tab = k.dram("x1_tab", [N, C]), k.dram("xn_tab", [N, C]), k.dram("y_tab", [NI * M, C])
    k.dst_pad = k.dram("dst_pad", [ET * EP])
    k.start_tab = k.dram("start_tab", [N + 1])
    k.parts = k.dram("parts", [ET * EP + 1, RW])
    k.chains = k.dram("chains", [ET + 1, RW])


def tile_of(a, t):
    return a[:, bass.ds(t, 1), :].rearrange("p a c -> p (a c)")


def first_phase(k):
    nc, st = k.nc, k.steps
    ctx = ExitStack()
    with ctx:
        sb = lambda n, s, d=F32: k.sb(n, s, d, ctx)
        srcq_i, dstq_i = sb("srcq_i", [Q, J * EP], I32), sb("dstq_i", [Q, J * EP], I32)
        srcq, dstq = sb("srcq", [Q, J * EP]), sb("dstq", [Q, J * EP])
        same = sb("same", [Q, J * EP + 1])
        first_b = sb("first_b", [128, ET])
        last_b = sb("last_b", [128, ET])
        trash = sb("trash", [P, NT, ET])
        before = sb("before", [P, NT])
        tile = sb("tile", [P, NT])
        tile_i = sb("tile_i", [P, NT], I32)
        window = sb("window", [P, NT, EP])
        start, end, last = sb("start", [P, NT]), sb("end", [P, NT]), sb("last", [P, NT])
        last_i, has, t0, t1 = sb("last_i", [P, NT], I32), sb("has", [P, NT]), sb("t0", [P, NT]), sb("t1", [P, NT])
        total = sb("total", [1, 1])
        w = sb("w", [128, 2, RW])
        att = sb("att", [128, 2, C])
        prod = sb("prod", [128, 2, C])
        xn = sb("xn", [P, TB, C])
        xt = sb("xt", [128, TB, 2, P])
        deg0 = sb("deg0", [1, 1])
        w_in, att_in = k.sem("w_in"), k.sem("att_in")
        deviations, roots = k.sem("p_deviations"), k.sem("p_roots")
        w_ready = k.sem("w_ready")
        xn_made, xt_turned, xt_made = k.sem("p_xn_made"), k.sem("p_xt_turned"), k.sem("p_xt_made")
        projected, taken, out_done = k.sem("projected"), k.sem("p_taken"), k.sem("p_out_done")
        padded = k.sem("padded")
        edges_in = k.sem("edges_in")
        x_in = k.sem("x_in")
        mask_kept = k.sem("mask_kept")
        consts = k.sem("consts")
        edges_f = k.sem("edges_f")
        pad_out = k.sem("pad_out")
        turned = k.sem("turned")
        ends_b = k.sem("ends_b")
        tiles_found = k.sem("tiles_found")
        windows_in = k.gather_sem("windows_in")
        starts_found = k.sem("starts_found")
        starts_out = k.sem("starts_out")
        ends_in = k.sem("ends_in")
        full = E // (J * EP)
        rest = E - full * J * EP

        block = ctx.enter_context(nc.Block())

        @block.sync
        def _(sp):
            sp.wait_ge(padded, 2)
            for a, t in ((k.a["dst"], dstq_i), (k.a["src"], srcq_i)):
                sp.dma_start(t[0:full, :], a[0:full * J * EP].rearrange("(q e) -> q e", e=J * EP)).then_inc(edges_in, 16)
                sp.dma_start(t[full:full + 1, 0:rest], a[full * J * EP:E].rearrange("(q e) -> q e", q=1)).then_inc(edges_in, 16)
            sp.wait_ge(edges_f, 1)
            sp.dma_start(k.dst_pad.rearrange("(q e) -> q e", q=Q), dstq[:, :]).then_inc(pad_out, 16)
            sp.wait_ge(starts_found, 1)
            sp.dma_start(k.start_tab[0:N].rearrange("(p t) -> p t", p=P), start[:, :]).then_inc(starts_out, 16)
            sp.dma_start(k.start_tab[N:N + 1].rearrange("(a b) -> a b", a=1), total[:, :]).then_inc(starts_out, 16)
            sp.wait_ge(starts_out, 32)
            sp.dma_start(end[:, :], k.start_tab[1:N + 1].rearrange("(p t) -> p t", p=P)).then_inc(ends_in, 16)
            sp.wait_ge(out_done, 32)

        @block.scalar
        def _(act):
            act.dma_start(w[:, :, 0:C], k.a["L0_gnn_W"].rearrange("(a p) c -> p a c", p=128)).then_inc(w_in, 16)
            for i, name in enumerate(("L0_gnn_att_src", "L0_gnn_att_dst")):
                act.dma_start(att[:, i, :], k.a[name].rearrange("(a h) d -> a (h d)", a=1).to_broadcast([128, C])).then_inc(att_in, 16)
            act.dma_start(k.res[:, :, :], k.a["x"].rearrange("(p t) c -> p t c", p=P)).then_inc(x_in, 16)
            norm_roots(k, act, deviations, roots)
            act.sem_inc(xt_made, TB)
            with act.Fori(0, NT // TB) as i:
                for s in range(TB):
                    act.wait_ge(xt_turned, i * TB + s + 1 + TB)
                    act.wait_ge(projected, i * TB + s + 1)
                    nc.scalar.copy(xt[:, s, :, :].rearrange("p a n -> p (a n)"), k.ps[s % 3][:, 0:2 * P]).then_inc(xt_made, 1)
            act.wait_ge(taken, NT + TB)
            act.dma_start(k.xh_tab.rearrange("(p t) c -> p t c", p=P), k.xh[:, :, 0:XW]).then_inc(out_done, 16)
            act.dma_start(k.adst_tab.rearrange("(p t) c -> p t c", p=P), k.xh[:, :, XW:RW]).then_inc(out_done, 16)

        @block.gpsimd
        def _(pool):
            me = st["pool"]
            nc.gpsimd.memset(srcq_i[:, :], 0).then_inc(padded, 1)
            nc.gpsimd.memset(dstq_i[:, :], N).then_inc(padded, 1)
            nc.gpsimd.memset(k.ones[:, :], 1.0)
            me(pool, nc.gpsimd.memset(k.ident[:, :], 0.0))
            nc.gpsimd.affine_select(out=k.ident[:, :], in_=k.ident[:, :], compare_op=ALU.not_equal, fill=1.0, base=0,
                                    pattern=[[-1, 128]], channel_multiplier=1)
            nc.gpsimd.iota(k.node[:, :], pattern=[[1, NT]], base=0, channel_multiplier=NT,
                           allow_small_or_imprecise_dtypes=True).then_inc(consts, 1)
            pool.wait_ge(tiles_found, 1)
            pool.wait_ge(pad_out, 16)
            for t in range(NT):
                pool.indirect_dma_start(out=window[:, t, :], out_offset=None, in_=k.dst_pad.rearrange("(a b) -> a b", b=EP),
                                        in_offset=bass.IndirectOffsetOnAxis(ap=tile_i[:, t:t + 1], axis=0)).then_inc(windows_in, 16)

        @block.tensor
        def _(pe):
            pe.wait_ge(edges_f, 4)
            pe.wait_ge(consts, 1)
            for b, t in enumerate((dstq, srcq, same, same)):
                for j in range(J):
                    at = j * EP + (b == 3)
                    last_mm = nc.tensor.transpose(k.ps[b][:, j * Q:(j + 1) * Q], t[:, at:at + EP], k.ident[0:Q, 0:Q])
                last_mm.then_inc(turned, 1)
            pe.wait_ge(ends_b, 1)
            nc.tensor.matmul(k.ps[4][:, 0:ET], k.ident[:, 0:1].to_broadcast([128, 128]), k.dst_e[:, :], start=True, stop=True).then_inc(turned, 1)
            nc.tensor.matmul(k.ps[5][:, 0:ET], k.ident[:, EP - 1:EP].to_broadcast([128, 128]), k.dst_e[:, :], start=True, stop=True).then_inc(turned, 1)
            pe.sem_inc(xt_turned, TB)
            pe.sem_inc(projected, TB)
            pe.wait_ge(w_ready, 1)
            pe.wait_ge(mask_kept, 6)
            with pe.Fori(0, NT // TB) as i:
                for s in range(TB):
                    pe.wait_ge(xn_made, i * TB + s + 1)
                    pe.wait_ge(xt_made, i * TB + TB if s < 3 else i * TB + s - 2 + TB)
                    for c in range(2):
                        last_mm = nc.tensor.transpose(k.ps[s % 3][:, c * P:(c + 1) * P],
                                                      xn[:, s, c * 128:(c + 1) * 128], k.ident[0:P, 0:P])
                    last_mm.then_inc(xt_turned, 1)
                for s in range(TB):
                    pe.wait_ge(xt_made, i * TB + s + 1 + TB)
                    pe.wait_ge(taken, i * TB + s + 1)
                    for c in range(2):
                        last_mm = nc.tensor.matmul(k.ps[3 + s][0:P, 0:RW], xt[:, s, c, :], w[:, c, :], start=(c == 0), stop=(c == 1))
                    last_mm.then_inc(projected, 1)

        @block.vector
        def _(dve):
            me = st["dve"]
            v = nc.vector
            dve.wait_ge(edges_in, 64)
            v.tensor_copy(dstq[:, :], dstq_i[:, :]).then_inc(edges_f, 1)
            dve.wait_ge(edges_f, 1)
            v.tensor_copy(srcq[:, :], srcq_i[:, :]).then_inc(edges_f, 1)
            me(dve, v.tensor_tensor(same[:, 1:J * EP], dstq[:, 1:J * EP], dstq[:, 0:J * EP - 1], ALU.is_equal))
            me(dve, v.memset(same[:, 0:J * EP + 1:EP], 0.0))
            v.tensor_copy(k.cont_q[:, :], same[:, 0:J * EP])
            me(dve, v.tensor_scalar(k.tile_dst[:, :], dstq[:, 0:J * EP:EP], float(N - 1), None, ALU.min))
            v.tensor_scalar(same[:, :], same[:, :], -1.0, BIG, ALU.add, ALU.mult).then_inc(edges_f, 2)
            for b, t in enumerate((k.dst_e, k.src_e, k.fwd_e, k.bwd_e)):
                dve.wait_ge(turned, b + 1)
                me(dve, v.tensor_copy(t[:, :].rearrange("p (q j) -> p j q", j=J),
                                      k.ps[b][:, 0:ET].rearrange("p (j q) -> p j q", j=J)))
                if b == 0:
                    dve.sem_inc(ends_b, 1)
            dve.wait_ge(turned, 6)
            v.tensor_copy(first_b[:, :], k.ps[4][:, 0:ET])
            me(dve, v.tensor_copy(last_b[:, :], k.ps[5][:, 0:ET]))
            dve.sem_inc(mask_kept, 6)
            me(dve, v.memset(k.joins[:, 0:1], 0.0))
            me(dve, v.tensor_tensor(k.joins[:, 1:ET], last_b[:, 1:ET], last_b[:, 0:ET - 1], ALU.is_equal))
            dve.wait_ge(consts, 1)
            with dve.Fori(0, NT) as t:
                v.tensor_scalar(tile_of(trash, t), first_b[0:P, :], k.node[:, bass.ds(t, 1)], None, ALU.is_lt, ALU.add,
                                accum_out=before[:, bass.ds(t, 1)])
            me(dve, v.memset(total[:, :], float(E)))
            me(dve, v.tensor_scalar(tile[:, :], before[:, :], -1.0, 0.0, ALU.add, ALU.max))
            v.tensor_copy(tile_i[:, :], tile[:, :]).then_inc(tiles_found, 1)
            dve.sem_inc(taken, TB)
            dve.wait_ge(w_in, 16)
            dve.wait_ge(att_in, 32)
            for i in range(2):
                me(dve, v.tensor_tensor(prod[:, :, :], w[:, :, 0:C], att[:, i:i + 1, :].to_broadcast([128, 2, C]), ALU.mult))
                me(dve, v.tensor_reduce(w[:, :, C + H * i:C + H * (i + 1)], prod[:, :, :].rearrange("p a (h d) -> p a h d", h=H), AX, ALU.add))
            dve.sem_inc(w_ready, 1)
            dve.wait_ge(x_in, 16)
            norm_stats(k, dve, k.res, None, deviations, roots)

            def norm_body(i):
                for s in range(TB):
                    t = i * TB + s
                    dve.wait_ge(xt_turned, i * TB + s + 1)
                    me(dve, v.tensor_scalar(xn[:, s, :], tile_of(k.res, t), k.mv[:, bass.ds(t, 1), 0:1].rearrange("p a c -> p (a c)"),
                                            k.rstd[:, bass.ds(t, 1)], ALU.subtract, ALU.mult))
                    v.tensor_tensor(tile_of(k.res, t), tile_of(k.res, t), xn[:, s, :], ALU.add).then_inc(xn_made, 1)

            def take_body(i):
                for s in range(TB):
                    dve.wait_ge(projected, i * TB + s + 1 + TB)
                    v.tensor_scalar(tile_of(k.xh, i * TB + s), k.ps[3 + s][0:P, 0:RW], 1.0, None, ALU.mult).then_inc(taken, 1)

            norm_body(0)
            with dve.Fori(0, NT // TB - 1) as i:
                me.loop(i, TB)
                norm_body(i + 1)
                take_body(i)
                me.end(NT // TB - 1)
            take_body(NT // TB - 1)
            dve.wait_ge(windows_in, 16 * NT)
            with dve.Fori(0, NT) as t:
                v.tensor_scalar(tile_of(trash, t)[:, 0:EP], tile_of(window, t), k.node[:, bass.ds(t, 1)], None,
                                ALU.is_lt, ALU.add, accum_out=before[:, bass.ds(t, 1)])
            me(dve, v.memset(deg0[:, :], 0.0))
            v.scalar_tensor_tensor(out=start[:, :], in0=tile[:, :], scalar=float(EP), in1=before[:, :], op0=ALU.mult,
                                   op1=ALU.add).then_inc(starts_found, 1)
            dve.wait_ge(starts_found, 1)
            dve.wait_ge(ends_in, 16)
            me(dve, v.tensor_tensor(k.deg[:, :], end[:, :], start[:, :], ALU.subtract))
            v.tensor_scalar(has[:, :], k.deg[:, :], 0.0, None, ALU.is_gt)
            me(dve, v.tensor_scalar(last[:, :], end[:, :], -1.0, 0.0, ALU.add, ALU.max))
            me(dve, v.tensor_copy(last_i[:, :], last[:, :]))
            me(dve, v.tensor_single_scalar(tile_i[:, :], last_i[:, :], 7, ALU.logical_shift_right))
            me(dve, v.tensor_copy(tile[:, :], tile_i[:, :]))
            v.tensor_scalar(t0[:, :], last[:, :], -float(NO_ROW), None, ALU.add)
            me(dve, v.scalar_tensor_tensor(out=t1[:, :], in0=tile[:, :], scalar=float(EP), in1=start[:, :],
                                           op0=ALU.mult, op1=ALU.is_gt))
            v.tensor_tensor(t0[:, :], t0[:, :], has[:, :], ALU.mult)
            me(dve, v.tensor_tensor(t1[:, :], t1[:, :], has[:, :], ALU.mult))
            v.tensor_scalar(k.main_row[:, :], t0[:, :], float(NO_ROW), None, ALU.add)
            me(dve, v.tensor_scalar(tile[:, :], tile[:, :], -1.0 - NO_CHAIN, None, ALU.add))
            me(dve, v.tensor_tensor(t1[:, :], t1[:, :], tile[:, :], ALU.mult))
            v.tensor_scalar(k.chain_row[:, :], t1[:, :], float(NO_CHAIN), None, ALU.add)
            me(dve, v.tensor_scalar(t0[:, :], start[:, :], -float(NO_ROW + 1), None, ALU.add))
            me(dve, v.tensor_tensor(t0[:, :], t0[:, :], has[:, :], ALU.mult))
            me(dve, v.tensor_scalar(k.start_row[:, :], t0[:, :], float(NO_ROW + 1), None, ALU.add))


def norm_stats(k, dve, src, ready, deviations, roots):
    v, me = k.nc.vector, k.steps["dve"]
    with dve.Fori(0, NT) as t:
        v.bn_stats(k.stats[:, bass.ds(t, 1), :].rearrange("p a s -> p (a s)"),
                   src[:, bass.ds(t, 1), :].rearrange("p a c -> p (a c)"))
    norm_factors(k, dve, deviations, roots)


def norm_factors(k, dve, deviations, roots):
    v, me = k.nc.vector, k.steps["dve"]
    me(dve, v.memset(k.rstd[:, :], 0.0))
    even, odd, mean, var = k.stats[:, :, 1], k.stats[:, :, 4], k.mv[:, :, 0], k.mv[:, :, 1]
    v.tensor_tensor(mean, even, odd, ALU.add)
    v.tensor_tensor(var, even, odd, ALU.subtract)
    me(dve, v.tensor_tensor(k.rstd[:, :], k.stats[:, :, 2], k.stats[:, :, 5], ALU.add))
    v.tensor_scalar(mean, mean, 0.5, None, ALU.mult)
    v.tensor_scalar(k.rstd[:, :], k.rstd[:, :], 1.0 / C, EPS, ALU.mult, ALU.add)
    me(dve, v.tensor_tensor(var, var, var, ALU.mult))
    v.scalar_tensor_tensor(out=k.rstd[:, :], in0=var, scalar=0.25, in1=k.rstd[:, :], op0=ALU.mult, op1=ALU.add).then_inc(deviations, 1)
    dve.wait_ge(roots, 1)
    me(dve, v.reciprocal(k.rstd[:, :], k.rstd[:, :]))


def norm_roots(k, act, deviations, roots):
    act.wait_ge(deviations, 1)
    k.nc.scalar.activation(k.rstd[:, :], k.rstd[:, :], ACT.Sqrt).then_inc(roots, 1)


def spread_phase(k):
    nc, st = k.nc, k.steps
    ctx = ExitStack()
    with ctx:
        sb = lambda n, s, d=F32: k.sb(n, s, d, ctx)
        sparse = sb("sparse", [Q, J * EP * H])
        filled = sb("filled", [Q, J * EP * H])
        firsts = sb("firsts", [Q, J, H])
        zeroed, cleared, firsts_in = k.sem("zeroed"), k.sem("cleared"), k.gather_sem("firsts_in")
        firsts_out, starts_out, sparse_in = k.sem("firsts_out"), k.gather_sem("node_starts_out"), k.sem("sparse_in")
        spread, turned, taken = k.sem("spread"), k.sem("s_turned"), k.sem("s_taken")
        block = ctx.enter_context(nc.Block())
        edge_rows = k.adst_edge.rearrange("(q m) h -> q (m h)", q=Q)

        @block.sync
        def _(sp):
            sp.wait_ge(zeroed, 1)
            sp.dma_start(edge_rows, sparse[:, :]).then_inc(cleared, 16)
            sp.wait_ge(cleared, 16)
            sp.wait_ge(firsts_in, 16 * J)
            sp.dma_start(k.adst_edge.rearrange("(q j e) h -> q j e h", q=Q, j=J)[:, :, 0, :], firsts[:, :, :]).then_inc(firsts_out, 16)
            sp.wait_ge(starts_out, 16 * NT)
            sp.dma_start(sparse[:, :], edge_rows).then_inc(sparse_in, 16)

        @block.gpsimd
        def _(pool):
            for j in range(J):
                pool.indirect_dma_start(out=firsts[:, j, :], out_offset=None, in_=k.adst_tab,
                                        in_offset=bass.IndirectOffsetOnAxis(ap=k.tile_dst[:, j:j + 1], axis=0)).then_inc(firsts_in, 16)
            pool.wait_ge(firsts_out, 16)
            for t in range(NT):
                pool.indirect_dma_start(out=k.adst_edge, out_offset=bass.IndirectOffsetOnAxis(ap=k.start_row[:, t:t + 1], axis=0),
                                        in_=k.xh[:, t, XW:RW], in_offset=None, bounds_check=NO_ROW - 1, oob_is_err=False).then_inc(starts_out, 16)

        @block.tensor
        def _(pe):
            pe.wait_ge(spread, H)
            for h in range(H):
                if h >= 4:
                    pe.wait_ge(taken, h - 3)
                for j in range(J):
                    m = nc.tensor.transpose(k.ps[h % 4][:, j * Q:(j + 1) * Q], filled[:, j * EP * H + h:(j + 1) * EP * H:H], k.ident[0:Q, 0:Q])
                m.then_inc(turned, 1)

        @block.scalar
        def _(act):
            for h in range(H):
                act.wait_ge(turned, h + 1)
                nc.scalar.copy(k.adst_e[:, :, h].rearrange("p (q j) -> p j q", j=J), k.ps[h % 4][:, 0:ET].rearrange("p (j q) -> p j q", j=J)).then_inc(taken, 1)

        @block.vector
        def _(dve):
            v = nc.vector
            v.memset(sparse[:, :], 0.0).then_inc(zeroed, 1)
            dve.wait_ge(sparse_in, 16)
            for h in range(H):
                for j in range(J):
                    m = v.tensor_tensor_scan(filled[:, j * EP * H + h:(j + 1) * EP * H:H], k.cont_q[:, j * EP:(j + 1) * EP],
                                             sparse[:, j * EP * H + h:(j + 1) * EP * H:H], 0.0, ALU.mult, ALU.add)
                m.then_inc(spread, 1)


def edge_phase(k, name, table, width, weighted):
    nc, st = k.nc, k.steps
    ctx = ExitStack()
    sums_w = C + H if weighted else C
    out_w = RW if weighted else C
    BK = 7
    R = 4
    with ctx:
        sb = lambda n, s, d=F32: k.sb(f"{name}_{n}", s, d, ctx)
        sem = lambda n: k.sem(f"{name}_{n}")
        ix = [sb(f"ix{s}", [EP, SB], I32) for s in range(R)]
        rows = [sb(f"rows{s}", [EP, SB, width]) for s in range(R)]
        dstb = [sb(f"dstb{s}", [EP, SB * EP]) for s in range(2)]
        same = [sb(f"same{s}", [EP, SB, EP]) for s in range(2)]
        outs = [sb(f"outs{s}", [EP, SB, out_w]) for s in range(2)]
        if weighted:
            logit0, logit, shifted = (sb(n, [EP, SB, H]) for n in ("logit0", "logit", "shifted"))
            mask8 = sb("mask8", [EP, 2, SB, H])
            masks = sb("masks", [SB * H, 2 * EP])
            running, maxima = sb("running", [SB * H, EP]), sb("maxima", [SB * H, EP])
        outs_free = sem("outs_free")
        ix_made, issuing = sem("ix_made"), sem("issuing")
        rows_in = [k.gather_sem(f"{name}_rows_in{s}") for s in range(R)]
        dstb_in = [sem(f"dstb_in{s}") for s in range(2)]
        outs_out = [sem(f"outs_out{s}") for s in range(2)]
        same_made, logits_made, logits_turned, masks_in = sem("same_made"), sem("logits_made"), sem("logits_turned"), sem("masks_in")
        maxima_made, maxima_turned, maxima_in, less_max = sem("maxima_made"), sem("maxima_turned"), sem("maxima_in"), sem("less_max")
        weights_made, messages, sums, taken = sem("weights_made"), sem("messages"), sem("sums"), sem("taken")
        block = ctx.enter_context(nc.Block())

        @block.sync
        def _(sp):
            out_rows = k.parts[0:ET * EP, 0:out_w].rearrange("(b t e) c -> e b t c", t=SB, e=EP)
            dst_rows = k.dst_pad.rearrange("(b e) -> b e", b=NB)
            sp.sem_inc(outs_free, 2)

            def load(b, s, guarded=True):
                if guarded:
                    sp.wait_ge(same_made, b)
                sp.dma_start(dstb[s][:, :], dst_rows[bass.ds(b, 1), :].to_broadcast([EP, SB * EP])).then_inc(dstb_in[s], 16)

            def store(b, s, turn):
                sp.wait_ge(taken, b * SB + SB + BK)
                if weighted:
                    sp.wait_ge(maxima_in, b + 1)
                sp.dma_start(out_rows[:, bass.ds(b, 1), :, :].rearrange("e b t c -> e (b t) c"), outs[s][:, :, :]).then_inc(outs_out[s], 16)
                sp.wait_ge(outs_out[s], 16 * turn + 16)
                sp.sem_inc(outs_free, 1)

            load(0, 0, guarded=False)
            with sp.Fori(0, NB // 2 - 1) as i:
                load(i * 2 + 1, 1)
                store(i * 2, 0, i)
                load(i * 2 + 2, 0)
                store(i * 2 + 1, 1, i)
            load(NB - 1, 1)
            store(NB - 2, 0, NB // 2 - 1)
            store(NB - 1, 1, NB // 2 - 1)

        @block.gpsimd
        def _(pool):
            with pool.Fori(0, NB // R) as i:
                for s in range(R):
                    b = i * R + s
                    pool.wait_ge(sums, b * SB + SB)
                    nc.gpsimd.tensor_copy(ix[s][:, :], k.src_e[:, bass.ds(b * SB, SB)]).then_inc(ix_made, 1)
                    pool.wait_ge(ix_made, b + 1)
                    pool.sem_inc(issuing, 1)
                    for t in range(SB):
                        pool.indirect_dma_start(out=rows[s][:, t, :], out_offset=None, in_=table,
                                                in_offset=bass.IndirectOffsetOnAxis(ap=ix[s][:, t:t + 1], axis=0)).then_inc(rows_in[s], 16)

        @block.vector
        def _(dve):
            v, me = nc.vector, st["dve"]
            dve.sem_inc(same_made, 1)
            with dve.Fori(0, NB // R) as i:
                if weighted:
                    me.loop(i, 2 * R)
                for s in range(R):
                    b = i * R + s
                    dve.wait_ge(dstb_in[s % 2], 16 * (R // 2) * i + 16 * (s // 2) + 16)
                    dve.wait_ge(sums, b * SB + SB * (R - 1))
                    v.tensor_tensor(same[s % 2][:, :, :], dstb[s % 2][:, :].rearrange("p (t e) -> p t e", t=SB),
                                    k.dst_e[:, bass.ds(b * SB, SB)].rearrange("p (t a) -> p t a", a=1).to_broadcast([EP, SB, EP]),
                                    ALU.is_equal).then_inc(same_made, 1)
                    if not weighted:
                        continue
                    for m, mask in enumerate((k.fwd_e, k.bwd_e)):
                        v.tensor_scalar(mask8[:, m, :, :], mask[:, bass.ds(b * SB, SB)].rearrange("p (t a) -> p t a", a=1).to_broadcast([EP, SB, H]),
                                        1.0, None, ALU.mult)
                    dve.wait_ge(rows_in[s], 16 * SB * i + 16 * SB)
                    me(dve, v.tensor_tensor(logit0[:, :, :], rows[s][:, :, C:C + H], k.adst_e[:, bass.ds(b * SB, SB), :], ALU.add))
                    v.scalar_tensor_tensor(out=logit[:, :, :], in0=logit0[:, :, :], scalar=0.2, in1=logit0[:, :, :], op0=ALU.mult, op1=ALU.max).then_inc(logits_made, 1)
                    dve.wait_ge(masks_in, b + 1)
                    me(dve, v.tensor_tensor_scan(running[:, :], masks[:, 0:EP], k.ps[0][0:SB * H, 0:EP], -BIG, ALU.add, ALU.max))
                    v.tensor_tensor_scan(maxima[:, ::-1], masks[:, EP:2 * EP][:, ::-1], running[:, ::-1], -BIG, ALU.add, ALU.max).then_inc(maxima_made, 1)
                    dve.wait_ge(maxima_in, b + 1)
                    v.tensor_tensor(shifted[:, :, :], logit[:, :, :], outs[s % 2][:, :, C + H:RW], ALU.subtract).then_inc(less_max, 1)
                    dve.wait_ge(weights_made, b + 2)
                    for half in range(2):
                        t0, t1 = half * SB // 2, (half + 1) * SB // 2
                        f = rows[s][:, t0:t1, 0:C].rearrange("p t (h d) -> p t h d", h=H)
                        v.tensor_tensor(f, f, rows[s][:, t0:t1, C:C + H].rearrange("p t (h a) -> p t h a", a=1).to_broadcast([EP, SB // 2, H, D]),
                                        ALU.mult).then_inc(messages, 1)
                if weighted:
                    me.end(NB // R)

        @block.tensor
        def _(pe):
            pe.sem_inc(sums, R * SB)
            with pe.Fori(0, NB // R) as i:
                for s in range(R):
                    b = i * R + s
                    if weighted:
                        pe.wait_ge(logits_made, b + 1)
                        pe.wait_ge(weights_made, b + 1)
                        nc.tensor.transpose(k.ps[0][0:SB * H, 0:EP], logit[:, :, :].rearrange("p t h -> p (t h)"), k.ident[:, :])
                        for m in range(2):
                            mm = nc.tensor.transpose(k.ps[0][0:SB * H, EP * (m + 1):EP * (m + 2)], mask8[:, m, :, :].rearrange("p t h -> p (t h)"), k.ident[:, :])
                        mm.then_inc(logits_turned, 1)
                        pe.wait_ge(maxima_made, b + 1)
                        nc.tensor.transpose(k.ps[0][:, 384:384 + SB * H], maxima[:, :], k.ident[0:SB * H, 0:SB * H]).then_inc(maxima_turned, 1)
                    pe.wait_ge(same_made, b + 2)
                    if not weighted:
                        pe.wait_ge(rows_in[s], 16 * SB * i + 16 * SB)
                    for t in range(SB):
                        if weighted and t % (SB // 2) == 0:
                            pe.wait_ge(messages, 2 * b + 1 + 2 * t // SB)
                        pe.wait_ge(taken, b * SB + t + 1)
                        nc.tensor.matmul(k.ps[1 + t % BK][:, 0:sums_w], same[s % 2][:, t, :], rows[s][:, t, 0:sums_w],
                                         start=True, stop=True).then_inc(sums, 1)

        @block.scalar
        def _(act):
            act.sem_inc(taken, BK)
            act.sem_inc(weights_made, 1)
            with act.Fori(0, NB // R) as i:
                for s in range(R):
                    b = i * R + s
                    act.wait_ge(outs_free, b + 1)
                    if weighted:
                        act.wait_ge(logits_turned, b + 1)
                        nc.scalar.copy(masks[:, :], k.ps[0][0:SB * H, EP:3 * EP]).then_inc(masks_in, 1)
                        act.wait_ge(maxima_turned, b + 1)
                        nc.scalar.copy(outs[s % 2][:, :, C + H:RW], k.ps[0][:, 384:384 + SB * H].rearrange("p (t h) -> p t h", h=H)).then_inc(maxima_in, 1)
                        act.wait_ge(less_max, b + 1)
                        nc.scalar.activation(rows[s][:, :, C:C + H], shifted[:, :, :], ACT.Exp).then_inc(weights_made, 1)
                    for t in range(SB):
                        act.wait_ge(sums, b * SB + t + 1 + R * SB)
                        nc.scalar.copy(outs[s % 2][:, t, 0:sums_w], k.ps[1 + t % BK][:, 0:sums_w]).then_inc(taken, 1)


def gather_rows(pool, into, table, row, rows_in):
    for t in range(NT):
        pool.indirect_dma_start(out=into[:, t, :], out_offset=None, in_=table,
                                in_offset=bass.IndirectOffsetOnAxis(ap=row[:, t:t + 1], axis=0)).then_inc(rows_in, 16)


def chain_phase(k, name, weighted):
    nc, st = k.nc, k.steps
    ctx = ExitStack()
    w = RW if weighted else C
    with ctx:
        sb = lambda n, s, d=F32: k.sb(f"{name}c_{n}", s, d, ctx)
        sem = lambda n: k.sem(f"{name}c_{n}")
        lasts, carried = sb("lasts", [Q, J, w]), sb("carried", [Q, J, w])
        last_t = [sb(f"last_t{c}", [128, ET]) for c in range(2)]
        sum_t = [sb(f"sum_t{c}", [128, ET]) for c in range(2)]
        dummy = sb("dummy", [1, RW])
        if weighted:
            den_t, max_t, den_c, max_c, neg, keep, scale = (sb(n, [H, ET]) for n in ("den_t", "max_t", "den_c", "max_c", "neg", "keep", "scale"))
            sel = sb("sel", [H, C])
        lasts_in, dummies, sel_made, turned = sem("lasts_in"), sem("dummies"), sem("sel_made"), sem("turned")
        dummies_out = sem("dummies_out")
        drops, factors, spread, scanned, back, rows_made, stored = (sem(n) for n in ("drops", "factors", "spread", "scanned", "back", "rows_made", "stored"))
        block = ctx.enter_context(nc.Block())

        @block.sync
        def _(sp):
            if weighted:
                sp.wait_ge(dummies, 1)
                sp.dma_start(k.parts[NO_ROW:NO_ROW + 1, :], dummy[:, :]).then_inc(dummies_out, 16)
                sp.dma_start(k.chains[NO_CHAIN:NO_CHAIN + 1, :], dummy[:, :]).then_inc(dummies_out, 16)
            sp.dma_start(lasts[:, :, :], k.parts[0:ET * EP, :].rearrange("(q j e) c -> q j e c", q=Q, j=J)[:, :, EP - 1, 0:w]).then_inc(lasts_in, 16)
            if weighted:
                sp.dma_start(k.xh[:, :, 0:XW], k.xh_tab.rearrange("(p t) c -> p t c", p=P)).then_inc(stored, 16)
                sp.dma_start(k.xh[:, :, XW:RW], k.adst_tab.rearrange("(p t) c -> p t c", p=P)).then_inc(stored, 16)
            sp.wait_ge(rows_made, 1)
            sp.dma_start(k.chains[0:ET, 0:w].rearrange("(q j) c -> q j c", j=J), carried[:, :, :]).then_inc(stored, 16)
            sp.wait_ge(stored, 48 if weighted else 16)

        @block.gpsimd
        def _(pool):
            if weighted:
                me = st["pool"]
                nc.gpsimd.memset(dummy[:, 0:C + H], 0.0)
                me(pool, nc.gpsimd.memset(dummy[:, C + H:RW], -BIG))
                pool.sem_inc(dummies, 1)
                me(pool, nc.gpsimd.memset(sel[:, :], 1.0))
                me(pool, nc.gpsimd.affine_select(out=sel[:, :], in_=sel[:, :], compare_op=ALU.is_ge, fill=0.0, base=0,
                                                 pattern=[[1, C]], channel_multiplier=-D))
                nc.gpsimd.affine_select(out=sel[:, :], in_=sel[:, :], compare_op=ALU.is_ge, fill=0.0, base=D - 1,
                                        pattern=[[-1, C]], channel_multiplier=D).then_inc(sel_made, 1)
                pool.wait_ge(dummies_out, 32)
            gather_rows(pool, k.mains, k.parts[:, :], k.main_row, k.mains_in)

        @block.tensor
        def _(pe):
            pe.wait_ge(lasts_in, 16)
            for c in range(2):
                for j in range(J):
                    m = nc.tensor.transpose(k.ps[c][:, j * Q:(j + 1) * Q], lasts[:, j, c * 128:(c + 1) * 128], k.ident[0:Q, 0:Q])
                m.then_inc(turned, 1)
            if weighted:
                for c in range(2):
                    for j in range(J):
                        m = nc.tensor.transpose(k.ps[2 + c][0:H, j * Q:(j + 1) * Q], lasts[:, j, C + c * H:C + (c + 1) * H], k.ident[0:Q, 0:Q])
                    m.then_inc(turned, 1)
                pe.wait_ge(sel_made, 1)
                pe.wait_ge(factors, 3)
                for c in range(2):
                    nc.tensor.matmul(k.ps[4 + c][:, 0:ET], sel[:, c * 128:(c + 1) * 128], keep[:, :], start=True, stop=True)
                    nc.tensor.matmul(k.ps[6 + c][:, 0:ET], sel[:, c * 128:(c + 1) * 128], scale[:, :], start=True, stop=True).then_inc(spread, 1)
            pe.wait_ge(scanned, 3 if weighted else 2)
            for c in range(2):
                for j in range(J):
                    m = nc.tensor.transpose(k.ps[c][0:Q, j * 128:(j + 1) * 128], sum_t[c][:, j:ET:J], k.ident[:, :])
                m.then_inc(back, 1)
            if weighted:
                for c, t in enumerate((den_c, max_c)):
                    for j in range(J):
                        m = nc.tensor.transpose(k.ps[2 + c][0:Q, j * H:(j + 1) * H], t[:, j:ET:J], k.ident[0:H, 0:H])
                    m.then_inc(back, 1)

        @block.scalar
        def _(act):
            if weighted:
                act.wait_ge(drops, 1)
                nc.scalar.activation(keep[:, :], keep[:, :], ACT.Exp).then_inc(factors, 1)
                nc.scalar.activation(scale[:, :], scale[:, :], ACT.Exp).then_inc(factors, 1)

        @block.vector
        def _(dve):
            v, me = nc.vector, st["dve"]

            def lay(dst, bank, parts):
                me(dve, v.tensor_copy(dst[:, :].rearrange("p (q j) -> p j q", j=J), k.ps[bank][0:parts, 0:ET].rearrange("p (j q) -> p j q", j=J)))

            for c in range(2):
                dve.wait_ge(turned, c + 1)
                lay(last_t[c], c, 128)
            if weighted:
                dve.wait_ge(turned, 4)
                lay(den_t, 2, H)
                lay(max_t, 3, H)
                me(dve, v.tensor_scalar(neg[:, :], k.joins[0:H, :], -1.0, BIG, ALU.add, ALU.mult))
                me(dve, v.tensor_tensor_scan(max_c[:, :], neg[:, :], max_t[:, :], -BIG, ALU.add, ALU.max))
                v.memset(keep[:, 0:1], 0.0)
                me(dve, v.tensor_tensor(keep[:, 1:ET], max_c[:, 0:ET - 1], max_c[:, 1:ET], ALU.subtract))
                me(dve, v.tensor_tensor(keep[:, :], keep[:, :], k.joins[0:H, :], ALU.mult))
                v.tensor_tensor(scale[:, :], max_t[:, :], max_c[:, :], ALU.subtract).then_inc(drops, 1)
                dve.wait_ge(factors, 2)
                v.tensor_tensor(keep[:, :], keep[:, :], k.joins[0:H, :], ALU.mult).then_inc(factors, 1)
                me(dve, v.tensor_tensor(den_t[:, :], den_t[:, :], scale[:, :], ALU.mult))
                v.tensor_tensor_scan(den_c[:, :], keep[:, :], den_t[:, :], 0.0, ALU.mult, ALU.add).then_inc(scanned, 1)
                for c in range(2):
                    dve.wait_ge(spread, c + 1)
                    me(dve, v.tensor_tensor(last_t[c][:, :], last_t[c][:, :], k.ps[6 + c][:, 0:ET], ALU.mult))
                    v.tensor_tensor_scan(sum_t[c][:, :], k.ps[4 + c][:, 0:ET], last_t[c][:, :], 0.0, ALU.mult, ALU.add).then_inc(scanned, 1)
            else:
                for c in range(2):
                    v.tensor_tensor_scan(sum_t[c][:, :], k.joins[:, :], last_t[c][:, :], 0.0, ALU.mult, ALU.add).then_inc(scanned, 1)
            for c in range(2):
                dve.wait_ge(back, c + 1)
                me(dve, v.tensor_copy(carried[:, :, c * 128:(c + 1) * 128], k.ps[c][0:Q, :].rearrange("p (j c) -> p j c", j=J)))
            if weighted:
                for c in range(2):
                    dve.wait_ge(back, c + 3)
                    me(dve, v.tensor_copy(carried[:, :, C + c * H:C + (c + 1) * H], k.ps[2 + c][0:Q, 0:J * H].rearrange("p (j h) -> p j h", j=J)))
            dve.sem_inc(rows_made, 1)


def gat_node_phase(k):
    nc, st = k.nc, k.steps
    ctx = ExitStack()
    BODIES = NT // TB
    with ctx:
        sb = lambda n, s, d=F32: k.sb(f"gn_{n}", s, d, ctx)
        sem = lambda n: k.sem(f"gn_{n}")
        main = k.mains
        chain = sb("chain", [P, NT, RW])
        own0, own = sb("own0", [P, NT, H]), sb("own", [P, NT, H])
        top, tmp = sb("top", [P, NT, H]), sb("tmp", [P, NT, H])
        den = sb("den", [P, NT, H])
        wt = sb("wt", [P, 3, NT, H])
        rowv = sb("rowv", [P, 3, C])
        mean, var = sb("mean", [P, C]), sb("var", [P, C])
        chains_in = k.gather_sem("gn_chains_in")
        vecs_in, gaps, weights, weights_made, own_made, joined, summed, centred, squared, dev, root = (
            sem(n) for n in ("vecs_in", "gaps", "weights", "weights_made", "own_made", "joined", "summed", "centred", "squared", "dev", "root"))
        block = ctx.enter_context(nc.Block())
        sq = chain

        @block.sync
        def _(sp):
            for i, name in enumerate(("L0_gnn_bias", "L0_gnn_gamma", "L0_gnn_beta")):
                sp.dma_start(rowv[:, i, :], k.a[name].rearrange("(a c) -> a c", a=1).to_broadcast([P, C])).then_inc(vecs_in, 16)

        @block.gpsimd
        def _(pool):
            gather_rows(pool, chain, k.chains[:, :], k.chain_row, chains_in)
            pool.wait_ge(vecs_in, 48)
            pool.wait_ge(weights_made, 1)
            for i in range(BODIES):
                tiles = slice(i * TB, (i + 1) * TB)
                node = k.xh[:, tiles, 0:C]
                heads = node.rearrange("p t (h d) -> p t h d", h=H)
                st["pool"](pool, nc.gpsimd.tensor_tensor(heads, heads, wt[:, 2, tiles, :].rearrange("p t (h a) -> p t h a", a=1).to_broadcast([P, TB, H, D]), ALU.mult))
                nc.gpsimd.tensor_tensor(node, node, rowv[:, 0:1, :].to_broadcast([P, TB, C]), ALU.add).then_inc(own_made, 1)

        @block.scalar
        def _(act):
            act.wait_ge(gaps, 1)
            nc.scalar.activation(wt[:, :, :, :], wt[:, :, :, :], ACT.Exp).then_inc(weights, 1)
            for i in range(BODIES):
                act.wait_ge(centred, i + 1)
                nc.scalar.activation(sq[:, i * TB:(i + 1) * TB, 0:C], k.xh[:, i * TB:(i + 1) * TB, 0:C], ACT.Square).then_inc(squared, 1)
            act.wait_ge(dev, 1)
            nc.scalar.activation(var[:, :], var[:, :], ACT.Sqrt).then_inc(root, 1)

        @block.tensor
        def _(pe):
            for bank, made, tile in ((k.ps[0], joined, k.xh), (k.ps[1], squared, sq)):
                for t in range(NT):
                    if t % TB == 0:
                        pe.wait_ge(made, t // TB + 1)
                    m = nc.tensor.matmul(bank[0:P, 0:C], k.ones[0:P, 0:P], tile[:, t, 0:C], start=(t == 0), stop=(t == NT - 1))
                m.then_inc(summed, 1)

        @block.vector
        def _(dve):
            v, me = nc.vector, st["dve"]
            me(dve, v.tensor_tensor(own0[:, :, :], k.xh[:, :, C:C + H], k.xh[:, :, C + H:RW], ALU.add))
            me(dve, v.scalar_tensor_tensor(out=own[:, :, :], in0=own0[:, :, :], scalar=0.2, in1=own0[:, :, :], op0=ALU.mult, op1=ALU.max))
            m1, m2 = main[:, :, C + H:RW], chain[:, :, C + H:RW]
            dve.wait_ge(k.mains_in, 16 * NT)
            me(dve, v.tensor_tensor(tmp[:, :, :], m1, own[:, :, :], ALU.max))
            dve.wait_ge(chains_in, 16 * NT)
            me(dve, v.tensor_tensor(top[:, :, :], tmp[:, :, :], m2, ALU.max))
            v.tensor_tensor(wt[:, 0, :, :], m1, top[:, :, :], ALU.subtract)
            v.tensor_tensor(wt[:, 1, :, :], m2, top[:, :, :], ALU.subtract)
            v.tensor_tensor(wt[:, 2, :, :], own[:, :, :], top[:, :, :], ALU.subtract).then_inc(gaps, 1)
            dve.wait_ge(weights, 1)
            v.tensor_tensor(den[:, :, :], wt[:, 0, :, :], main[:, :, C:C + H], ALU.mult)
            me(dve, v.tensor_tensor(tmp[:, :, :], wt[:, 1, :, :], chain[:, :, C:C + H], ALU.mult))
            me(dve, v.tensor_tensor(den[:, :, :], den[:, :, :], tmp[:, :, :], ALU.add))
            me(dve, v.tensor_tensor(den[:, :, :], den[:, :, :], wt[:, 2, :, :], ALU.add))
            me(dve, v.reciprocal(den[:, :, :], den[:, :, :]))
            me(dve, v.tensor_tensor(wt[:, :, :, :], wt[:, :, :, :], den[:, :, :].rearrange("p (a t) h -> p a t h", a=1).to_broadcast([P, 3, NT, H]), ALU.mult))
            dve.sem_inc(weights_made, 1)
            with dve.Fori(0, BODIES) as i:
                me.loop(i, 2)
                tiles = bass.ds(i * TB, TB)
                for j, a in enumerate((main[:, tiles, 0:C], chain[:, tiles, 0:C])):
                    a = a.rearrange("p t (h d) -> p t h d", h=H)
                    m = v.tensor_tensor(a, a, wt[:, j, tiles, :].rearrange("p t (h a) -> p t h a", a=1).to_broadcast([P, TB, H, D]), ALU.mult)
                me(dve, m)
                me(dve, v.tensor_tensor(main[:, tiles, 0:C], main[:, tiles, 0:C], chain[:, tiles, 0:C], ALU.add))
                dve.wait_ge(own_made, i + 1)
                v.tensor_tensor(k.xh[:, tiles, 0:C], k.xh[:, tiles, 0:C], main[:, tiles, 0:C], ALU.add).then_inc(joined, 1)
                me.end(BODIES)
            dve.wait_ge(vecs_in, 48)
            me(dve, v.tensor_tensor(k.res[:, :, :], k.res[:, :, :], rowv[:, 2:3, :].to_broadcast([P, NT, C]), ALU.add))
            dve.wait_ge(summed, 1)
            me(dve, v.tensor_scalar(mean[:, :], k.ps[0][0:P, 0:C], 1.0 / N, None, ALU.mult))

            def over(row):
                return row.rearrange("p (a c) -> p a c", a=1).to_broadcast([P, TB, C])

            for i in range(BODIES):
                feat = k.xh[:, i * TB:(i + 1) * TB, 0:C]
                v.tensor_tensor(feat, feat, over(mean[:, :]), ALU.subtract).then_inc(centred, 1)
            dve.wait_ge(summed, 2)
            v.tensor_scalar(var[:, :], k.ps[1][0:P, 0:C], 1.0 / N, EPS, ALU.mult, ALU.add).then_inc(dev, 1)
            dve.wait_ge(root, 1)
            me(dve, v.reciprocal(var[:, :], var[:, :]))
            me(dve, v.tensor_tensor(var[:, :], var[:, :], rowv[:, 1, :], ALU.mult))
            for i in range(BODIES):
                tiles = slice(i * TB, (i + 1) * TB)
                feat = k.xh[:, tiles, 0:C]
                me(dve, v.tensor_tensor(feat, feat, over(var[:, :]), ALU.mult))
                m = v.tensor_tensor(k.res[:, tiles, :], k.res[:, tiles, :], feat, ALU.add)
            me(dve, m)


class Turning:

    def __init__(self, k, name, ctx):
        self.k = k
        self.xn = k.sb(f"{name}_xn", [P, TB, C], F32, ctx)
        self.xt = k.sb(f"{name}_xt", [128, TB, 2, P], F32, ctx)
        self.made, self.turned, self.kept, self.multiplied, self.taken = (
            k.sem(f"{name}_{n}") for n in ("made", "turned", "kept", "multiplied", "taken"))

    def on_tensor(self, pe, multiply):
        pe.sem_inc(self.turned, TB)
        pe.sem_inc(self.multiplied, TB)
        with pe.Fori(0, NT // TB) as i:
            for s in range(TB):
                pe.wait_ge(self.made, i * TB + s + 1)
                pe.wait_ge(self.kept, i * TB + TB if s < 3 else i * TB + s - 2 + TB)
                for c in range(2):
                    m = self.k.nc.tensor.transpose(self.k.ps[s % 3][:, c * P:(c + 1) * P], self.xn[:, s, c * 128:(c + 1) * 128], self.k.ident[0:P, 0:P])
                m.then_inc(self.turned, 1)
            for s in range(TB):
                pe.wait_ge(self.kept, i * TB + s + 1 + TB)
                pe.wait_ge(self.taken, i * TB + s + 1)
                multiply(s).then_inc(self.multiplied, 1)

    def on_scalar(self, act):
        act.sem_inc(self.kept, TB)
        with act.Fori(0, NT // TB) as i:
            for s in range(TB):
                act.wait_ge(self.turned, i * TB + s + 1 + TB)
                act.wait_ge(self.multiplied, i * TB + s + 1)
                self.k.nc.scalar.copy(self.xt[:, s, :, :].rearrange("p a n -> p (a n)"), self.k.ps[s % 3][:, 0:2 * P]).then_inc(self.kept, 1)

    def on_vector(self, dve, fill, take, steps=0, after=None):
        me, bodies = self.k.steps["dve"], NT // TB

        def fill_body(i):
            for s in range(TB):
                dve.wait_ge(self.turned, i * TB + s + 1)
                fill(i * TB + s, s).then_inc(self.made, 1)

        def take_body(i):
            for s in range(TB):
                dve.wait_ge(self.multiplied, i * TB + s + 1 + TB)
                take(i * TB + s, s).then_inc(self.taken, 1)
            if after is not None:
                dve.wait_ge(self.taken, i * TB + 2 * TB)
                for s in range(TB):
                    after(i * TB + s)

        dve.sem_inc(self.taken, TB)
        fill_body(0)
        with dve.Fori(0, bodies - 1) as i:
            me.loop(i, steps)
            fill_body(i + 1)
            take_body(i)
            me.end(bodies - 1)
        take_body(bodies - 1)


def normed(k, out, t):
    return k.nc.vector.tensor_scalar(out, tile_of(k.res, t), k.mv[:, bass.ds(t, 1), 0:1].rearrange("p a c -> p (a c)"),
                                     k.rstd[:, bass.ds(t, 1)], ALU.subtract, ALU.mult)


NE, HID = 8, 682
M = 128
NI = (2 * N + NE * (M - 1)) // M
HH = HID // 2
HB = [(a, b, min(128, HH - 128 * b)) for a in range(2) for b in range(3)]


def router_phase(k):
    nc, st = k.nc, k.steps
    ctx = ExitStack()
    with ctx:
        sb = lambda n, s, d=F32: k.sb(f"r_{n}", s, d, ctx)
        sem = lambda n: k.sem(f"r_{n}")
        q = Turning(k, "r", ctx)
        rw, rwt = sb("rw", [NE, C]), sb("rwt", [128, 2, NE])
        xn1 = sb("xn1", [P, NT, C])
        prob, rest, hit, cand = (sb(n, [P, NT, NE]) for n in ("prob", "rest", "hit", "cand"))
        oh = sb("oh", [P, 2, NT, NE])
        both, tot, inc, slot = (sb(n, [P, NT, NE]) for n in ("both", "tot", "inc", "slot"))
        expert, item, lane = sb("expert", [P, NE]), sb("item", [P, NI]), sb("lane", [P, M])
        peak, idx, den = sb("peak", [P, NT]), sb("idx", [P, NT]), sb("den", [P, NT])
        tiles, tiles_i, ends, begins = sb("tiles", [P, NE]), sb("tiles_i", [P, NE], I32), sb("ends", [P, NE]), sb("begins", [P, NE])
        pos, hi, lo = sb("pos", [P, 2, NT]), sb("hi", [P, 2, NT]), sb("lo", [P, 2, NT])
        hi_i = sb("hi_i", [P, 2, NT], I32)
        before = sb("before", [P, P])
        at_lane, at_item = sb("at_lane", [P, 2 * NT, M]), sb("at_item", [P, 2 * NT, NI])
        over = sb("over", [P, NI, NE])
        of_item = sb("of_item", [P, NI])
        rw_in, rw_turned, rw_ready, deviations, roots = (sem(n) for n in ("rw_in", "rw_turned", "rw_ready", "deviations", "roots"))
        logits_done, xn_out, less_peak, exped, chosen, counted, places, tokens = (sem(n) for n in ("logits_done", "xn_out", "less_peak", "exped", "chosen", "counted", "places", "tokens"))
        iotas = sem("iotas")
        block = ctx.enter_context(nc.Block())

        @block.sync
        def _(sp):
            sp.dma_start(rw[:, :], k.a["L0_ffn_router_w"]).then_inc(rw_in, 16)
            sp.dma_start(k.x1_tab.rearrange("(p t) c -> p t c", p=P), k.res[:, :, :]).then_inc(xn_out, 16)
            sp.wait_ge(logits_done, 1)
            sp.dma_start(k.xn_tab.rearrange("(p t) c -> p t c", p=P), xn1[:, :, :]).then_inc(xn_out, 16)
            sp.wait_ge(xn_out, 32)

        @block.gpsimd
        def _(pool):
            me = st["pool"]
            nc.gpsimd.iota(expert[:, :], pattern=[[1, NE]], base=0, channel_multiplier=0, allow_small_or_imprecise_dtypes=True)
            nc.gpsimd.iota(item[:, :], pattern=[[1, NI]], base=0, channel_multiplier=0, allow_small_or_imprecise_dtypes=True)
            nc.gpsimd.iota(lane[:, :], pattern=[[1, M]], base=0, channel_multiplier=0, allow_small_or_imprecise_dtypes=True)
            me(pool, nc.gpsimd.memset(before[:, :], 1.0))
            nc.gpsimd.affine_select(out=before[:, :], in_=before[:, :], compare_op=ALU.is_ge, fill=0.0, base=-1,
                                    pattern=[[1, P]], channel_multiplier=-1).then_inc(iotas, 1)

        @block.tensor
        def _(pe):
            pe.wait_ge(rw_in, 16)
            for c in range(2):
                m = nc.tensor.transpose(k.ps[0][:, c * NE:(c + 1) * NE], rw[:, c * 128:(c + 1) * 128], k.ident[0:NE, 0:NE])
            m.then_inc(rw_turned, 1)
            pe.wait_ge(rw_ready, 1)

            def multiply(s):
                for c in range(2):
                    m = nc.tensor.matmul(k.ps[3 + s][0:P, 0:NE], q.xt[:, s, c, :], rwt[:, c, :], start=(c == 0), stop=(c == 1))
                return m

            q.on_tensor(pe, multiply)
            pe.wait_ge(iotas, 1)
            pe.wait_ge(chosen, 1)
            flat = both[:, :, :].rearrange("p t e -> p (t e)")
            nc.tensor.matmul(k.ps[0][0:P, 0:NT * NE], before[:, :], flat, start=True, stop=True)
            nc.tensor.matmul(k.ps[1][0:P, 0:NT * NE], k.ones[0:P, 0:P], flat, start=True, stop=True).then_inc(counted, 1)
            pe.wait_ge(places, 1)
            for j in range(2 * NT):
                m = nc.tensor.matmul(k.ps[2][:, 0:NI], at_lane[:, j, :], at_item[:, j, :], start=(j == 0), stop=(j == 2 * NT - 1))
            m.then_inc(tokens, 1)

        @block.scalar
        def _(act):
            norm_roots(k, act, deviations, roots)
            q.on_scalar(act)
            act.wait_ge(less_peak, 1)
            nc.scalar.activation(prob[:, :, :], prob[:, :, :], ACT.Exp).then_inc(exped, 1)

        @block.vector
        def _(dve):
            v, me = nc.vector, st["dve"]

            def wide(a):
                return a[:, :].rearrange("p (t a) -> p t a", a=1).to_broadcast([P, NT, NE])

            def long(a):
                return a[:, :].rearrange("p (a e) -> p a e", a=1).to_broadcast([P, NT, NE])

            dve.wait_ge(rw_turned, 1)
            v.tensor_copy(rwt[:, :, :], k.ps[0][:, 0:2 * NE].rearrange("p (a e) -> p a e", a=2)).then_inc(rw_ready, 1)
            norm_stats(k, dve, k.res, None, deviations, roots)

            def fill(t, s):
                me(dve, normed(k, q.xn[:, s, :], t))
                return v.tensor_scalar(tile_of(xn1, t), q.xn[:, s, :], 1.0, None, ALU.mult)

            def take(t, s):
                return v.tensor_scalar(tile_of(prob, t), k.ps[3 + s][0:P, 0:NE], 1.0, None, ALU.mult)

            q.on_vector(dve, fill, take, TB)
            me(dve, v.tensor_copy(den[:, :], k.rstd[:, :]))
            dve.sem_inc(logits_done, 1)
            me(dve, v.tensor_reduce(peak[:, :], prob[:, :, :], AX, ALU.max))
            v.tensor_tensor(prob[:, :, :], prob[:, :, :], wide(peak), ALU.subtract).then_inc(less_peak, 1)
            dve.wait_ge(exped, 1)
            me(dve, v.tensor_reduce(den[:, :], prob[:, :, :], AX, ALU.add))
            me(dve, v.reciprocal(den[:, :], den[:, :]))
            me(dve, v.tensor_tensor(prob[:, :, :], prob[:, :, :], wide(den), ALU.mult))
            dve.wait_ge(iotas, 1)
            v.tensor_copy(rest[:, :, :], prob[:, :, :])
            me(dve, v.tensor_scalar(tiles[:, :], expert[:, :], -float(NE), None, ALU.add))
            for j in range(2):
                me(dve, v.tensor_reduce(k.gate[:, j, :], rest[:, :, :], AX, ALU.max))
                me(dve, v.tensor_tensor(hit[:, :, :], rest[:, :, :], wide(k.gate[:, j, :]), ALU.is_equal))
                me(dve, v.tensor_tensor(cand[:, :, :], hit[:, :, :], long(tiles), ALU.mult))
                me(dve, v.tensor_reduce(idx[:, :], cand[:, :, :], AX, ALU.min))
                me(dve, v.tensor_scalar(idx[:, :], idx[:, :], float(NE), None, ALU.add))
                me(dve, v.tensor_tensor(oh[:, j, :, :], wide(idx), long(expert), ALU.is_equal))
                if j == 0:
                    me(dve, v.scalar_tensor_tensor(out=rest[:, :, :], in0=oh[:, 0, :, :], scalar=-2.0, in1=rest[:, :, :], op0=ALU.mult, op1=ALU.add))
            me(dve, v.tensor_tensor(both[:, :, :], oh[:, 0, :, :], oh[:, 1, :, :], ALU.add))
            dve.sem_inc(chosen, 1)
            me(dve, v.scalar_tensor_tensor(out=den[:, :], in0=k.gate[:, 0, :], scalar=1e-9, in1=k.gate[:, 1, :], op0=ALU.add, op1=ALU.add))
            me(dve, v.reciprocal(den[:, :], den[:, :]))
            for j in range(2):
                v.tensor_tensor(k.gate[:, j, :], k.gate[:, j, :], den[:, :], ALU.mult)
            dve.wait_ge(counted, 1)
            me(dve, v.tensor_copy(tot[:, :, :], k.ps[1][0:P, 0:NT * NE].rearrange("p (t e) -> p t e", e=NE)))
            for e in range(NE):
                m = v.tensor_tensor_scan(inc[:, :, e], k.ones[0:P, 0:NT], tot[:, :, e], 0.0, ALU.mult, ALU.add)
            me(dve, m)
            me(dve, v.tensor_scalar(tiles[:, :], inc[:, NT - 1, :], float(M - 1), None, ALU.add))
            me(dve, v.tensor_copy(tiles_i[:, :], tiles[:, :]))
            me(dve, v.tensor_single_scalar(tiles_i[:, :], tiles_i[:, :], 7, ALU.logical_shift_right))
            me(dve, v.tensor_copy(tiles[:, :], tiles_i[:, :]))
            me(dve, v.tensor_tensor_scan(ends[:, :], k.ones[0:P, 0:NE], tiles[:, :], 0.0, ALU.mult, ALU.add))
            me(dve, v.tensor_tensor(begins[:, :], ends[:, :], tiles[:, :], ALU.subtract))
            me(dve, v.tensor_scalar(begins[:, :], begins[:, :], float(M), None, ALU.mult))
            me(dve, v.tensor_tensor(slot[:, :, :], inc[:, :, :], tot[:, :, :], ALU.subtract))
            me(dve, v.tensor_tensor(slot[:, :, :], slot[:, :, :], k.ps[0][0:P, 0:NT * NE].rearrange("p (t e) -> p t e", e=NE), ALU.add))
            me(dve, v.tensor_tensor(slot[:, :, :], slot[:, :, :], long(begins), ALU.add))
            for j in range(2):
                me(dve, v.tensor_tensor(cand[:, :, :], oh[:, j, :, :], slot[:, :, :], ALU.mult))
                me(dve, v.tensor_reduce(pos[:, j, :], cand[:, :, :], AX, ALU.add))
            me(dve, v.tensor_copy(k.place[:, :, :], pos[:, :, :]))
            me(dve, v.tensor_single_scalar(hi_i[:, :, :], k.place[:, :, :], 7, ALU.logical_shift_right))
            me(dve, v.tensor_copy(hi[:, :, :], hi_i[:, :, :]))
            me(dve, v.scalar_tensor_tensor(out=lo[:, :, :], in0=hi[:, :, :], scalar=-float(M), in1=pos[:, :, :], op0=ALU.mult, op1=ALU.add))
            v.tensor_tensor(at_lane[:, :, :], lane[:, :].rearrange("p (a m) -> p a m", a=1).to_broadcast([P, 2 * NT, M]),
                            lo[:, :, :].rearrange("p j (t a) -> p (j t) a", a=1).to_broadcast([P, 2 * NT, M]), ALU.is_equal)
            me(dve, v.tensor_tensor(at_item[:, :, :], item[:, :].rearrange("p (a m) -> p a m", a=1).to_broadcast([P, 2 * NT, NI]),
                                    hi[:, :, :].rearrange("p j (t a) -> p (j t) a", a=1).to_broadcast([P, 2 * NT, NI]), ALU.is_equal))
            for j in range(2):
                m = v.tensor_tensor(at_item[:, j * NT:(j + 1) * NT, :], at_item[:, j * NT:(j + 1) * NT, :],
                                    k.node[:, :].rearrange("p (t a) -> p t a", a=1).to_broadcast([P, NT, NI]), ALU.mult)
            me(dve, m)
            dve.sem_inc(places, 1)
            me(dve, v.tensor_tensor(over[:, :, :], item[:, :].rearrange("p (i a) -> p i a", a=1).to_broadcast([P, NI, NE]),
                                    ends[:, :].rearrange("p (a e) -> p a e", a=1).to_broadcast([P, NI, NE]), ALU.is_ge))
            me(dve, v.tensor_reduce(of_item[:, :], over[:, :, :], AX, ALU.add))
            me(dve, v.tensor_scalar(k.item_expert[:, :], of_item[0:1, :], float(NE - 1), None, ALU.min))
            dve.wait_ge(tokens, 1)
            me(dve, v.tensor_copy(k.slot_token[:, :], k.ps[2][:, 0:NI]))


def weights_phase(k):
    nc = k.nc
    ctx = ExitStack()
    FB = HID // 128
    TAIL = HID - FB * 128
    with ctx:
        sb = lambda n, s, d=F32: k.sb(f"w_{n}", s, d, ctx)
        sem = lambda n: k.sem(f"w_{n}")
        raw = [[sb(f"raw{m}{s}", [128, FB + 1, C] if m < 2 else [128, 2, HID]) for s in range(2)] for m in range(3)]
        come = [[sem(f"come{m}{s}") for s in range(2)] for m in range(3)]
        turned, act_kept, dve_kept, used = sem("turned"), sem("act_kept"), sem("dve_kept"), sem("used")
        block = ctx.enter_context(nc.Block())
        names = ("L0_ffn_w1", "L0_ffn_w3", "L0_ffn_w2")

        def groups(e, s):
            for m in range(2):
                for c in range(2):
                    for b0, b1 in ((0, 4), (4, FB + 1)):
                        ins = [(raw[m][s][0:(128 if b < FB else TAIL), b, c * 128:(c + 1) * 128], (b - b0) * 128, 128 if b < FB else TAIL) for b in range(b0, b1)]
                        n = sum(x[2] for x in ins)
                        yield m, 128, ins, (k.w1t, k.w3t)[m][:, c, e, b0 * 128:b0 * 128 + n], n
            for a in range(2):
                for blocks in ((0, 1), (2,)):
                    rows = 128 if len(blocks) == 2 else HH - 256
                    ins = [(raw[2][s][:, c, a * HH + b * 128:a * HH + b * 128 + rows], (b - blocks[0]) * C + c * 128, 128) for b in blocks for c in range(2)]
                    yield 2, rows, ins, k.w2t[0:rows, 3 * a + blocks[0]:3 * a + blocks[-1] + 1, e, :], len(blocks) * C

        G = 12

        @block.sync
        def _(sp):
            for e in range(NE):
                s = e % 2
                if e >= 2:
                    sp.wait_ge(turned, G * (e - 1))
                for m, name in enumerate(names):
                    if m < 2:
                        sp.dma_start(raw[m][s][:, 0:FB, :], k.a[name][e, 0:FB * 128, :].rearrange("(b p) c -> p b c", p=128)).then_inc(come[m][s], 16)
                        sp.dma_start(raw[m][s][0:TAIL, FB, :], k.a[name][e, FB * 128:HID, :]).then_inc(come[m][s], 16)
                    else:
                        sp.dma_start(raw[m][s][:, :, :], k.a[name][e].rearrange("(a p) h -> p a h", p=128)).then_inc(come[m][s], 16)

        @block.tensor
        def _(pe):
            n = 0
            for e in range(NE):
                s = e % 2
                for m, rows, ins, dst, width in groups(e, s):
                    pe.wait_ge(come[m][s], (32 if m < 2 else 16) * (e // 2 + 1))
                    if n >= 8:
                        pe.wait_ge((act_kept, dve_kept)[n % 2], (n - 8) // 2 + 1)
                    for x, at, w in ins:
                        t = nc.tensor.transpose(k.ps[n % 8][0:rows, at:at + w], x, k.ident[0:x.shape[0], 0:x.shape[0]])
                    t.then_inc(turned, 1)
                    n += 1

        def keep(eng, odd, copy, kept):
            n = 0
            for e in range(NE):
                for m, rows, ins, dst, width in groups(e, e % 2):
                    if n % 2 == odd:
                        eng.wait_ge(turned, n + 1)
                        src = k.ps[n % 8][0:rows, 0:width]
                        copy(dst, src if m < 2 else src.rearrange("p (b c) -> p b c", c=C)).then_inc(kept, 1)
                    n += 1

        @block.scalar
        def _(act):
            keep(act, 0, nc.scalar.copy, act_kept)

        @block.vector
        def _(dve):
            keep(dve, 1, nc.vector.tensor_copy, dve_kept)


def experts_phase(k):
    nc = k.nc
    ctx = ExitStack()
    with ctx:
        sb = lambda n, s, d=F32: k.sb(f"e_{n}", s, d, ctx)
        sem = lambda n: k.sem(f"e_{n}")
        ix = [sb(f"ix{s}", [M, 1], I32) for s in range(2)]
        x = [sb(f"x{s}", [M, C]) for s in range(2)]
        xt = [sb(f"xt{s}", [128, 2, M]) for s in range(2)]
        gated = [sb(f"gated{a}", [M, HH]) for a in range(2)]
        h = [sb(f"h{a}", [M, HH]) for a in range(2)]
        ht = [sb(f"ht{s}", [128, 6, M]) for s in range(2)]
        y = [sb(f"y{s}", [M, C]) for s in range(2)]
        x_in = [k.gather_sem(f"e_x_in{s}") for s in range(2)]
        y_out = [sem(f"y_out{s}") for s in range(2)]
        ix_made, issuing, x_turned, x_kept = sem("ix_made"), sem("issuing"), sem("x_turned"), sem("x_kept")
        up, silued, h_made, h_turned, h_kept = sem("up"), sem("silued"), sem("h_made"), sem("h_turned"), sem("h_kept")
        down, y_kept, y_free = sem("down"), sem("y_kept"), sem("y_free")
        block = ctx.enter_context(nc.Block())
        TURN, UP, GATE, TH, DOWN = k.ps[0], (k.ps[1], k.ps[3]), (k.ps[2], k.ps[4]), (k.ps[5], k.ps[6]), k.ps[7]

        @block.gpsimd
        def _(pool):
            with pool.Fori(0, NI // 2) as i:
                for s in range(2):
                    pool.wait_ge(x_turned, i * 2 + s + 1)
                    nc.gpsimd.tensor_copy(ix[s][:, :], k.slot_token[:, bass.ds(i * 2 + s, 1)]).then_inc(ix_made, 1)
                    pool.wait_ge(ix_made, i * 2 + s + 1)
                    pool.sem_inc(issuing, 1)
                    pool.indirect_dma_start(out=x[s][:, :], out_offset=None, in_=k.xn_tab,
                                            in_offset=bass.IndirectOffsetOnAxis(ap=ix[s][:, 0:1], axis=0)).then_inc(x_in[s], 16)

        @block.sync
        def _(sp):
            rows = k.y_tab.rearrange("(i p) c -> i p c", p=M)
            sp.sem_inc(y_free, 2)
            with sp.Fori(0, NI // 2) as i:
                for s in range(2):
                    sp.wait_ge(y_kept, i * 2 + s + 2)
                    sp.dma_start(rows[bass.ds(i * 2 + s, 1), :, :].rearrange("a p c -> (a p) c"), y[s][:, :]).then_inc(y_out[s], 16)
                    sp.wait_ge(y_out[s], 16 * i + 16)
                    sp.sem_inc(y_free, 1)

        @block.tensor
        def _(pe):
            pe.sem_inc(x_turned, 2)
            pe.sem_inc(h_turned, 2)

            def turn_x(i, s):
                pe.wait_ge(x_in[s], 16 * ((i - s) // 2) + 16 if isinstance(i, int) else x_in_at[s] * 16 + 16)
                pe.wait_ge(x_kept, i + 1)
                for c in range(2):
                    m = nc.tensor.transpose(TURN[:, c * M:(c + 1) * M], x[s][:, c * 128:(c + 1) * 128], k.ident[:, :])
                m.then_inc(x_turned, 1)

            x_in_at = {}

            def go_up(i, s, a, e):
                if a == 0:
                    pe.wait_ge(x_kept, i + 2)
                pe.wait_ge(h_made, 2 * i + a + 1)
                for bank, w in ((UP[a], k.w1t), (GATE[a], k.w3t)):
                    for c in range(2):
                        m = nc.tensor.matmul(bank[:, 0:HH], xt[s][:, c, :], weights(w, c, e, a), start=(c == 0), stop=(c == 1))
                m.then_inc(up, 1)

            def weights(w, c, e, a):
                return w[:, c, bass.ds(e, 1), a * HH:(a + 1) * HH].rearrange("p a h -> p (a h)")

            def turn_h(i, s, a):
                pe.wait_ge(h_made, 2 * i + a + 3)
                pe.wait_ge(h_kept, 2 * i + a + 1)
                for (_, b, n) in HB[3 * a:3 * a + 3]:
                    m = nc.tensor.transpose(TH[a][0:n, b * M:(b + 1) * M], h[a][:, b * 128:b * 128 + n], k.ident[:, :])
                m.then_inc(h_turned, 1)

            def go_down(i, s, e):
                pe.wait_ge(h_kept, 2 * i + 4)
                pe.wait_ge(y_kept, i + 1)
                for j, (a, b, n) in enumerate(HB):
                    m = nc.tensor.matmul(DOWN[:, 0:C], ht[s][0:n, j, :], k.w2t[0:n, j, bass.ds(e, 1), :].rearrange("p a c -> p (a c)"),
                                         start=(j == 0), stop=(j == 5))
                m.then_inc(down, 1)

            def expert(i):
                return pe.value_load(k.item_expert[0:1, bass.ds(i, 1)], min_val=0, max_val=NE - 1)

            e0 = expert(0)
            turn_x(0, 0)
            go_up(0, 0, 0, e0)
            go_up(0, 0, 1, e0)
            turn_h(0, 0, 0)
            turn_x(1, 1)

            def item(i, s, more=True):
                e, e_before = expert(i), expert(i - 1)
                go_up(i, s, 0, e)
                turn_h(i - 1, 1 - s, 1)
                go_up(i, s, 1, e)
                go_down(i - 1, 1 - s, e_before)
                turn_h(i, s, 0)
                if more:
                    turn_x(i + 1, 1 - s)

            with pe.Fori(0, NI // 2 - 1) as i:
                x_in_at[0], x_in_at[1] = i + 1, i + 1
                item(i * 2 + 1, 1)
                item(i * 2 + 2, 0)
            item(NI - 1, 1, more=False)
            turn_h(NI - 1, 1, 1)
            go_down(NI - 1, 1, expert(NI - 1))

        @block.scalar
        def _(act):
            act.sem_inc(x_kept, 1)
            act.sem_inc(h_kept, 2)
            act.sem_inc(y_kept, 1)

            def keep_x(i, s):
                act.wait_ge(x_turned, i + 3)
                nc.scalar.copy(xt[s][:, :, :].rearrange("p a m -> p (a m)"), TURN[:, 0:2 * M]).then_inc(x_kept, 1)

            def silu(i, a):
                act.wait_ge(up, 2 * i + a + 1)
                nc.scalar.activation(gated[a][:, :], UP[a][:, 0:HH], ACT.Silu).then_inc(silued, 1)

            def keep_h(i, s, a):
                act.wait_ge(h_turned, 2 * i + a + 3)
                j = 3 * a
                nc.scalar.copy(ht[s][:, j:j + 2, :].rearrange("p b m -> p (b m)"), TH[a][:, 0:2 * M])
                n = HB[j + 2][2]
                nc.scalar.copy(ht[s][0:n, j + 2, :], TH[a][0:n, 2 * M:3 * M]).then_inc(h_kept, 1)

            def keep_y(i, s):
                act.wait_ge(down, i + 1)
                act.wait_ge(y_free, i + 1)
                nc.scalar.copy(y[s][:, :], DOWN[:, 0:C]).then_inc(y_kept, 1)

            keep_x(0, 0)
            silu(0, 0)
            silu(0, 1)
            keep_h(0, 0, 0)
            keep_x(1, 1)

            def item(i, s, more=True):
                silu(i, 0)
                keep_h(i - 1, 1 - s, 1)
                silu(i, 1)
                keep_y(i - 1, 1 - s)
                keep_h(i, s, 0)
                if more:
                    keep_x(i + 1, 1 - s)

            with act.Fori(0, NI // 2 - 1) as i:
                item(i * 2 + 1, 1)
                item(i * 2 + 2, 0)
            item(NI - 1, 1, more=False)
            keep_h(NI - 1, 1, 1)
            keep_y(NI - 1, 1)

        @block.vector
        def _(dve):
            dve.sem_inc(h_made, 2)
            with dve.Fori(0, NI) as i:
                for a in range(2):
                    dve.wait_ge(silued, i * 2 + a + 1)
                    dve.wait_ge(up, i * 2 + a + 1)
                    dve.wait_ge(h_turned, i * 2 + a + 1)
                    nc.vector.tensor_tensor(h[a][:, :], gated[a][:, :], GATE[a][:, 0:HH], ALU.mult).then_inc(h_made, 1)


def combine_phase(k):
    nc, st = k.nc, k.steps
    ctx = ExitStack()
    GROUPS = NT // TB
    with ctx:
        sb = lambda n, s, d=F32: k.sb(f"c_{n}", s, d, ctx)
        sem = lambda n: k.sem(f"c_{n}")
        ys = sb("ys", [P, 2, NT, C])
        xn = sb("xn", [P, NT, C])
        x1_in, deviations, roots, normed_s, out_done = (sem(n) for n in ("x1_in", "deviations", "roots", "normed", "out_done"))
        squares0 = sem("squares0")
        ys_in = [k.gather_sem(f"c_ys_in{g}") for g in range(GROUPS)]
        block = ctx.enter_context(nc.Block())

        @block.sync
        def _(sp):
            sp.dma_start(k.res[:, :, :], k.x1_tab.rearrange("(p t) c -> p t c", p=P)).then_inc(x1_in, 16)
            att = k.att
            squares_in, wx_in, small_in, bout_in = k.att_in
            for t, name in ((att["w_x"], "L1_ffn_W_x"), (att["w_fx"], "L1_ffn_W_fx"), (att["w_out"], "L1_ffn_W_out")):
                sp.dma_start(t[:, :, :], k.a[name].rearrange("(a p) c -> p a c", p=128)).then_inc(wx_in, 16)
            sp.dma_start(att["b_fx"][:, :], k.a["L1_ffn_b_fx"].rearrange("(a c) -> a c", a=1)).then_inc(small_in, 16)
            with nc.allow_non_contiguous_dma(reason="512 single values"):
                sp.dma_start(att["b_x"][:, :], k.a["L1_ffn_b_x"].rearrange("(a p) -> p a", p=128)).then_inc(small_in, 16)
            sp.dma_start(att["b_slice"][:, :, :], k.a["L1_ffn_b_slice"].rearrange("(a b c) -> a b c", a=1, b=1).to_broadcast([1, H, HD])).then_inc(small_in, 16)
            sp.dma_start(att["temp"][:, :], k.a["L1_ffn_temperature"].rearrange("a h b c -> a (h b c)")).then_inc(small_in, 16)
            sp.dma_start(att["temp_b"][:, :], k.a["L1_ffn_temperature"].rearrange("a h b c -> a (h b c)").to_broadcast([128, H])).then_inc(small_in, 16)
            sp.dma_start(att["b_out"][:, :], k.a["L1_ffn_b_out"].rearrange("(a c) -> a c", a=1).to_broadcast([P, C])).then_inc(bout_in, 16)
            sp.wait_ge(squares0, 1)
            for i, name in enumerate(("L1_ffn_W_slice", "L1_ffn_W_q", "L1_ffn_W_k", "L1_ffn_W_v")):
                for d in range(2):
                    sp.dma_start(att["square"][64 * d:64 * d + 64, i, 64 * d:64 * d + 64], k.a[name]).then_inc(squares_in, 16)
            table = k.xn_tab.rearrange("(p t) c -> p t c", p=P)
            for g in range(GROUPS):
                sp.wait_ge(normed_s, (g + 1) * TB)
                sp.dma_start(table[:, g * TB:(g + 1) * TB, :], xn[:, g * TB:(g + 1) * TB, :]).then_inc(out_done, 16)
            sp.wait_ge(out_done, 16 * GROUPS)

        @block.gpsimd
        def _(pool):
            nc.gpsimd.memset(k.att["square"][:, :, :], 0.0).then_inc(squares0, 1)
            for t in range(NT):
                for j in range(2):
                    pool.indirect_dma_start(out=ys[:, j, t, :], out_offset=None, in_=k.y_tab,
                                            in_offset=bass.IndirectOffsetOnAxis(ap=k.place[:, j, t:t + 1], axis=0)).then_inc(ys_in[t // TB], 16)

        @block.scalar
        def _(act):
            norm_roots(k, act, deviations, roots)

        @block.vector
        def _(dve):
            v, me = nc.vector, st["dve"]
            dve.wait_ge(x1_in, 16)
            for g in range(GROUPS):
                dve.wait_ge(ys_in[g], 16 * 2 * TB)
                for j in range(2):
                    for t in range(g * TB, (g + 1) * TB):
                        m = v.scalar_tensor_tensor(out=k.res[:, t, :], in0=ys[:, j, t, :], scalar=k.gate[:, j, t:t + 1], in1=k.res[:, t, :], op0=ALU.mult, op1=ALU.add)
                    me(dve, m)
                for t in range(g * TB, (g + 1) * TB):
                    v.bn_stats(k.stats[:, t, :], k.res[:, t, :])
            norm_factors(k, dve, deviations, roots)
            with dve.Fori(0, NT) as t:
                normed(k, tile_of(xn, t), t).then_inc(normed_s, 1)


HD = 64
NP = H * HD // 128
HG = H * HD




def gnn_node_phase(k):
    nc, st = k.nc, k.steps
    ctx = ExitStack()
    with ctx:
        sb = lambda n, s, d=F32: k.sb(f"n_{n}", s, d, ctx)
        sem = lambda n: k.sem(f"n_{n}")
        q = Turning(k, "n", ctx)
        square, diag, w_comb, bias_x, b_out = (k.att[n] for n in ("square", "diag", "w_comb", "bias", "b_out"))
        w_x, b_x, b_slice, temp, temp_b = (k.att[n] for n in ("w_x", "b_x", "b_slice", "temp", "temp_b"))
        w_xt = sb("w_xt", [128, NP, C])
        bias_row = sb("bias_row", [1, HG])
        squares_in, wx_in, small_in, bout_in = k.att_in
        prep, prep_pe = sem("prep"), sem("prep_pe")
        w, wt = sb("w", [128, 2, C]), sb("wt", [128, 2, C])
        bias = sb("bias", [P, C])
        inv, part = sb("inv", [P, NT]), sb("part", [P, NT])
        chain = sb("chain", [P, NT, RW])
        w_in, bias_in, w_turned, w_ready = sem("w_in"), sem("bias_in"), sem("w_turned"), sem("w_ready")
        chains_in = k.gather_sem("n_chains_in")
        block = ctx.enter_context(nc.Block())

        @block.sync
        def _(sp):
            sp.dma_start(w[:, :, :], k.a["L1_gnn_W"].rearrange("(a p) c -> p a c", p=128)).then_inc(w_in, 16)
            sp.dma_start(bias[:, :], k.a["L1_gnn_b"].rearrange("(a c) -> a c", a=1).to_broadcast([P, C])).then_inc(bias_in, 16)

        @block.gpsimd
        def _(pool):
            g, me = nc.gpsimd, st["pool"]
            me(pool, g.memset(diag[:, :], 0.0))
            g.memset(diag[0:64, 0:64], 1.0)
            me(pool, g.memset(diag[64:128, 64:128], 1.0))
            gather_rows(pool, chain, k.chains[:, :], k.chain_row, chains_in)

        @block.tensor
        def _(pe):
            pe.wait_ge(w_in, 16)
            for c in range(2):
                for a in range(2):
                    m = nc.tensor.transpose(k.ps[c][:, a * 128:(a + 1) * 128], w[:, a, c * 128:(c + 1) * 128], k.ident[:, :])
                m.then_inc(w_turned, 1)
            pe.wait_ge(w_ready, 2)
            t_ = nc.tensor
            pe.wait_ge(wx_in, 48)
            for a in range(NP):
                for c in range(2):
                    m = t_.transpose(k.ps[a][:, c * 128:(c + 1) * 128], w_x[:, c, a * 128:(a + 1) * 128], k.ident[:, :])
                m.then_inc(prep_pe, 1)
            pe.wait_ge(squares_in, 128)
            pe.wait_ge(small_in, 80)
            pe.wait_ge(prep, NP)
            for c in range(2):
                for a in range(NP):
                    m = t_.matmul(k.ps[4 + c][:, a * 128:(a + 1) * 128], w_xt[:, a, c * 128:(c + 1) * 128], square[:, 0, :], start=True, stop=True)
                m.then_inc(prep_pe, 1)
            for a in range(NP):
                m = t_.matmul(k.ps[6][0:1, a * 128:(a + 1) * 128], b_x[:, a:a + 1], square[:, 0, :], start=True, stop=True)
            m.then_inc(prep_pe, 1)
            pe.wait_ge(prep, NP + 1)
            t_.matmul(k.ps[7][0:P, :], k.ones[0:1, 0:P], bias_row[:, :], start=True, stop=True).then_inc(prep_pe, 1)
            pe.wait_ge(prep, NP + 4)

            def multiply(s):
                for c in range(2):
                    m = nc.tensor.matmul(k.ps[3 + s][0:P, 0:C], q.xt[:, s, c, :], wt[:, c, :], start=(c == 0), stop=(c == 1))
                return m

            q.on_tensor(pe, multiply)

        @block.scalar
        def _(act):
            q.on_scalar(act)

        @block.vector
        def _(dve):
            v, me = nc.vector, st["dve"]
            me(dve, v.tensor_scalar(inv[:, :], k.deg[:, :], 1.0, None, ALU.add))
            me(dve, v.reciprocal(inv[:, :], inv[:, :]))
            me(dve, v.tensor_tensor(part[:, :], inv[:, :], k.deg[:, :], ALU.mult))
            dve.wait_ge(bias_in, 16)
            with dve.Fori(0, NT) as t:
                v.scalar_tensor_tensor(out=tile_of(k.res, t), in0=bias[:, :], scalar=part[:, bass.ds(t, 1)], in1=tile_of(k.res, t), op0=ALU.mult, op1=ALU.add)
            for c in range(2):
                dve.wait_ge(w_turned, c + 1)
                v.tensor_copy(wt[:, c, :], k.ps[c][:, 0:C]).then_inc(w_ready, 1)
            for a in range(NP):
                dve.wait_ge(prep_pe, a + 1)
                v.tensor_copy(w_xt[:, a, :], k.ps[a][:, 0:C]).then_inc(prep, 1)
            dve.wait_ge(small_in, 80)
            for t in (temp, temp_b):
                me(dve, v.tensor_scalar(t[:, :], t[:, :], 0.1, 5.0, ALU.max, ALU.min))
                me(dve, v.reciprocal(t[:, :], t[:, :]))
            dve.wait_ge(prep_pe, NP + 3)
            me(dve, v.tensor_tensor(bias_row[:, :], k.ps[6][0:1, :], b_slice[:, :, :].rearrange("p h g -> p (h g)"), ALU.add))
            r = bias_row[:, :].rearrange("p (h g) -> p h g", h=H)
            v.tensor_tensor(r, r, temp[:, :].rearrange("p (h a) -> p h a", a=1).to_broadcast([1, H, HD]), ALU.mult).then_inc(prep, 1)
            for c in range(2):
                v.tensor_tensor(w_comb[:, c, :].rearrange("p (h g) -> p h g", h=H), k.ps[4 + c][:, :].rearrange("p (h g) -> p h g", h=H),
                                temp_b[:, :].rearrange("p (h a) -> p h a", a=1).to_broadcast([128, H, HD]), ALU.mult).then_inc(prep, 1)
            dve.wait_ge(prep_pe, NP + 4)
            v.tensor_copy(bias_x[:, :], k.ps[7][0:P, :]).then_inc(prep, 1)
            dve.wait_ge(bout_in, 16)

            dve.wait_ge(k.mains_in, 16 * NT)
            dve.wait_ge(chains_in, 16 * NT)

            def fill(t, s):
                return v.tensor_tensor(q.xn[:, s, :], tile_of(k.mains, t)[:, 0:C], tile_of(chain, t)[:, 0:C], ALU.add)

            def take(t, s):
                return v.scalar_tensor_tensor(out=tile_of(k.res, t), in0=k.ps[3 + s][0:P, 0:C], scalar=inv[:, bass.ds(t, 1)], in1=tile_of(k.res, t), op0=ALU.mult, op1=ALU.add)

            def stats(t):
                return v.bn_stats(tile_of(k.stats, t), tile_of(k.res, t))

            q.on_vector(dve, fill, take, after=stats)


def attention_phase(k):
    nc, st = k.nc, k.steps
    ctx = ExitStack()
    with ctx:
        sb = lambda n, s, d=F32: k.sb(f"t_{n}", s, d, ctx)
        sem = lambda n: k.sem(f"t_{n}")
        w_fx, w_out, square, diag, w_comb, b_fx, bias, b_out = (
            k.att[n] for n in ("w_fx", "w_out", "square", "diag", "w_comb", "b_fx", "bias", "b_out"))
        xn = sb("xn", [P, TB, C + 1])
        xt = sb("xt", [128, TB, 2, P])
        logit = sb("logit", [P, TB, H, HD])
        peak, total = sb("peak", [P, TB, H]), sb("total", [P, TB, H])
        wt = sb("wt", [128, NT, NP, P])
        u, inv = sb("u", [128, NP, C + 1]), sb("inv", [128, NP])
        ut, share = sb("ut", [128, 2, HG]), sb("share", [1, HG])
        token, qt, kt, val = (sb(n, [128, NP, 128]) for n in ("token", "qt", "kt", "val"))
        score, attn, attn_t, mixed = sb("score", [128, NP, HD]), sb("attn", [128, NP, 128]), sb("attn_t", [128, NP, 128]), sb("mixed", [128, NP, 128])
        apeak, asum = sb("apeak", [128, NP]), sb("asum", [128, NP])
        v2 = sb("v2", [128, NP, C])
        xones, deviations, roots = sem("xones"), sem("deviations"), sem("roots")
        made, turned, kept, logits, biased, peaked, less, exped, summed, weighed, w_turned, w_kept, added = (
            sem(n) for n in ("made", "turned", "kept", "logits", "biased", "peaked", "less", "exped", "summed", "weighed", "w_turned", "w_kept", "added"))
        mid, mid_pe, mid_act = sem("mid"), sem("mid_pe"), sem("mid_act")
        result, joined, stored = sem("result"), sem("joined"), sem("stored")
        block = ctx.enter_context(nc.Block())
        T, L, X, U = k.ps[0], (k.ps[1], k.ps[2]), k.ps[3], k.ps[4:8]

        @block.sync
        def _(sp):
            rows = k.out.rearrange("(p t) c -> p t c", p=P)
            with sp.Fori(0, NT // TB) as i:
                sp.wait_ge(joined, i * TB + TB)
                sp.dma_start(rows[:, bass.ds(i * TB, TB), :], k.res[:, bass.ds(i * TB, TB), :]).then_inc(stored, 16)
            sp.wait_ge(stored, 16 * (NT // TB))

        @block.gpsimd
        def _(pool):
            g, me = nc.gpsimd, st["pool"]
            g.memset(attn[:, :, :], 0.0).then_inc(xones, 1)
            pool.wait_ge(xones, 1)
            g.memset(xn[:, :, C:C + 1], 1.0).then_inc(xones, 1)

            def less_peak(t, s):
                pool.wait_ge(peaked, t + 1)
                g.tensor_tensor(logit[:, s, :, :], logit[:, s, :, :], peak[:, s, :].rearrange("p (h a) -> p h a", a=1).to_broadcast([P, H, HD]), ALU.subtract).then_inc(less, 1)

            def weigh(t, s):
                pool.wait_ge(summed, t + 1)
                g.tensor_tensor(logit[:, s, :, :], logit[:, s, :, :], total[:, s, :].rearrange("p (h a) -> p h a", a=1).to_broadcast([P, H, HD]), ALU.mult).then_inc(weighed, 1)

            def body(i):
                for s in range(TB):
                    less_peak(i * TB + s, s)
                    if s or not isinstance(i, int):
                        weigh(i * TB + s - 1, (s - 1) % TB)

            body(0)
            with pool.Fori(1, NT // TB) as i:
                body(i)
            weigh(NT - 1, TB - 1)

        @block.tensor
        def _(pe):
            t_ = nc.tensor
            pe.wait_ge(xones, 2)

            def turn(t, s):
                pe.wait_ge(made, t + 1)
                pe.wait_ge(kept, t + 1)
                for c in range(2):
                    m = t_.transpose(T[:, c * P:(c + 1) * P], xn[:, s, c * 128:(c + 1) * 128], k.ident[0:P, 0:P])
                m.then_inc(turned, 1)

            def score_nodes(t, s, bank, biased_at):
                pe.wait_ge(kept, t + 2)
                pe.wait_ge(biased, biased_at)
                for c in range(2):
                    m = t_.matmul(bank[0:P, :], xt[:, s, c, :], w_comb[:, c, :], start=(c == 0), stop=(c == 1))
                m.then_inc(logits, 1)

            def slices(t, s, first=False, last=False):
                pe.wait_ge(weighed, t + 1)
                pe.wait_ge(w_kept, t + 1)
                w = logit[:, s, :, :].rearrange("p h g -> p (h g)")
                for a in range(NP):
                    m = t_.transpose(X[:, a * P:(a + 1) * P], w[:, a * 128:(a + 1) * 128], k.ident[0:P, 0:P])
                m.then_inc(w_turned, 1)
                for a in range(NP):
                    m = t_.matmul(U[a][:, 0:C + 1], w[:, a * 128:(a + 1) * 128], xn[:, s, :], start=first, stop=last, skip_group_check=True)
                m.then_inc(added, 1)

            def body(i):
                for s in range(TB):
                    t = i * TB + s
                    turn(t, s)
                    score_nodes(t, s, L[s % 2], t + 1 if s == 0 else t)
                    if s >= 2 or not isinstance(i, int):
                        slices(t - 2, (s - 2) % TB, first=isinstance(t, int) and t == 2)

            body(0)
            with pe.Fori(1, NT // TB) as i:
                body(i)
            slices(NT - 2, TB - 2)
            slices(NT - 1, TB - 1, last=True)

            pe.wait_ge(w_kept, NT + 1)
            pe.wait_ge(mid, 1)
            for c in range(2):
                for a in range(NP):
                    m = t_.transpose(k.ps[c][:, a * 128:(a + 1) * 128], u[:, a, c * 128:(c + 1) * 128], k.ident[:, :])
                m.then_inc(mid_pe, 1)
            for a in range(NP):
                m = t_.transpose(k.ps[2][0:1, a * 128:(a + 1) * 128], u[:, a, C:C + 1], k.ident[:, :])
            m.then_inc(mid_pe, 1)
            pe.wait_ge(mid, 4)
            for a in range(NP):
                cols = slice(a * 128, (a + 1) * 128)
                for c in range(2):
                    t_.matmul(k.ps[3][:, cols], w_fx[:, c, cols], ut[:, c, cols], start=(c == 0), stop=False)
                m = t_.matmul(k.ps[3][:, cols], b_fx[:, cols], share[:, cols], start=False, stop=True)
            m.then_inc(mid_pe, 1)
            pe.wait_ge(mid, 5)
            for a in range(NP):
                cols = slice(a * 128, (a + 1) * 128)
                t_.matmul(k.ps[4][:, cols], square[:, 1, :], token[:, a, :], start=True, stop=True)
                t_.matmul(k.ps[5][:, cols], square[:, 2, :], token[:, a, :], start=True, stop=True)
                m = t_.matmul(k.ps[6][:, cols], token[:, a, :], square[:, 3, :], start=True, stop=True)
            m.then_inc(mid_pe, 1)
            pe.wait_ge(mid, 8)
            for a in range(NP):
                m = t_.matmul(k.ps[7][:, a * 128:(a + 1) * 128], qt[:, a, :], kt[:, a, :], start=True, stop=True)
            m.then_inc(mid_pe, 1)
            pe.wait_ge(mid, 9)
            for a in range(NP):
                m = t_.transpose(k.ps[0][:, a * 128:(a + 1) * 128], attn[:, a, :], k.ident[:, :])
            m.then_inc(mid_pe, 1)
            pe.wait_ge(mid, 10)
            for a in range(NP):
                m = t_.matmul(k.ps[1][:, a * 128:(a + 1) * 128], val[:, a, :], attn_t[:, a, :], start=True, stop=True)
            m.then_inc(mid_pe, 1)
            pe.wait_ge(mid, 11)
            for a in range(NP):
                m = t_.matmul(k.ps[2 + a // 2][:, (a % 2) * C:(a % 2 + 1) * C], mixed[:, a, :], w_out[:, a, :], start=True, stop=True)
            m.then_inc(mid_pe, 1)
            pe.wait_ge(mid, 13)

            for t in range(NT):
                if t >= 8:
                    pe.wait_ge(joined, t - 7)
                for a in range(NP):
                    m = t_.matmul(k.ps[t % 8][0:P, 0:C], wt[:, t, a, :], v2[:, a, :], start=(a == 0), stop=(a == NP - 1))
                m.then_inc(result, 1)

        @block.scalar
        def _(act):
            a_ = nc.scalar
            norm_roots(k, act, deviations, roots)
            act.sem_inc(kept, 1)
            act.sem_inc(w_kept, 1)

            def keep(t, s):
                act.wait_ge(turned, t + 1)
                a_.copy(xt[:, s, :, :].rearrange("p a n -> p (a n)"), T[:, 0:2 * P]).then_inc(kept, 1)

            def exp(t, s):
                act.wait_ge(less, t + 1)
                a_.activation(logit[:, s, :, :], logit[:, s, :, :], ACT.Exp).then_inc(exped, 1)

            def keep_w(t, s):
                act.wait_ge(w_turned, t + 1)
                a_.copy(wt[:, bass.ds(t, 1), :, :].rearrange("p b a n -> p (b a n)"), X[:, 0:NP * P]).then_inc(w_kept, 1)

            def body(i):
                for s in range(TB):
                    t = i * TB + s
                    keep(t, s)
                    if s or not isinstance(i, int):
                        exp(t - 1, (s - 1) % TB)
                    if s >= 2 or not isinstance(i, int):
                        keep_w(t - 2, (s - 2) % TB)

            body(0)
            with act.Fori(1, NT // TB) as i:
                body(i)
            exp(NT - 1, TB - 1)
            keep_w(NT - 2, TB - 2)
            keep_w(NT - 1, TB - 1)
            act.wait_ge(mid_act, 1)
            a_.activation(score[:, :, :], score[:, :, :], ACT.Exp, scale=float(HD) ** -0.5).then_inc(mid_act, 1)

        @block.vector
        def _(dve):
            v, me = nc.vector, st["dve"]
            norm_factors(k, dve, deviations, roots)
            dve.wait_ge(xones, 2)
            dve.sem_inc(biased, 1)

            def fill(t, s):
                normed(k, xn[:, s, 0:C], t).then_inc(made, 1)

            def add_bias(t, s):
                dve.wait_ge(logits, t + 1)
                v.tensor_tensor(logit[:, s, :, :].rearrange("p h g -> p (h g)"), L[s % 2][0:P, :], bias[:, :], ALU.add).then_inc(biased, 1)
                dve.wait_ge(biased, t + 2)
                v.tensor_reduce(peak[:, s, :], logit[:, s, :, :], AX, ALU.max).then_inc(peaked, 1)

            def add_up(t, s):
                dve.wait_ge(exped, t + 1)
                me(dve, v.tensor_reduce(total[:, s, :], logit[:, s, :, :], AX, ALU.add))
                v.reciprocal(total[:, s, :], total[:, s, :]).then_inc(summed, 1)

            def body(i):
                first = isinstance(i, int)
                if not first:
                    me.loop(i - 1, TB)
                for s in range(TB):
                    if not first:
                        dve.wait_ge(added, i * TB + s - TB + 1)
                    fill(i * TB + s, s)
                    add_bias(i * TB + s, s)
                    if s or not first:
                        add_up(i * TB + s - 1, (s - 1) % TB)
                if not first:
                    me.end(NT // TB - 1)

            body(0)
            with dve.Fori(1, NT // TB) as i:
                body(i)
            add_up(NT - 1, TB - 1)

            dve.wait_ge(added, NT)
            for a in range(NP):
                m = v.tensor_scalar(inv[:, a:a + 1], U[a][:, C:C + 1], 1e-5, None, ALU.add)
            me(dve, m)
            me(dve, v.reciprocal(inv[:, :], inv[:, :]))
            for a in range(NP):
                m = v.tensor_scalar(u[:, a, :], U[a][:, 0:C + 1], inv[:, a:a + 1], None, ALU.mult)
            m.then_inc(mid, 1)
            for c in range(2):
                dve.wait_ge(mid_pe, c + 1)
                v.tensor_copy(ut[:, c, :], k.ps[c][:, :]).then_inc(mid, 1)
            dve.wait_ge(mid_pe, 3)
            v.tensor_copy(share[:, :], k.ps[2][0:1, :]).then_inc(mid, 1)
            dve.wait_ge(mid_pe, 4)
            v.tensor_tensor(token[:, :, :], k.ps[3][:, :].rearrange("p (a g) -> p a g", a=NP),
                            diag[:, :].rearrange("p (b g) -> p b g", b=1).to_broadcast([128, NP, 128]), ALU.mult).then_inc(mid, 1)
            dve.wait_ge(mid_pe, 5)
            for t, b in ((qt, 4), (kt, 5), (val, 6)):
                v.tensor_copy(t[:, :, :].rearrange("p a g -> p (a g)"), k.ps[b][:, :]).then_inc(mid, 1)
            dve.wait_ge(mid_pe, 6)
            for d in range(2):
                rows = slice(64 * d, 64 * d + 64)
                m = v.tensor_copy(score[rows, :, :], k.ps[7][rows, :].rearrange("p (a g) -> p a g", a=NP)[:, :, 64 * d:64 * d + 64])
            me(dve, m)
            me(dve, v.tensor_reduce(apeak[:, :], score[:, :, :], AX, ALU.max))
            v.tensor_tensor(score[:, :, :], score[:, :, :], apeak[:, :].rearrange("p (a b) -> p a b", b=1).to_broadcast([128, NP, HD]), ALU.subtract).then_inc(mid_act, 1)
            dve.wait_ge(mid_act, 2)
            me(dve, v.tensor_reduce(asum[:, :], score[:, :, :], AX, ALU.add))
            me(dve, v.reciprocal(asum[:, :], asum[:, :]))
            for d in range(2):
                rows = slice(64 * d, 64 * d + 64)
                m = v.tensor_tensor(attn[rows, :, 64 * d:64 * d + 64], score[rows, :, :],
                                    asum[rows, :].rearrange("p (a b) -> p a b", b=1).to_broadcast([64, NP, HD]), ALU.mult)
            m.then_inc(mid, 1)
            dve.wait_ge(mid_pe, 7)
            v.tensor_copy(attn_t[:, :, :].rearrange("p a g -> p (a g)"), k.ps[0][:, :]).then_inc(mid, 1)
            dve.wait_ge(mid_pe, 8)
            v.tensor_copy(mixed[:, :, :].rearrange("p a g -> p (a g)"), k.ps[1][:, :]).then_inc(mid, 1)
            dve.wait_ge(mid_pe, 9)
            for a in range(2):
                v.tensor_copy(v2[:, 2 * a:2 * a + 2, :].rearrange("p a c -> p (a c)"), k.ps[2 + a][:, :]).then_inc(mid, 1)
            me(dve, v.tensor_tensor(k.res[:, :, :], k.res[:, :, :], b_out[:, :].rearrange("p (a c) -> p a c", a=1).to_broadcast([P, NT, C]), ALU.add))
            for t in range(NT):
                dve.wait_ge(result, t + 1)
                v.tensor_tensor(k.res[:, t, :], k.res[:, t, :], k.ps[t % 8][0:P, 0:C], ALU.add).then_inc(joined, 1)


def build(nc, out, **arrays):
    ctx = ExitStack()
    with ctx:
        k = Kernel(nc, ctx, out, arrays)
        setup(k)
        k.open_layer()
        with ExitStack() as gat:
            k.adst_e = k.sb("adst_e", [EP, ET, H], F32, gat)
            with ExitStack() as projecting:
                k.xh = k.sb("xh", [P, NT, RW], F32, projecting)
                first_phase(k)
                spread_phase(k)
            edge_phase(k, "gat", k.xh_tab, XW, True)
        with ExitStack() as gat:
            k.xh = k.sb("xh_back", [P, NT, RW], F32, gat)
            k.mains, k.mains_in = k.sb("gat_mains", [P, NT, RW], F32, gat), k.gather_sem("gat_mains_in")
            chain_phase(k, "gat", True)
            gat_node_phase(k)
        k.close_layer()
        k.open_layer()
        router_phase(k)
        with ExitStack() as moe:
            k.w1t, k.w3t = (k.sb(n, [128, 2, NE, HID], F32, moe) for n in ("w1t", "w3t"))
            k.w2t = k.sb("w2t", [128, 6, NE, C], F32, moe)
            weights_phase(k)
            experts_phase(k)
        k.att = {n: k.sb(f"att_{n}", s) for n, s in (
            ("w_fx", [128, 2, HG]), ("w_out", [128, NP, C]), ("w_comb", [128, 2, HG]), ("diag", [128, 128]),
            ("square", [128, 4, 128]),
            ("b_fx", [1, HG]), ("bias", [P, HG]), ("b_out", [P, C]), ("w_x", [128, 2, HG]), ("b_x", [128, NP]),
            ("b_slice", [1, H, HD]), ("temp", [1, H]), ("temp_b", [128, H]))}
        k.att_in = [ctx.enter_context(nc.semaphore(f"att_{n}_in")) for n in ("squares", "w", "small", "b_out")]
        combine_phase(k)
        k.close_layer()
        k.open_layer()
        edge_phase(k, "gnn", k.xn_tab, C, False)
        with ExitStack() as gnn:
            k.mains, k.mains_in = k.sb("gnn_mains", [P, NT, RW], F32, gnn), k.gather_sem("gnn_mains_in")
            chain_phase(k, "gnn", False)
            gnn_node_phase(k)
        attention_phase(k)
        k.close_layer()
_INS = ['x','src','dst','L0_gnn_W','L0_gnn_att_src','L0_gnn_att_dst','L0_gnn_bias','L0_gnn_gamma','L0_gnn_beta','L0_ffn_router_w','L0_ffn_w1','L0_ffn_w2','L0_ffn_w3','L1_gnn_W','L1_gnn_b','L1_ffn_W_fx','L1_ffn_b_fx','L1_ffn_W_x','L1_ffn_b_x','L1_ffn_W_slice','L1_ffn_b_slice','L1_ffn_W_q','L1_ffn_W_k','L1_ffn_W_v','L1_ffn_W_out','L1_ffn_b_out','L1_ffn_temperature']


def kernel(**inputs):
    import numpy as _np
    import concourse.bacc as _bacc
    from concourse import mybir as _mybir
    from concourse.bass_utils import run_bass_kernel_spmd as _run

    nc = _bacc.Bacc("TRN2", target_bir_lowering=False, num_devices=1)
    arrays, args = {}, {}
    for name in _INS:
        a = _np.ascontiguousarray(inputs[name])
        arrays[f"in_{name}_dram"] = a
        args[name] = nc.dram_tensor(f"in_{name}_dram", a.shape, _mybir.dt.from_np(a.dtype), kind="ExternalInput").ap()
    out = nc.dram_tensor("out_0_dram", (3125, 256), _mybir.dt.float32, kind="ExternalOutput").ap()
    build(nc, out, **args)
    r = _run(nc, [arrays], core_ids=[0])
    return r.results[0]["out_0_dram"]
```

```python
from contextlib import ExitStack

import numpy as np
import concourse.bass as bass
from concourse import mybir

F32 = mybir.dt.float32
F32R = mybir.dt.float32r
I32 = mybir.dt.int32
U32 = mybir.dt.uint32
ALU = mybir.AluOpType
ACT = mybir.ActivationFunctionType
AX = mybir.AxisListType.X

N, C, E = 3125, 256, 50000
P, NT = 125, 25
TB = 5
H, D = 8, 32
EP = 128
ET = 392
SB = 14
NB = ET // SB
Q, J = 98, 4
XW = C + H
RW = C + 2 * H
NO_ROW = ET * EP
NO_CHAIN = ET
BIG = 3e38
EPS = 1e-5


class Steps:

    def __init__(self, sem):
        self.sem, self.n, self.turn = sem, 0, None

    def __call__(self, eng, ins):
        ins.then_inc(self.sem, 1)
        self.n += 1
        eng.wait_ge(self.sem, self.n if self.turn is None else self.turn * self.k + self.n)

    def loop(self, turn, k):
        self.turn, self.k, self.first = turn, k, self.n

    def end(self, turns):
        assert self.n - self.first == self.k, (self.n - self.first, self.k)
        self.n, self.turn = self.first + self.k * turns, None


class Kernel:

    def __init__(self, nc, ctx, out, arrays):
        self.nc, self.ctx, self.out, self.a = nc, ctx, out, arrays
        self.opened = None
        self.steps = {e: Steps(self.sem(f"{e}_steps")) for e in ("pe", "act", "dve", "pool")}

    def sb(self, name, shape, dt=F32, ctx=None):
        return (ctx or self.ctx).enter_context(self.nc.sbuf_tensor(name, shape, dt))

    def sem(self, name):
        s = self.nc.semaphore(name)
        if self.opened is None:
            return self.ctx.enter_context(s)
        self.opened.append(self.layer.enter_context(s))
        return self.opened[-1]

    def gather_sem(self, name):
        return self.ctx.enter_context(self.nc.semaphore(name))

    def open_layer(self):
        self.opened, self.layer = [], ExitStack()

    def close_layer(self):
        with self.nc.Block() as block:

            @block.gpsimd
            def _(pool):
                for s in self.opened:
                    pool.sem_clear(s)
        self.layer.close()
        self.opened = None

    def dram(self, name, shape, dt=F32):
        return self.nc.dram_tensor(name, shape, dt, kind=SCRATCH).ap()


SCRATCH = "Internal"


def setup(k):
    k.ps = [k.ctx.enter_context(k.nc.psum_tensor(f"bank{i}", [128, 512], F32)) for i in range(8)]
    k.ident = k.sb("ident", [128, 128])
    k.ones = k.sb("ones", [128, 128])
    k.res = k.sb("res", [P, NT, C])
    k.stats = k.sb("stats", [P, NT, 6])
    k.mv = k.sb("mv", [P, NT, 2])
    k.rstd = k.sb("rstd", [P, NT])
    k.node = k.sb("node", [P, NT])
    k.deg = k.sb("deg", [P, NT])
    k.main_row = k.sb("main_row", [P, NT], I32)
    k.chain_row = k.sb("chain_row", [P, NT], I32)
    k.start_row = k.sb("start_row", [P, NT], I32)
    k.src_e = k.sb("src_e", [EP, ET], I32)
    k.dst_e = k.sb("dst_e", [EP, ET])
    k.fwd_e = k.sb("fwd_e", [EP, ET])
    k.bwd_e = k.sb("bwd_e", [EP, ET])
    k.joins = k.sb("joins", [128, ET])
    k.cont_q = k.sb("cont_q", [Q, J * EP])
    k.tile_dst = k.sb("tile_dst", [Q, J], I32)
    k.xh_tab = k.dram("xh_tab", [N, XW])
    k.adst_tab = k.dram("adst_tab", [N, H])
    k.adst_edge = k.dram("adst_edge", [ET * EP, H])
    k.gate = k.sb("gate", [P, 2, NT])
    k.place = k.sb("place", [P, 2, NT], I32)
    k.item_expert = k.sb("item_expert", [1, NI], I32)
    k.slot_token = k.sb("slot_token", [M, NI], I32)
    k.x1_tab, k.xn_tab, k.y_tab = k.dram("x1_tab", [N, C]), k.dram("xn_tab", [N, C]), k.dram("y_tab", [NI * M, C])
    k.dst_pad = k.dram("dst_pad", [ET * EP])
    k.start_tab = k.dram("start_tab", [N + 1])
    k.parts = k.dram("parts", [ET * EP + 1, RW])
    k.chains = k.dram("chains", [ET + 1, RW])


def tile_of(a, t):
    return a[:, bass.ds(t, 1), :].rearrange("p a c -> p (a c)")


def first_phase(k):
    nc, st = k.nc, k.steps
    ctx = ExitStack()
    with ctx:
        sb = lambda n, s, d=F32: k.sb(n, s, d, ctx)
        srcq_i, dstq_i = sb("srcq_i", [Q, J * EP], I32), sb("dstq_i", [Q, J * EP], I32)
        srcq, dstq = sb("srcq", [Q, J * EP]), sb("dstq", [Q, J * EP])
        same = sb("same", [Q, J * EP + 1])
        first_b = sb("first_b", [128, ET])
        last_b = sb("last_b", [128, ET])
        trash = sb("trash", [P, NT, ET])
        before = sb("before", [P, NT])
        tile = sb("tile", [P, NT])
        tile_i = sb("tile_i", [P, NT], I32)
        window = sb("window", [P, NT, EP])
        start, end, last = sb("start", [P, NT]), sb("end", [P, NT]), sb("last", [P, NT])
        last_i, has, t0, t1 = sb("last_i", [P, NT], I32), sb("has", [P, NT]), sb("t0", [P, NT]), sb("t1", [P, NT])
        total = sb("total", [1, 1])
        w = sb("w", [128, 2, RW])
        att = sb("att", [128, 2, C])
        prod = sb("prod", [128, 2, C])
        xn = sb("xn", [P, TB, C])
        xt = sb("xt", [128, TB, 2, P])
        zeros = sb("zeros", [Q, J * EP])
        zeroed, cleared = k.sem("zeroed"), k.sem("cleared")
        mark = sb("mark", [1, 1])
        w_in, att_in = k.sem("w_in"), k.sem("att_in")
        deviations, roots = k.sem("p_deviations"), k.sem("p_roots")
        w_ready = k.sem("w_ready")
        xn_made, xt_turned, xt_made = k.sem("p_xn_made"), k.sem("p_xt_turned"), k.sem("p_xt_made")
        projected, taken, out_done = k.sem("projected"), k.sem("p_taken"), k.sem("p_out_done")
        padded = k.sem("padded")
        edges_in = k.sem("edges_in")
        x_in = k.sem("x_in")
        banks_read = k.sem("banks_read")
        consts = k.sem("consts")
        edges_f = k.sem("edges_f")
        pad_out = k.sem("pad_out")
        turned = k.sem("turned")
        ends_b = k.sem("ends_b")
        tiles_found = k.sem("tiles_found")
        windows_in = k.gather_sem("windows_in")
        starts_found = k.sem("starts_found")
        starts_out = k.sem("starts_out")
        ends_in = k.sem("ends_in")
        full = E // (J * EP)
        rest = E - full * J * EP

        block = ctx.enter_context(nc.Block())

        @block.sync
        def _(sp):
            sp.wait_ge(padded, 2)
            for a, t in ((k.a["dst"], dstq_i), (k.a["src"], srcq_i)):
                sp.dma_start(t[0:full, :], a[0:full * J * EP].rearrange("(q e) -> q e", e=J * EP)).then_inc(edges_in, 16)
                sp.dma_start(t[full:full + 1, 0:rest], a[full * J * EP:E].rearrange("(q e) -> q e", q=1)).then_inc(edges_in, 16)
            sp.wait_ge(zeroed, 1)
            for h in range(H):
                sp.dma_start(k.adst_edge.rearrange("(q m) h -> q (m h)", q=Q)[:, h * J * EP:(h + 1) * J * EP], zeros[:, :]).then_inc(cleared, 16)
            sp.wait_ge(edges_f, 1)
            sp.dma_start(k.dst_pad.rearrange("(q e) -> q e", q=Q), dstq[:, :]).then_inc(pad_out, 16)
            sp.wait_ge(starts_found, 1)
            sp.dma_start(k.start_tab[0:N].rearrange("(p t) -> p t", p=P), start[:, :]).then_inc(starts_out, 16)
            sp.dma_start(k.start_tab[N:N + 1].rearrange("(a b) -> a b", a=1), total[:, :]).then_inc(starts_out, 16)
            sp.wait_ge(starts_out, 32)
            sp.dma_start(end[:, :], k.start_tab[1:N + 1].rearrange("(p t) -> p t", p=P)).then_inc(ends_in, 16)
            sp.wait_ge(cleared, 16 * H)
            sp.wait_ge(out_done, 32)

        @block.scalar
        def _(act):
            act.dma_start(w[:, :, 0:C], k.a["L0_gnn_W"].rearrange("(a p) c -> p a c", p=128)).then_inc(w_in, 16)
            for i, name in enumerate(("L0_gnn_att_src", "L0_gnn_att_dst")):
                act.dma_start(att[:, i, :], k.a[name].rearrange("(a h) d -> a (h d)", a=1).to_broadcast([128, C])).then_inc(att_in, 16)
            act.dma_start(k.res[:, :, :], k.a["x"].rearrange("(p t) c -> p t c", p=P)).then_inc(x_in, 16)
            norm_roots(k, act, deviations, roots)
            act.sem_inc(xt_made, TB)
            with act.Fori(0, NT // TB) as i:
                for s in range(TB):
                    act.wait_ge(xt_turned, i * TB + s + 1 + TB)
                    act.wait_ge(projected, i * TB + s + 1)
                    nc.scalar.copy(xt[:, s, :, :].rearrange("p a n -> p (a n)"), k.ps[s % 3][:, 0:2 * P]).then_inc(xt_made, 1)
            act.wait_ge(taken, NT + TB)
            act.dma_start(k.xh_tab.rearrange("(p t) c -> p t c", p=P), k.xh[:, :, 0:XW]).then_inc(out_done, 16)
            act.dma_start(k.adst_tab.rearrange("(p t) c -> p t c", p=P), k.xh[:, :, XW:RW]).then_inc(out_done, 16)

        @block.gpsimd
        def _(pool):
            me = st["pool"]
            nc.gpsimd.memset(srcq_i[:, :], 0).then_inc(padded, 1)
            nc.gpsimd.memset(dstq_i[:, :], N).then_inc(padded, 1)
            nc.gpsimd.memset(zeros[:, :], 0.0).then_inc(zeroed, 1)
            nc.gpsimd.memset(k.ones[:, :], 1.0)
            me(pool, nc.gpsimd.memset(k.ident[:, :], 0.0))
            nc.gpsimd.affine_select(out=k.ident[:, :], in_=k.ident[:, :], compare_op=ALU.not_equal, fill=1.0, base=0,
                                    pattern=[[-1, 128]], channel_multiplier=1)
            nc.gpsimd.iota(k.node[:, :], pattern=[[1, NT]], base=0, channel_multiplier=NT,
                           allow_small_or_imprecise_dtypes=True).then_inc(consts, 1)
            pool.wait_ge(tiles_found, 1)
            pool.wait_ge(pad_out, 16)
            for t in range(NT):
                pool.indirect_dma_start(out=window[:, t, :], out_offset=None, in_=k.dst_pad.rearrange("(a b) -> a b", b=EP),
                                        in_offset=bass.IndirectOffsetOnAxis(ap=tile_i[:, t:t + 1], axis=0)).then_inc(windows_in, 16)

        @block.tensor
        def _(pe):
            pe.wait_ge(edges_f, 4)
            pe.wait_ge(consts, 1)
            for b, t in enumerate((dstq, srcq, same, same)):
                for j in range(J):
                    at = j * EP + (b == 3)
                    last_mm = nc.tensor.transpose(k.ps[b][:, j * Q:(j + 1) * Q], t[:, at:at + EP], k.ident[0:Q, 0:Q])
                last_mm.then_inc(turned, 1)
            pe.wait_ge(ends_b, 1)
            nc.tensor.matmul(k.ps[4][:, 0:ET], k.ident[:, 0:1].to_broadcast([128, 128]), k.dst_e[:, :], start=True, stop=True).then_inc(turned, 1)
            nc.tensor.matmul(k.ps[5][:, 0:ET], k.ident[:, EP - 1:EP].to_broadcast([128, 128]), k.dst_e[:, :], start=True, stop=True).then_inc(turned, 1)
            pe.sem_inc(xt_turned, TB)
            pe.sem_inc(projected, TB)
            pe.wait_ge(w_ready, 1)
            pe.wait_ge(banks_read, 1)
            with pe.Fori(0, NT // TB) as i:
                for s in range(TB):
                    pe.wait_ge(xn_made, i * TB + s + 1)
                    pe.wait_ge(xt_made, i * TB + TB if s < 3 else i * TB + s - 2 + TB)
                    for c in range(2):
                        last_mm = nc.tensor.transpose(k.ps[s % 3][:, c * P:(c + 1) * P],
                                                      xn[:, s, c * 128:(c + 1) * 128], k.ident[0:P, 0:P])
                    last_mm.then_inc(xt_turned, 1)
                for s in range(TB):
                    pe.wait_ge(xt_made, i * TB + s + 1 + TB)
                    pe.wait_ge(taken, i * TB + s + 1)
                    for c in range(2):
                        last_mm = nc.tensor.matmul(k.ps[3 + s][0:P, 0:RW], xt[:, s, c, :], w[:, c, :], start=(c == 0), stop=(c == 1))
                    last_mm.then_inc(projected, 1)

        @block.vector
        def _(dve):
            me = st["dve"]
            v = nc.vector
            dve.wait_ge(edges_in, 64)
            v.tensor_copy(dstq[:, :], dstq_i[:, :]).then_inc(edges_f, 1)
            dve.wait_ge(edges_f, 1)
            v.tensor_copy(srcq[:, :], srcq_i[:, :]).then_inc(edges_f, 1)
            me(dve, v.tensor_tensor(same[:, 1:J * EP], dstq[:, 1:J * EP], dstq[:, 0:J * EP - 1], ALU.is_equal))
            me(dve, v.memset(same[:, 0:J * EP + 1:EP], 0.0))
            v.tensor_copy(k.cont_q[:, :], same[:, 0:J * EP])
            me(dve, v.tensor_scalar(k.tile_dst[:, :], dstq[:, 0:J * EP:EP], float(N - 1), None, ALU.min))
            v.tensor_scalar(same[:, :], same[:, :], -1.0, BIG, ALU.add, ALU.mult).then_inc(edges_f, 2)
            for b, t in enumerate((k.dst_e, k.src_e, k.fwd_e, k.bwd_e)):
                dve.wait_ge(turned, b + 1)
                me(dve, v.tensor_copy(t[:, :].rearrange("p (q j) -> p j q", j=J),
                                      k.ps[b][:, 0:ET].rearrange("p (j q) -> p j q", j=J)))
                if b == 0:
                    dve.sem_inc(ends_b, 1)
            dve.wait_ge(turned, 6)
            v.tensor_copy(first_b[:, :], k.ps[4][:, 0:ET])
            me(dve, v.tensor_copy(last_b[:, :], k.ps[5][:, 0:ET]))
            dve.sem_inc(banks_read, 1)
            me(dve, v.memset(k.joins[:, 0:1], 0.0))
            me(dve, v.tensor_tensor(k.joins[:, 1:ET], last_b[:, 1:ET], last_b[:, 0:ET - 1], ALU.is_equal))
            dve.wait_ge(consts, 1)
            with dve.Fori(0, NT) as t:
                v.tensor_scalar(tile_of(trash, t), first_b[0:P, :], k.node[:, bass.ds(t, 1)], None, ALU.is_lt, ALU.add,
                                accum_out=before[:, bass.ds(t, 1)])
            me(dve, v.memset(total[:, :], float(E)))
            me(dve, v.tensor_scalar(tile[:, :], before[:, :], -1.0, 0.0, ALU.add, ALU.max))
            v.tensor_copy(tile_i[:, :], tile[:, :]).then_inc(tiles_found, 1)
            dve.sem_inc(taken, TB)
            dve.wait_ge(w_in, 16)
            dve.wait_ge(att_in, 32)
            for i in range(2):
                me(dve, v.tensor_tensor(prod[:, :, :], w[:, :, 0:C], att[:, i:i + 1, :].to_broadcast([128, 2, C]), ALU.mult))
                me(dve, v.tensor_reduce(w[:, :, C + H * i:C + H * (i + 1)], prod[:, :, :].rearrange("p a (h d) -> p a h d", h=H), AX, ALU.add))
            dve.sem_inc(w_ready, 1)
            dve.wait_ge(x_in, 16)
            norm_stats(k, dve, deviations, roots)

            def norm_body(i):
                for s in range(TB):
                    t = i * TB + s
                    dve.wait_ge(xt_turned, i * TB + s + 1)
                    me(dve, v.tensor_scalar(xn[:, s, :], tile_of(k.res, t), k.mv[:, bass.ds(t, 1), 0:1].rearrange("p a c -> p (a c)"),
                                            k.rstd[:, bass.ds(t, 1)], ALU.subtract, ALU.mult))
                    v.tensor_tensor(tile_of(k.res, t), tile_of(k.res, t), xn[:, s, :], ALU.add).then_inc(xn_made, 1)

            def take_body(i):
                for s in range(TB):
                    dve.wait_ge(projected, i * TB + s + 1 + TB)
                    v.tensor_scalar(tile_of(k.xh, i * TB + s), k.ps[3 + s][0:P, 0:RW], 1.0, None, ALU.mult).then_inc(taken, 1)

            norm_body(0)
            with dve.Fori(0, NT // TB - 1) as i:
                me.loop(i, TB)
                norm_body(i + 1)
                take_body(i)
                me.end(NT // TB - 1)
            take_body(NT // TB - 1)
            dve.wait_ge(windows_in, 16 * NT)
            with dve.Fori(0, NT) as t:
                v.tensor_scalar(tile_of(trash, t)[:, 0:EP], tile_of(window, t), k.node[:, bass.ds(t, 1)], None,
                                ALU.is_lt, ALU.add, accum_out=before[:, bass.ds(t, 1)])
            me(dve, v.memset(mark[:, :], 0.0))
            v.scalar_tensor_tensor(out=start[:, :], in0=tile[:, :], scalar=float(EP), in1=before[:, :], op0=ALU.mult,
                                   op1=ALU.add).then_inc(starts_found, 1)
            dve.wait_ge(starts_found, 1)
            dve.wait_ge(ends_in, 16)
            me(dve, v.tensor_tensor(k.deg[:, :], end[:, :], start[:, :], ALU.subtract))
            v.tensor_scalar(has[:, :], k.deg[:, :], 0.0, None, ALU.is_gt)
            me(dve, v.tensor_scalar(last[:, :], end[:, :], -1.0, 0.0, ALU.add, ALU.max))
            me(dve, v.tensor_copy(last_i[:, :], last[:, :]))
            me(dve, v.tensor_single_scalar(tile_i[:, :], last_i[:, :], 7, ALU.logical_shift_right))
            me(dve, v.tensor_copy(tile[:, :], tile_i[:, :]))
            v.tensor_scalar(t0[:, :], last[:, :], -float(NO_ROW), None, ALU.add)
            me(dve, v.scalar_tensor_tensor(out=t1[:, :], in0=tile[:, :], scalar=float(EP), in1=start[:, :],
                                           op0=ALU.mult, op1=ALU.is_gt))
            v.tensor_tensor(t0[:, :], t0[:, :], has[:, :], ALU.mult)
            me(dve, v.tensor_tensor(t1[:, :], t1[:, :], has[:, :], ALU.mult))
            v.tensor_scalar(k.main_row[:, :], t0[:, :], float(NO_ROW), None, ALU.add)
            me(dve, v.tensor_scalar(tile[:, :], tile[:, :], -1.0 - NO_CHAIN, None, ALU.add))
            me(dve, v.tensor_tensor(t1[:, :], t1[:, :], tile[:, :], ALU.mult))
            v.tensor_scalar(k.chain_row[:, :], t1[:, :], float(NO_CHAIN), None, ALU.add)
            me(dve, v.tensor_scalar(t0[:, :], start[:, :], -float(NO_ROW + 1), None, ALU.add))
            me(dve, v.tensor_tensor(t0[:, :], t0[:, :], has[:, :], ALU.mult))
            me(dve, v.tensor_scalar(k.start_row[:, :], t0[:, :], float(NO_ROW + 1), None, ALU.add))


def norm_stats(k, dve, deviations, roots):
    v = k.nc.vector
    with dve.Fori(0, NT) as t:
        v.bn_stats(k.stats[:, bass.ds(t, 1), :].rearrange("p a s -> p (a s)"),
                   tile_of(k.res, t))
    norm_factors(k, dve, deviations, roots)


def norm_factors(k, dve, deviations, roots):
    v, me = k.nc.vector, k.steps["dve"]
    me(dve, v.memset(k.rstd[:, :], 0.0))
    even, odd, mean, var = k.stats[:, :, 1], k.stats[:, :, 4], k.mv[:, :, 0], k.mv[:, :, 1]
    v.tensor_tensor(mean, even, odd, ALU.add)
    v.tensor_tensor(var, even, odd, ALU.subtract)
    me(dve, v.tensor_tensor(k.rstd[:, :], k.stats[:, :, 2], k.stats[:, :, 5], ALU.add))
    v.tensor_scalar(mean, mean, 0.5, None, ALU.mult)
    v.tensor_scalar(k.rstd[:, :], k.rstd[:, :], 1.0 / C, EPS, ALU.mult, ALU.add)
    me(dve, v.tensor_tensor(var, var, var, ALU.mult))
    v.scalar_tensor_tensor(out=k.rstd[:, :], in0=var, scalar=0.25, in1=k.rstd[:, :], op0=ALU.mult, op1=ALU.add).then_inc(deviations, 1)
    dve.wait_ge(roots, 1)
    me(dve, v.reciprocal(k.rstd[:, :], k.rstd[:, :]))


def norm_roots(k, act, deviations, roots):
    act.wait_ge(deviations, 1)
    k.nc.scalar.activation(k.rstd[:, :], k.rstd[:, :], ACT.Sqrt).then_inc(roots, 1)


def spread_phase(k):
    nc, st = k.nc, k.steps
    ctx = ExitStack()
    with ctx:
        sb = lambda n, s, d=F32: k.sb(n, s, d, ctx)
        sparse = sb("sparse", [Q, J * EP * H])
        filled = sb("filled", [Q, J * EP * H])
        firsts = sb("firsts", [Q, J, H])
        firsts_in = k.gather_sem("firsts_in")
        starts_out, sparse_in = k.gather_sem("node_starts_out"), k.sem("sparse_in")
        spread, turned, taken = k.sem("spread"), k.sem("s_turned"), k.sem("s_taken")
        block = ctx.enter_context(nc.Block())
        edge_rows = k.adst_edge.rearrange("(q m) h -> q (m h)", q=Q)

        @block.sync
        def _(sp):
            sp.wait_ge(starts_out, 16 * NT)
            sp.dma_start(sparse[:, :], edge_rows).then_inc(sparse_in, 16)

        @block.gpsimd
        def _(pool):
            for t in range(NT):
                pool.indirect_dma_start(out=k.adst_edge, out_offset=bass.IndirectOffsetOnAxis(ap=k.start_row[:, t:t + 1], axis=0),
                                        in_=k.xh[:, t, XW:RW], in_offset=None, bounds_check=NO_ROW - 1, oob_is_err=False).then_inc(starts_out, 16)
            for j in range(J):
                pool.indirect_dma_start(out=firsts[:, j, :], out_offset=None, in_=k.adst_tab,
                                        in_offset=bass.IndirectOffsetOnAxis(ap=k.tile_dst[:, j:j + 1], axis=0)).then_inc(firsts_in, 16)
            for t in range(SB):
                pool.indirect_dma_start(out=k.slots[0][0][:, t, :], out_offset=None, in_=k.xh_tab,
                                        in_offset=bass.IndirectOffsetOnAxis(ap=k.src_e[:, t:t + 1], axis=0)).then_inc(k.slots[0][1], 16)

        @block.tensor
        def _(pe):
            pe.wait_ge(spread, H)
            for h in range(H):
                if h >= 4:
                    pe.wait_ge(taken, h - 3)
                for j in range(J):
                    m = nc.tensor.transpose(k.ps[h % 4][:, j * Q:(j + 1) * Q], filled[:, j * EP * H + h:(j + 1) * EP * H:H], k.ident[0:Q, 0:Q])
                m.then_inc(turned, 1)

        @block.scalar
        def _(act):
            for h in range(H):
                act.wait_ge(turned, h + 1)
                nc.scalar.copy(k.adst_e[:, :, h].rearrange("p (q j) -> p j q", j=J), k.ps[h % 4][:, 0:ET].rearrange("p (j q) -> p j q", j=J)).then_inc(taken, 1)

        @block.vector
        def _(dve):
            v = nc.vector
            dve.wait_ge(sparse_in, 16)
            dve.wait_ge(firsts_in, 16 * J)
            st["dve"](dve, v.tensor_copy(sparse[:, :].rearrange("q (j m) -> q j m", j=J)[:, :, 0:H], firsts[:, :, :]))
            for h in range(H):
                v.tensor_tensor_scan(filled[:, h::H], k.cont_q[:, :], sparse[:, h::H], 0.0, ALU.mult, ALU.add).then_inc(spread, 1)


R = 4


def rows_slots(k, name, width, slots, ctx):
    return [(k.sb(f"{name}_rows{s}", [EP, SB, width], F32, ctx), k.gather_sem(f"{name}_rows_in{s}")) for s in slots]


def edge_phase(k, name, table, weighted, here):
    nc, st = k.nc, k.steps
    ctx = ExitStack()
    sums_w = C + H if weighted else C
    out_w = RW if weighted else C
    BK = 7
    rows, rows_in = zip(*k.slots)
    with ctx:
        sb = lambda n, s, d=F32: k.sb(f"{name}_{n}", s, d, ctx)
        sem = lambda n: k.sem(f"{name}_{n}")
        ix = [sb(f"ix{s}", [EP, SB], I32) for s in range(R)]
        dstb = [sb(f"dstb{s}", [EP, SB * EP]) for s in range(2)]
        same = [sb(f"same{s}", [EP, SB, EP]) for s in range(2)]
        outs = [sb(f"outs{s}", [EP, SB, out_w]) for s in range(2)]
        if weighted:
            logit0, logit, shifted = (sb(n, [EP, SB, H]) for n in ("logit0", "logit", "shifted"))
            mask8 = sb("mask8", [EP, 2, SB, H])
            masks = sb("masks", [SB * H, 2 * EP])
            running, maxima = sb("running", [SB * H, EP]), sb("maxima", [SB * H, EP])
        outs_free = sem("outs_free")
        ix_made, issuing = sem("ix_made"), sem("issuing")
        dstb_in = [sem(f"dstb_in{s}") for s in range(2)]
        outs_out = [sem(f"outs_out{s}") for s in range(2)]
        same_made, logits_made, logits_turned, masks_in = sem("same_made"), sem("logits_made"), sem("logits_turned"), sem("masks_in")
        maxima_made, maxima_turned, maxima_in, less_max = sem("maxima_made"), sem("maxima_turned"), sem("maxima_in"), sem("less_max")
        weights_made, messages, sums, taken = sem("weights_made"), sem("messages"), sem("sums"), sem("taken")
        block = ctx.enter_context(nc.Block())

        @block.sync
        def _(sp):
            out_rows = k.parts[0:ET * EP, 0:out_w].rearrange("(b t e) c -> e b t c", t=SB, e=EP)
            dst_rows = k.dst_pad.rearrange("(b e) -> b e", b=NB)
            sp.sem_inc(outs_free, 2)

            def load(b, s, guarded=True):
                if guarded:
                    sp.wait_ge(same_made, b)
                sp.dma_start(dstb[s][:, :], dst_rows[bass.ds(b, 1), :].to_broadcast([EP, SB * EP])).then_inc(dstb_in[s], 16)

            def store(b, s, turn):
                sp.wait_ge(taken, b * SB + SB + BK)
                if weighted:
                    sp.wait_ge(maxima_in, b + 1)
                sp.dma_start(out_rows[:, bass.ds(b, 1), :, :].rearrange("e b t c -> e (b t) c"), outs[s][:, :, :]).then_inc(outs_out[s], 16)
                sp.wait_ge(outs_out[s], 16 * turn + 16)
                sp.sem_inc(outs_free, 1)

            load(0, 0, guarded=False)
            with sp.Fori(0, NB // 2 - 1) as i:
                load(i * 2 + 1, 1)
                store(i * 2, 0, i)
                load(i * 2 + 2, 0)
                store(i * 2 + 1, 1, i)
            load(NB - 1, 1)
            store(NB - 2, 0, NB // 2 - 1)
            store(NB - 1, 1, NB // 2 - 1)

        @block.gpsimd
        def _(pool):
            def gather(b, s):
                pool.wait_ge(sums, b * SB + SB)
                nc.gpsimd.tensor_copy(ix[s][:, :], k.src_e[:, bass.ds(b * SB, SB)]).then_inc(ix_made, 1)
                pool.wait_ge(ix_made, b + 1 - here)
                pool.sem_inc(issuing, 1)
                for t in range(SB):
                    pool.indirect_dma_start(out=rows[s][:, t, :], out_offset=None, in_=table,
                                            in_offset=bass.IndirectOffsetOnAxis(ap=ix[s][:, t:t + 1], axis=0)).then_inc(rows_in[s], 16)

            for s in range(here, R):
                gather(s, s)
            with pool.Fori(1, NB // R) as i:
                for s in range(R):
                    gather(i * R + s, s)

        @block.vector
        def _(dve):
            v, me = nc.vector, st["dve"]
            dve.sem_inc(same_made, 1)
            with dve.Fori(0, NB // R) as i:
                if weighted:
                    me.loop(i, 2 * R)
                for s in range(R):
                    b = i * R + s
                    dve.wait_ge(dstb_in[s % 2], 16 * (R // 2) * i + 16 * (s // 2) + 16)
                    dve.wait_ge(sums, b * SB + SB * (R - 1))
                    v.tensor_tensor(same[s % 2][:, :, :], dstb[s % 2][:, :].rearrange("p (t e) -> p t e", t=SB),
                                    k.dst_e[:, bass.ds(b * SB, SB)].rearrange("p (t a) -> p t a", a=1).to_broadcast([EP, SB, EP]),
                                    ALU.is_equal).then_inc(same_made, 1)
                    if not weighted:
                        continue
                    for m, mask in enumerate((k.fwd_e, k.bwd_e)):
                        v.tensor_scalar(mask8[:, m, :, :], mask[:, bass.ds(b * SB, SB)].rearrange("p (t a) -> p t a", a=1).to_broadcast([EP, SB, H]),
                                        1.0, None, ALU.mult)
                    dve.wait_ge(rows_in[s], 16 * SB * i + 16 * SB)
                    me(dve, v.tensor_tensor(logit0[:, :, :], rows[s][:, :, C:C + H], k.adst_e[:, bass.ds(b * SB, SB), :], ALU.add))
                    v.scalar_tensor_tensor(out=logit[:, :, :], in0=logit0[:, :, :], scalar=0.2, in1=logit0[:, :, :], op0=ALU.mult, op1=ALU.max).then_inc(logits_made, 1)
                    dve.wait_ge(masks_in, b + 1)
                    me(dve, v.tensor_tensor_scan(running[:, :], masks[:, 0:EP], k.ps[0][0:SB * H, 0:EP], -BIG, ALU.add, ALU.max))
                    v.tensor_tensor_scan(maxima[:, ::-1], masks[:, EP:2 * EP][:, ::-1], running[:, ::-1], -BIG, ALU.add, ALU.max).then_inc(maxima_made, 1)
                    dve.wait_ge(maxima_in, b + 1)
                    v.tensor_tensor(shifted[:, :, :], logit[:, :, :], outs[s % 2][:, :, C + H:RW], ALU.subtract).then_inc(less_max, 1)
                    dve.wait_ge(weights_made, b + 2)
                    for half in range(2):
                        t0, t1 = half * SB // 2, (half + 1) * SB // 2
                        f = rows[s][:, t0:t1, 0:C].rearrange("p t (h d) -> p t h d", h=H)
                        v.tensor_tensor(f, f, rows[s][:, t0:t1, C:C + H].rearrange("p t (h a) -> p t h a", a=1).to_broadcast([EP, SB // 2, H, D]),
                                        ALU.mult).then_inc(messages, 1)
                if weighted:
                    me.end(NB // R)

        @block.tensor
        def _(pe):
            pe.sem_inc(sums, R * SB)
            with pe.Fori(0, NB // R) as i:
                for s in range(R):
                    b = i * R + s
                    if weighted:
                        pe.wait_ge(logits_made, b + 1)
                        pe.wait_ge(weights_made, b + 1)
                        nc.tensor.transpose(k.ps[0][0:SB * H, 0:EP], logit[:, :, :].rearrange("p t h -> p (t h)"), k.ident[:, :])
                        for m in range(2):
                            mm = nc.tensor.transpose(k.ps[0][0:SB * H, EP * (m + 1):EP * (m + 2)], mask8[:, m, :, :].rearrange("p t h -> p (t h)"), k.ident[:, :])
                        mm.then_inc(logits_turned, 1)
                        pe.wait_ge(maxima_made, b + 1)
                        nc.tensor.transpose(k.ps[0][:, 384:384 + SB * H], maxima[:, :], k.ident[0:SB * H, 0:SB * H]).then_inc(maxima_turned, 1)
                    pe.wait_ge(same_made, b + 2)
                    if not weighted:
                        pe.wait_ge(rows_in[s], 16 * SB * i + 16 * SB)
                    for t in range(SB):
                        if weighted and t % (SB // 2) == 0:
                            pe.wait_ge(messages, 2 * b + 1 + 2 * t // SB)
                        pe.wait_ge(taken, b * SB + t + 1)
                        nc.tensor.matmul(k.ps[1 + t % BK][:, 0:sums_w], same[s % 2][:, t, :], rows[s][:, t, 0:sums_w],
                                         start=True, stop=True).then_inc(sums, 1)

        @block.scalar
        def _(act):
            act.sem_inc(taken, BK)
            act.sem_inc(weights_made, 1)
            with act.Fori(0, NB // R) as i:
                for s in range(R):
                    b = i * R + s
                    act.wait_ge(outs_free, b + 1)
                    if weighted:
                        act.wait_ge(logits_turned, b + 1)
                        nc.scalar.copy(masks[:, :], k.ps[0][0:SB * H, EP:3 * EP]).then_inc(masks_in, 1)
                        act.wait_ge(maxima_turned, b + 1)
                        nc.scalar.copy(outs[s % 2][:, :, C + H:RW], k.ps[0][:, 384:384 + SB * H].rearrange("p (t h) -> p t h", h=H)).then_inc(maxima_in, 1)
                        act.wait_ge(less_max, b + 1)
                        nc.scalar.activation(rows[s][:, :, C:C + H], shifted[:, :, :], ACT.Exp).then_inc(weights_made, 1)
                    for t in range(SB):
                        act.wait_ge(sums, b * SB + t + 1 + R * SB)
                        nc.scalar.copy(outs[s % 2][:, t, 0:sums_w], k.ps[1 + t % BK][:, 0:sums_w]).then_inc(taken, 1)


def gather_rows(pool, into, table, row, rows_in):
    for t in range(NT):
        pool.indirect_dma_start(out=into[:, t, :], out_offset=None, in_=table,
                                in_offset=bass.IndirectOffsetOnAxis(ap=row[:, t:t + 1], axis=0)).then_inc(rows_in, 16)


def chain_phase(k, name, weighted):
    nc, st = k.nc, k.steps
    ctx = ExitStack()
    w = RW if weighted else C
    with ctx:
        sb = lambda n, s, d=F32: k.sb(f"{name}c_{n}", s, d, ctx)
        sem = lambda n: k.sem(f"{name}c_{n}")
        lasts, carried = sb("lasts", [Q, J, w]), sb("carried", [Q, J, w])
        last_t = [sb(f"last_t{c}", [128, ET]) for c in range(2)]
        sum_t = [sb(f"sum_t{c}", [128, ET]) for c in range(2)]
        dummy = sb("dummy", [1, RW])
        if weighted:
            den_t, max_t, den_c, max_c, neg, keep, scale = (sb(n, [H, ET]) for n in ("den_t", "max_t", "den_c", "max_c", "neg", "keep", "scale"))
            sel = sb("sel", [H, C])
        lasts_in, dummies, sel_made, turned = sem("lasts_in"), sem("dummies"), sem("sel_made"), sem("turned")
        dummies_out = sem("dummies_out")
        drops, factors, spread, scanned, back, rows_made, stored = (sem(n) for n in ("drops", "factors", "spread", "scanned", "back", "rows_made", "stored"))
        block = ctx.enter_context(nc.Block())

        @block.sync
        def _(sp):
            if weighted:
                sp.wait_ge(dummies, 1)
                sp.dma_start(k.parts[NO_ROW:NO_ROW + 1, :], dummy[:, :]).then_inc(dummies_out, 16)
                sp.dma_start(k.chains[NO_CHAIN:NO_CHAIN + 1, :], dummy[:, :]).then_inc(dummies_out, 16)
            sp.dma_start(lasts[:, :, :], k.parts[0:ET * EP, :].rearrange("(q j e) c -> q j e c", q=Q, j=J)[:, :, EP - 1, 0:w]).then_inc(lasts_in, 16)
            if weighted:
                sp.dma_start(k.xh[:, :, 0:XW], k.xh_tab.rearrange("(p t) c -> p t c", p=P)).then_inc(stored, 16)
                sp.dma_start(k.xh[:, :, XW:RW], k.adst_tab.rearrange("(p t) c -> p t c", p=P)).then_inc(stored, 16)
            sp.wait_ge(rows_made, 1)
            sp.dma_start(k.chains[0:ET, 0:w].rearrange("(q j) c -> q j c", j=J), carried[:, :, :]).then_inc(stored, 16)
            sp.wait_ge(stored, 48 if weighted else 16)

        @block.gpsimd
        def _(pool):
            if weighted:
                me = st["pool"]
                nc.gpsimd.memset(dummy[:, 0:C + H], 0.0)
                me(pool, nc.gpsimd.memset(dummy[:, C + H:RW], -BIG))
                pool.sem_inc(dummies, 1)
                me(pool, nc.gpsimd.memset(sel[:, :], 1.0))
                me(pool, nc.gpsimd.affine_select(out=sel[:, :], in_=sel[:, :], compare_op=ALU.is_ge, fill=0.0, base=0,
                                                 pattern=[[1, C]], channel_multiplier=-D))
                nc.gpsimd.affine_select(out=sel[:, :], in_=sel[:, :], compare_op=ALU.is_ge, fill=0.0, base=D - 1,
                                        pattern=[[-1, C]], channel_multiplier=D).then_inc(sel_made, 1)
                pool.wait_ge(dummies_out, 32)
            gather_rows(pool, k.mains, k.parts[:, :], k.main_row, k.mains_in)

        @block.tensor
        def _(pe):
            pe.wait_ge(lasts_in, 16)
            for c in range(2):
                for j in range(J):
                    m = nc.tensor.transpose(k.ps[c][:, j * Q:(j + 1) * Q], lasts[:, j, c * 128:(c + 1) * 128], k.ident[0:Q, 0:Q])
                m.then_inc(turned, 1)
            if weighted:
                for c in range(2):
                    for j in range(J):
                        m = nc.tensor.transpose(k.ps[2 + c][0:H, j * Q:(j + 1) * Q], lasts[:, j, C + c * H:C + (c + 1) * H], k.ident[0:Q, 0:Q])
                    m.then_inc(turned, 1)
                pe.wait_ge(sel_made, 1)
                pe.wait_ge(factors, 3)
                for c in range(2):
                    nc.tensor.matmul(k.ps[4 + c][:, 0:ET], sel[:, c * 128:(c + 1) * 128], keep[:, :], start=True, stop=True)
                    nc.tensor.matmul(k.ps[6 + c][:, 0:ET], sel[:, c * 128:(c + 1) * 128], scale[:, :], start=True, stop=True).then_inc(spread, 1)
            pe.wait_ge(scanned, 3 if weighted else 2)
            for c in range(2):
                for j in range(J):
                    m = nc.tensor.transpose(k.ps[c][0:Q, j * 128:(j + 1) * 128], sum_t[c][:, j:ET:J], k.ident[:, :])
                m.then_inc(back, 1)
            if weighted:
                for c, t in enumerate((den_c, max_c)):
                    for j in range(J):
                        m = nc.tensor.transpose(k.ps[2 + c][0:Q, j * H:(j + 1) * H], t[:, j:ET:J], k.ident[0:H, 0:H])
                    m.then_inc(back, 1)

        @block.scalar
        def _(act):
            if weighted:
                act.wait_ge(drops, 1)
                nc.scalar.activation(keep[:, :], keep[:, :], ACT.Exp).then_inc(factors, 1)
                nc.scalar.activation(scale[:, :], scale[:, :], ACT.Exp).then_inc(factors, 1)

        @block.vector
        def _(dve):
            v, me = nc.vector, st["dve"]

            def lay(dst, bank, parts):
                me(dve, v.tensor_copy(dst[:, :].rearrange("p (q j) -> p j q", j=J), k.ps[bank][0:parts, 0:ET].rearrange("p (j q) -> p j q", j=J)))

            for c in range(2):
                dve.wait_ge(turned, c + 1)
                lay(last_t[c], c, 128)
            if weighted:
                dve.wait_ge(turned, 4)
                lay(den_t, 2, H)
                lay(max_t, 3, H)
                me(dve, v.tensor_scalar(neg[:, :], k.joins[0:H, :], -1.0, BIG, ALU.add, ALU.mult))
                me(dve, v.tensor_tensor_scan(max_c[:, :], neg[:, :], max_t[:, :], -BIG, ALU.add, ALU.max))
                v.memset(keep[:, 0:1], 0.0)
                me(dve, v.tensor_tensor(keep[:, 1:ET], max_c[:, 0:ET - 1], max_c[:, 1:ET], ALU.subtract))
                me(dve, v.tensor_tensor(keep[:, :], keep[:, :], k.joins[0:H, :], ALU.mult))
                v.tensor_tensor(scale[:, :], max_t[:, :], max_c[:, :], ALU.subtract).then_inc(drops, 1)
                dve.wait_ge(factors, 2)
                v.tensor_tensor(keep[:, :], keep[:, :], k.joins[0:H, :], ALU.mult).then_inc(factors, 1)
                me(dve, v.tensor_tensor(den_t[:, :], den_t[:, :], scale[:, :], ALU.mult))
                v.tensor_tensor_scan(den_c[:, :], keep[:, :], den_t[:, :], 0.0, ALU.mult, ALU.add).then_inc(scanned, 1)
                for c in range(2):
                    dve.wait_ge(spread, c + 1)
                    me(dve, v.tensor_tensor(last_t[c][:, :], last_t[c][:, :], k.ps[6 + c][:, 0:ET], ALU.mult))
                    v.tensor_tensor_scan(sum_t[c][:, :], k.ps[4 + c][:, 0:ET], last_t[c][:, :], 0.0, ALU.mult, ALU.add).then_inc(scanned, 1)
            else:
                for c in range(2):
                    v.tensor_tensor_scan(sum_t[c][:, :], k.joins[:, :], last_t[c][:, :], 0.0, ALU.mult, ALU.add).then_inc(scanned, 1)
            for c in range(2):
                dve.wait_ge(back, c + 1)
                me(dve, v.tensor_copy(carried[:, :, c * 128:(c + 1) * 128], k.ps[c][0:Q, :].rearrange("p (j c) -> p j c", j=J)))
            if weighted:
                for c in range(2):
                    dve.wait_ge(back, c + 3)
                    me(dve, v.tensor_copy(carried[:, :, C + c * H:C + (c + 1) * H], k.ps[2 + c][0:Q, 0:J * H].rearrange("p (j h) -> p j h", j=J)))
            dve.sem_inc(rows_made, 1)


def gat_node_phase(k):
    nc, st = k.nc, k.steps
    ctx = ExitStack()
    BODIES = NT // TB
    with ctx:
        sb = lambda n, s, d=F32: k.sb(f"gn_{n}", s, d, ctx)
        sem = lambda n: k.sem(f"gn_{n}")
        main = k.mains
        chain = sb("chain", [P, NT, RW])
        own0, own = sb("own0", [P, NT, H]), sb("own", [P, NT, H])
        top, tmp = sb("top", [P, NT, H]), sb("tmp", [P, NT, H])
        den = sb("den", [P, NT, H])
        wt = sb("wt", [P, 3, NT, H])
        rowv = sb("rowv", [P, 3, C])
        mean, var = sb("mean", [P, C]), sb("var", [P, C])
        chains_in = k.gather_sem("gn_chains_in")
        vecs_in, gaps, weights, weights_made, own_made, joined, summed, centred, squared, dev, root = (
            sem(n) for n in ("vecs_in", "gaps", "weights", "weights_made", "own_made", "joined", "summed", "centred", "squared", "dev", "root"))
        block = ctx.enter_context(nc.Block())
        sq = chain

        @block.sync
        def _(sp):
            for i, name in enumerate(("L0_gnn_bias", "L0_gnn_gamma", "L0_gnn_beta")):
                sp.dma_start(rowv[:, i, :], k.a[name].rearrange("(a c) -> a c", a=1).to_broadcast([P, C])).then_inc(vecs_in, 16)

        @block.gpsimd
        def _(pool):
            gather_rows(pool, chain, k.chains[:, :], k.chain_row, chains_in)
            pool.wait_ge(vecs_in, 48)
            pool.wait_ge(weights_made, 1)
            for i in range(BODIES):
                tiles = slice(i * TB, (i + 1) * TB)
                node = k.xh[:, tiles, 0:C]
                heads = node.rearrange("p t (h d) -> p t h d", h=H)
                st["pool"](pool, nc.gpsimd.tensor_tensor(heads, heads, wt[:, 2, tiles, :].rearrange("p t (h a) -> p t h a", a=1).to_broadcast([P, TB, H, D]), ALU.mult))
                nc.gpsimd.tensor_tensor(node, node, rowv[:, 0:1, :].to_broadcast([P, TB, C]), ALU.add).then_inc(own_made, 1)

        @block.scalar
        def _(act):
            act.wait_ge(gaps, 1)
            nc.scalar.activation(wt[:, :, :, :], wt[:, :, :, :], ACT.Exp).then_inc(weights, 1)
            for i in range(BODIES):
                act.wait_ge(centred, i + 1)
                nc.scalar.activation(sq[:, i * TB:(i + 1) * TB, 0:C], k.xh[:, i * TB:(i + 1) * TB, 0:C], ACT.Square).then_inc(squared, 1)
            act.wait_ge(dev, 1)
            nc.scalar.activation(var[:, :], var[:, :], ACT.Sqrt).then_inc(root, 1)

        @block.tensor
        def _(pe):
            for bank, made, tile in ((k.ps[0], joined, k.xh), (k.ps[1], squared, sq)):
                for t in range(NT):
                    if t % TB == 0:
                        pe.wait_ge(made, t // TB + 1)
                    m = nc.tensor.matmul(bank[0:P, 0:C], k.ones[0:P, 0:P], tile[:, t, 0:C], start=(t == 0), stop=(t == NT - 1))
                m.then_inc(summed, 1)

        @block.vector
        def _(dve):
            v, me = nc.vector, st["dve"]
            me(dve, v.tensor_tensor(own0[:, :, :], k.xh[:, :, C:C + H], k.xh[:, :, C + H:RW], ALU.add))
            me(dve, v.scalar_tensor_tensor(out=own[:, :, :], in0=own0[:, :, :], scalar=0.2, in1=own0[:, :, :], op0=ALU.mult, op1=ALU.max))
            m1, m2 = main[:, :, C + H:RW], chain[:, :, C + H:RW]
            dve.wait_ge(k.mains_in, 16 * NT)
            me(dve, v.tensor_tensor(tmp[:, :, :], m1, own[:, :, :], ALU.max))
            dve.wait_ge(chains_in, 16 * NT)
            me(dve, v.tensor_tensor(top[:, :, :], tmp[:, :, :], m2, ALU.max))
            v.tensor_tensor(wt[:, 0, :, :], m1, top[:, :, :], ALU.subtract)
            v.tensor_tensor(wt[:, 1, :, :], m2, top[:, :, :], ALU.subtract)
            v.tensor_tensor(wt[:, 2, :, :], own[:, :, :], top[:, :, :], ALU.subtract).then_inc(gaps, 1)
            dve.wait_ge(weights, 1)
            v.tensor_tensor(den[:, :, :], wt[:, 0, :, :], main[:, :, C:C + H], ALU.mult)
            me(dve, v.tensor_tensor(tmp[:, :, :], wt[:, 1, :, :], chain[:, :, C:C + H], ALU.mult))
            me(dve, v.tensor_tensor(den[:, :, :], den[:, :, :], tmp[:, :, :], ALU.add))
            me(dve, v.tensor_tensor(den[:, :, :], den[:, :, :], wt[:, 2, :, :], ALU.add))
            me(dve, v.reciprocal(den[:, :, :], den[:, :, :]))
            me(dve, v.tensor_tensor(wt[:, :, :, :], wt[:, :, :, :], den[:, :, :].rearrange("p (a t) h -> p a t h", a=1).to_broadcast([P, 3, NT, H]), ALU.mult))
            dve.sem_inc(weights_made, 1)
            with dve.Fori(0, BODIES) as i:
                me.loop(i, 2)
                tiles = bass.ds(i * TB, TB)
                for j, a in enumerate((main[:, tiles, 0:C], chain[:, tiles, 0:C])):
                    a = a.rearrange("p t (h d) -> p t h d", h=H)
                    m = v.tensor_tensor(a, a, wt[:, j, tiles, :].rearrange("p t (h a) -> p t h a", a=1).to_broadcast([P, TB, H, D]), ALU.mult)
                me(dve, m)
                me(dve, v.tensor_tensor(main[:, tiles, 0:C], main[:, tiles, 0:C], chain[:, tiles, 0:C], ALU.add))
                dve.wait_ge(own_made, i + 1)
                v.tensor_tensor(k.xh[:, tiles, 0:C], k.xh[:, tiles, 0:C], main[:, tiles, 0:C], ALU.add).then_inc(joined, 1)
                me.end(BODIES)
            dve.wait_ge(vecs_in, 48)
            me(dve, v.tensor_tensor(k.res[:, :, :], k.res[:, :, :], rowv[:, 2:3, :].to_broadcast([P, NT, C]), ALU.add))
            dve.wait_ge(summed, 1)
            me(dve, v.tensor_scalar(mean[:, :], k.ps[0][0:P, 0:C], 1.0 / N, None, ALU.mult))

            def over(row):
                return row.rearrange("p (a c) -> p a c", a=1).to_broadcast([P, TB, C])

            for i in range(BODIES):
                feat = k.xh[:, i * TB:(i + 1) * TB, 0:C]
                v.tensor_tensor(feat, feat, over(mean[:, :]), ALU.subtract).then_inc(centred, 1)
            dve.wait_ge(summed, 2)
            v.tensor_scalar(var[:, :], k.ps[1][0:P, 0:C], 1.0 / N, EPS, ALU.mult, ALU.add).then_inc(dev, 1)
            dve.wait_ge(root, 1)
            me(dve, v.reciprocal(var[:, :], var[:, :]))
            me(dve, v.tensor_tensor(var[:, :], var[:, :], rowv[:, 1, :], ALU.mult))
            for i in range(BODIES):
                tiles = slice(i * TB, (i + 1) * TB)
                feat = k.xh[:, tiles, 0:C]
                me(dve, v.tensor_tensor(feat, feat, over(var[:, :]), ALU.mult))
                m = v.tensor_tensor(k.res[:, tiles, :], k.res[:, tiles, :], feat, ALU.add)
            me(dve, m)


class Turning:

    def __init__(self, k, name, ctx):
        self.k = k
        self.xn = k.sb(f"{name}_xn", [P, TB, C], F32, ctx)
        self.xt = k.sb(f"{name}_xt", [128, TB, 2, P], F32, ctx)
        self.made, self.turned, self.kept, self.multiplied, self.taken = (
            k.sem(f"{name}_{n}") for n in ("made", "turned", "kept", "multiplied", "taken"))

    def on_tensor(self, pe, multiply):
        pe.sem_inc(self.turned, TB)
        pe.sem_inc(self.multiplied, TB)
        with pe.Fori(0, NT // TB) as i:
            for s in range(TB):
                pe.wait_ge(self.made, i * TB + s + 1)
                pe.wait_ge(self.kept, i * TB + TB if s < 3 else i * TB + s - 2 + TB)
                for c in range(2):
                    m = self.k.nc.tensor.transpose(self.k.ps[s % 3][:, c * P:(c + 1) * P], self.xn[:, s, c * 128:(c + 1) * 128], self.k.ident[0:P, 0:P])
                m.then_inc(self.turned, 1)
            for s in range(TB):
                pe.wait_ge(self.kept, i * TB + s + 1 + TB)
                pe.wait_ge(self.taken, i * TB + s + 1)
                multiply(s).then_inc(self.multiplied, 1)

    def on_scalar(self, act):
        act.sem_inc(self.kept, TB)
        with act.Fori(0, NT // TB) as i:
            for s in range(TB):
                act.wait_ge(self.turned, i * TB + s + 1 + TB)
                act.wait_ge(self.multiplied, i * TB + s + 1)
                self.k.nc.scalar.copy(self.xt[:, s, :, :].rearrange("p a n -> p (a n)"), self.k.ps[s % 3][:, 0:2 * P]).then_inc(self.kept, 1)

    def on_vector(self, dve, fill, take, steps=0, after=None):
        me, bodies = self.k.steps["dve"], NT // TB

        def fill_body(i):
            for s in range(TB):
                dve.wait_ge(self.turned, i * TB + s + 1)
                fill(i * TB + s, s).then_inc(self.made, 1)

        def take_body(i):
            for s in range(TB):
                dve.wait_ge(self.multiplied, i * TB + s + 1 + TB)
                take(i * TB + s, s).then_inc(self.taken, 1)
            if after is not None:
                dve.wait_ge(self.taken, i * TB + 2 * TB)
                for s in range(TB):
                    after(i * TB + s)

        dve.sem_inc(self.taken, TB)
        fill_body(0)
        with dve.Fori(0, bodies - 1) as i:
            me.loop(i, steps)
            fill_body(i + 1)
            take_body(i)
            me.end(bodies - 1)
        take_body(bodies - 1)


def normed(k, out, t):
    return k.nc.vector.tensor_scalar(out, tile_of(k.res, t), k.mv[:, bass.ds(t, 1), 0:1].rearrange("p a c -> p (a c)"),
                                     k.rstd[:, bass.ds(t, 1)], ALU.subtract, ALU.mult)


NE, HID = 8, 682
M = 128
NI = (2 * N + NE * (M - 1)) // M
HB = (0, HID // 4 * 2 + 2, HID)
HW = HB[1]


def router_phase(k):
    nc, st = k.nc, k.steps
    ctx = ExitStack()
    with ctx:
        sb = lambda n, s, d=F32: k.sb(f"r_{n}", s, d, ctx)
        sem = lambda n: k.sem(f"r_{n}")
        q = Turning(k, "r", ctx)
        rw, rwt = sb("rw", [NE, C]), sb("rwt", [128, 2, NE])
        xn1 = sb("xn1", [P, NT, C])
        prob, rest, hit, cand = (sb(n, [P, NT, NE]) for n in ("prob", "rest", "hit", "cand"))
        oh = sb("oh", [P, 2, NT, NE])
        both, tot, inc, slot = (sb(n, [P, NT, NE]) for n in ("both", "tot", "inc", "slot"))
        expert, item, lane = sb("expert", [P, NE]), sb("item", [P, NI]), sb("lane", [P, M])
        peak, idx, den = sb("peak", [P, NT]), sb("idx", [P, NT]), sb("den", [P, NT])
        tiles, tiles_i, ends, begins = sb("tiles", [P, NE]), sb("tiles_i", [P, NE], I32), sb("ends", [P, NE]), sb("begins", [P, NE])
        pos, hi, lo = sb("pos", [P, 2, NT]), sb("hi", [P, 2, NT]), sb("lo", [P, 2, NT])
        hi_i = sb("hi_i", [P, 2, NT], I32)
        before = sb("before", [P, P])
        at_lane, at_item = sb("at_lane", [P, 2 * NT, M]), sb("at_item", [P, 2 * NT, NI])
        over = sb("over", [P, NI, NE])
        of_item = sb("of_item", [P, NI])
        rw_in, rw_turned, rw_ready, deviations, roots = (sem(n) for n in ("rw_in", "rw_turned", "rw_ready", "deviations", "roots"))
        logits_done, xn_out, less_peak, exped, chosen, counted, places, tokens = (sem(n) for n in ("logits_done", "xn_out", "less_peak", "exped", "chosen", "counted", "places", "tokens"))
        iotas = sem("iotas")
        block = ctx.enter_context(nc.Block())

        @block.sync
        def _(sp):
            sp.dma_start(rw[:, :], k.a["L0_ffn_router_w"]).then_inc(rw_in, 16)
            sp.dma_start(k.x1_tab.rearrange("(p t) c -> p t c", p=P), k.res[:, :, :]).then_inc(xn_out, 16)
            sp.wait_ge(logits_done, 1)
            sp.dma_start(k.xn_tab.rearrange("(p t) c -> p t c", p=P), xn1[:, :, :]).then_inc(xn_out, 16)
            sp.wait_ge(xn_out, 32)

        @block.gpsimd
        def _(pool):
            me = st["pool"]
            nc.gpsimd.iota(expert[:, :], pattern=[[1, NE]], base=0, channel_multiplier=0, allow_small_or_imprecise_dtypes=True)
            nc.gpsimd.iota(item[:, :], pattern=[[1, NI]], base=0, channel_multiplier=0, allow_small_or_imprecise_dtypes=True)
            nc.gpsimd.iota(lane[:, :], pattern=[[1, M]], base=0, channel_multiplier=0, allow_small_or_imprecise_dtypes=True)
            me(pool, nc.gpsimd.memset(before[:, :], 1.0))
            nc.gpsimd.affine_select(out=before[:, :], in_=before[:, :], compare_op=ALU.is_ge, fill=0.0, base=-1,
                                    pattern=[[1, P]], channel_multiplier=-1).then_inc(iotas, 1)

        @block.tensor
        def _(pe):
            pe.wait_ge(rw_in, 16)
            for c in range(2):
                m = nc.tensor.transpose(k.ps[0][:, c * NE:(c + 1) * NE], rw[:, c * 128:(c + 1) * 128], k.ident[0:NE, 0:NE])
            m.then_inc(rw_turned, 1)
            pe.wait_ge(rw_ready, 1)

            def multiply(s):
                for c in range(2):
                    m = nc.tensor.matmul(k.ps[3 + s][0:P, 0:NE], q.xt[:, s, c, :], rwt[:, c, :], start=(c == 0), stop=(c == 1))
                return m

            q.on_tensor(pe, multiply)
            pe.wait_ge(iotas, 1)
            pe.wait_ge(chosen, 1)
            flat = both[:, :, :].rearrange("p t e -> p (t e)")
            nc.tensor.matmul(k.ps[0][0:P, 0:NT * NE], before[:, :], flat, start=True, stop=True)
            nc.tensor.matmul(k.ps[1][0:P, 0:NT * NE], k.ones[0:P, 0:P], flat, start=True, stop=True).then_inc(counted, 1)
            pe.wait_ge(places, 1)
            for j in range(2 * NT):
                m = nc.tensor.matmul(k.ps[2][:, 0:NI], at_lane[:, j, :], at_item[:, j, :], start=(j == 0), stop=(j == 2 * NT - 1))
            m.then_inc(tokens, 1)

        @block.scalar
        def _(act):
            norm_roots(k, act, deviations, roots)
            q.on_scalar(act)
            act.wait_ge(less_peak, 1)
            nc.scalar.activation(prob[:, :, :], prob[:, :, :], ACT.Exp).then_inc(exped, 1)

        @block.vector
        def _(dve):
            v, me = nc.vector, st["dve"]

            def wide(a):
                return a[:, :].rearrange("p (t a) -> p t a", a=1).to_broadcast([P, NT, NE])

            def long(a):
                return a[:, :].rearrange("p (a e) -> p a e", a=1).to_broadcast([P, NT, NE])

            dve.wait_ge(rw_turned, 1)
            v.tensor_copy(rwt[:, :, :], k.ps[0][:, 0:2 * NE].rearrange("p (a e) -> p a e", a=2)).then_inc(rw_ready, 1)
            norm_stats(k, dve, deviations, roots)

            def fill(t, s):
                me(dve, normed(k, q.xn[:, s, :], t))
                return v.tensor_scalar(tile_of(xn1, t), q.xn[:, s, :], 1.0, None, ALU.mult)

            def take(t, s):
                return v.tensor_scalar(tile_of(prob, t), k.ps[3 + s][0:P, 0:NE], 1.0, None, ALU.mult)

            q.on_vector(dve, fill, take, TB)
            me(dve, v.tensor_copy(den[:, :], k.rstd[:, :]))
            dve.sem_inc(logits_done, 1)
            me(dve, v.tensor_reduce(peak[:, :], prob[:, :, :], AX, ALU.max))
            v.tensor_tensor(prob[:, :, :], prob[:, :, :], wide(peak), ALU.subtract).then_inc(less_peak, 1)
            dve.wait_ge(exped, 1)
            me(dve, v.tensor_reduce(den[:, :], prob[:, :, :], AX, ALU.add))
            me(dve, v.reciprocal(den[:, :], den[:, :]))
            me(dve, v.tensor_tensor(prob[:, :, :], prob[:, :, :], wide(den), ALU.mult))
            dve.wait_ge(iotas, 1)
            v.tensor_copy(rest[:, :, :], prob[:, :, :])
            me(dve, v.tensor_scalar(tiles[:, :], expert[:, :], -float(NE), None, ALU.add))
            for j in range(2):
                me(dve, v.tensor_reduce(k.gate[:, j, :], rest[:, :, :], AX, ALU.max))
                me(dve, v.tensor_tensor(hit[:, :, :], rest[:, :, :], wide(k.gate[:, j, :]), ALU.is_equal))
                me(dve, v.tensor_tensor(cand[:, :, :], hit[:, :, :], long(tiles), ALU.mult))
                me(dve, v.tensor_reduce(idx[:, :], cand[:, :, :], AX, ALU.min))
                me(dve, v.tensor_scalar(idx[:, :], idx[:, :], float(NE), None, ALU.add))
                me(dve, v.tensor_tensor(oh[:, j, :, :], wide(idx), long(expert), ALU.is_equal))
                if j == 0:
                    me(dve, v.scalar_tensor_tensor(out=rest[:, :, :], in0=oh[:, 0, :, :], scalar=-2.0, in1=rest[:, :, :], op0=ALU.mult, op1=ALU.add))
            me(dve, v.tensor_tensor(both[:, :, :], oh[:, 0, :, :], oh[:, 1, :, :], ALU.add))
            dve.sem_inc(chosen, 1)
            me(dve, v.scalar_tensor_tensor(out=den[:, :], in0=k.gate[:, 0, :], scalar=1e-9, in1=k.gate[:, 1, :], op0=ALU.add, op1=ALU.add))
            me(dve, v.reciprocal(den[:, :], den[:, :]))
            for j in range(2):
                v.tensor_tensor(k.gate[:, j, :], k.gate[:, j, :], den[:, :], ALU.mult)
            dve.wait_ge(counted, 1)
            me(dve, v.tensor_copy(tot[:, :, :], k.ps[1][0:P, 0:NT * NE].rearrange("p (t e) -> p t e", e=NE)))
            for e in range(NE):
                m = v.tensor_tensor_scan(inc[:, :, e], k.ones[0:P, 0:NT], tot[:, :, e], 0.0, ALU.mult, ALU.add)
            me(dve, m)
            me(dve, v.tensor_scalar(tiles[:, :], inc[:, NT - 1, :], float(M - 1), None, ALU.add))
            me(dve, v.tensor_copy(tiles_i[:, :], tiles[:, :]))
            me(dve, v.tensor_single_scalar(tiles_i[:, :], tiles_i[:, :], 7, ALU.logical_shift_right))
            me(dve, v.tensor_copy(tiles[:, :], tiles_i[:, :]))
            me(dve, v.tensor_tensor_scan(ends[:, :], k.ones[0:P, 0:NE], tiles[:, :], 0.0, ALU.mult, ALU.add))
            me(dve, v.tensor_tensor(begins[:, :], ends[:, :], tiles[:, :], ALU.subtract))
            me(dve, v.tensor_scalar(begins[:, :], begins[:, :], float(M), None, ALU.mult))
            me(dve, v.tensor_tensor(slot[:, :, :], inc[:, :, :], tot[:, :, :], ALU.subtract))
            me(dve, v.tensor_tensor(slot[:, :, :], slot[:, :, :], k.ps[0][0:P, 0:NT * NE].rearrange("p (t e) -> p t e", e=NE), ALU.add))
            me(dve, v.tensor_tensor(slot[:, :, :], slot[:, :, :], long(begins), ALU.add))
            for j in range(2):
                me(dve, v.tensor_tensor(cand[:, :, :], oh[:, j, :, :], slot[:, :, :], ALU.mult))
                me(dve, v.tensor_reduce(pos[:, j, :], cand[:, :, :], AX, ALU.add))
            me(dve, v.tensor_copy(k.place[:, :, :], pos[:, :, :]))
            me(dve, v.tensor_single_scalar(hi_i[:, :, :], k.place[:, :, :], 7, ALU.logical_shift_right))
            me(dve, v.tensor_copy(hi[:, :, :], hi_i[:, :, :]))
            me(dve, v.scalar_tensor_tensor(out=lo[:, :, :], in0=hi[:, :, :], scalar=-float(M), in1=pos[:, :, :], op0=ALU.mult, op1=ALU.add))
            v.tensor_tensor(at_lane[:, :, :], lane[:, :].rearrange("p (a m) -> p a m", a=1).to_broadcast([P, 2 * NT, M]),
                            lo[:, :, :].rearrange("p j (t a) -> p (j t) a", a=1).to_broadcast([P, 2 * NT, M]), ALU.is_equal)
            me(dve, v.tensor_tensor(at_item[:, :, :], item[:, :].rearrange("p (a m) -> p a m", a=1).to_broadcast([P, 2 * NT, NI]),
                                    hi[:, :, :].rearrange("p j (t a) -> p (j t) a", a=1).to_broadcast([P, 2 * NT, NI]), ALU.is_equal))
            for j in range(2):
                m = v.tensor_tensor(at_item[:, j * NT:(j + 1) * NT, :], at_item[:, j * NT:(j + 1) * NT, :],
                                    k.node[:, :].rearrange("p (t a) -> p t a", a=1).to_broadcast([P, NT, NI]), ALU.mult)
            me(dve, m)
            dve.sem_inc(places, 1)
            me(dve, v.tensor_tensor(over[:, :, :], item[:, :].rearrange("p (i a) -> p i a", a=1).to_broadcast([P, NI, NE]),
                                    ends[:, :].rearrange("p (a e) -> p a e", a=1).to_broadcast([P, NI, NE]), ALU.is_ge))
            me(dve, v.tensor_reduce(of_item[:, :], over[:, :, :], AX, ALU.add))
            me(dve, v.tensor_scalar(k.item_expert[:, :], of_item[0:1, :], float(NE - 1), None, ALU.min))
            dve.wait_ge(tokens, 1)
            me(dve, v.tensor_copy(k.slot_token[:, :], k.ps[2][:, 0:NI]))


def weights_phase(k, a):
    nc = k.nc
    ctx = ExitStack()
    HH = HB[a + 1] - HB[a]
    BLOCKS = [(b, min(128, HH - 128 * b)) for b in range(-(-HH // 128))]
    with ctx:
        sb = lambda n, s, d=F32: k.sb(f"w{a}_{n}", s, d, ctx)
        sem = lambda n: k.sem(f"w{a}_{n}")
        raw = [[sb(f"raw{m}{s}", [128, 3, C] if m < 2 else [128, 2, HH]) for s in range(2)] for m in range(3)]
        come = [[sem(f"come{m}{s}") for s in range(2)] for m in range(3)]
        turned, high_made, low_made = sem("turned"), sem("high_made"), sem("low_made")
        block = ctx.enter_context(nc.Block())
        names = ("L0_ffn_w1", "L0_ffn_w3", "L0_ffn_w2")

        def groups():
            for e in range(NE):
                s = e % 2
                for m in range(2):
                    for c in range(2):
                        ins = [(raw[m][s][0:n, b, c * 128:(c + 1) * 128], b * 128, n) for b, n in BLOCKS]
                        yield e, m, 128, ins, [t[:, c, e, 0:HH] for t in (k.w1, k.w3)[m]]
                for blocks in (BLOCKS[0:2], BLOCKS[2:3]):
                    rows, b0 = blocks[0][1], blocks[0][0]
                    ins = [(raw[2][s][:, c, b * 128:b * 128 + n], (b - b0) * C + c * 128, 128) for b, n in blocks for c in range(2)]
                    yield e, 2, rows, ins, [t[0:rows, b0:b0 + len(blocks), e, :] for t in k.w2]

        def bank(n, rows, dst):
            if len(dst.shape) == 2:
                return k.ps[n % 8][0:rows, 0:HH]
            return k.ps[n % 8][0:rows, 0:dst.shape[1] * C].rearrange("p (b c) -> p b c", c=C)

        G = 6

        @block.sync
        def _(sp):
            for e in range(NE):
                s = e % 2
                if e >= 2:
                    sp.wait_ge(turned, G * (e - 1))
                for m, name in enumerate(names):
                    if m < 2:
                        full = 128 * (len(BLOCKS) - 1)
                        sp.dma_start(raw[m][s][:, 0:len(BLOCKS) - 1, :], k.a[name][e, HB[a]:HB[a] + full, :].rearrange("(b p) c -> p b c", p=128)).then_inc(come[m][s], 16)
                        sp.dma_start(raw[m][s][0:HH - full, len(BLOCKS) - 1, :], k.a[name][e, HB[a] + full:HB[a + 1], :]).then_inc(come[m][s], 16)
                    else:
                        sp.dma_start(raw[m][s][:, :, :], k.a[name][e].rearrange("(b p) h -> p b h", p=128)[:, :, HB[a]:HB[a + 1]]).then_inc(come[m][s], 16)

        @block.tensor
        def _(pe):
            for n, (e, m, rows, ins, dst) in enumerate(groups()):
                pe.wait_ge(come[m][e % 2], (32 if m < 2 else 16) * (e // 2 + 1))
                if n >= 8:
                    pe.wait_ge(low_made, n - 7)
                for x, at, w in ins:
                    t = nc.tensor.transpose(k.ps[n % 8][0:rows, at:at + w], x, k.ident[0:x.shape[0], 0:x.shape[0]])
                t.then_inc(turned, 1)

        @block.scalar
        def _(act):
            for n, (e, m, rows, ins, dst) in enumerate(groups()):
                act.wait_ge(turned, n + 1)
                nc.scalar.copy(dst[0], bank(n, rows, dst[0])).then_inc(high_made, 1)

        @block.vector
        def _(dve):
            for n, (e, m, rows, ins, dst) in enumerate(groups()):
                dve.wait_ge(high_made, n + 1)
                nc.vector.tensor_tensor(dst[1], bank(n, rows, dst[0]), dst[0], ALU.subtract).then_inc(low_made, 1)


def experts_phase(k, a):
    nc = k.nc
    ctx = ExitStack()
    HH = HB[a + 1] - HB[a]
    BLOCKS = [(b, min(128, HH - 128 * b)) for b in range(-(-HH // 128))]
    X = 4
    with ctx:
        sb = lambda n, s, d=F32: k.sb(f"e{a}_{n}", s, d, ctx)
        sem = lambda n: k.sem(f"e{a}_{n}")
        ix = [sb(f"ix{s}", [M, 1], I32) for s in range(X)]
        x = [sb(f"x{s}", [M, C]) for s in range(X)]
        xt = [[sb(f"xt{part}{s}", [128, 2, M], F32R) for part in ("high", "low")] for s in range(2)]
        gated = [sb(f"gated{s}", [M, HH]) for s in range(2)]
        h = [sb(f"h{s}", [M, HH]) for s in range(2)]
        ht = [[sb(f"ht{part}{s}", [128, 3, M], F32R) for part in ("high", "low")] for s in range(2)]
        y = [sb(f"y{s}", [M, C]) for s in range(2)]
        x_in = [k.gather_sem(f"e{a}_x_in{s}") for s in range(X)]
        y_out = [sem(f"y_out{s}") for s in range(2)]
        y_in = [sem(f"y_in{s}") for s in range(2)]
        ix_made, issuing, x_turned, x_high, x_kept = (sem(n) for n in ("ix_made", "issuing", "x_turned", "x_high", "x_kept"))
        up, silued, h_made, h_turned, h_high, h_kept = (sem(n) for n in ("up", "silued", "h_made", "h_turned", "h_high", "h_kept"))
        down, y_kept, y_free = sem("down"), sem("y_kept"), sem("y_free")
        block = ctx.enter_context(nc.Block())
        TURN, UP, GATE, TH, DOWN = k.ps[0], k.ps[1:3], k.ps[3:5], k.ps[5], k.ps[6:8]
        PRODUCTS = ((0, 0), (0, 1), (1, 0))
        FULL = 2 * M
        TAIL = BLOCKS[2][1]

        @block.gpsimd
        def _(pool):
            with pool.Fori(0, NI // X) as i:
                for s in range(X):
                    pool.wait_ge(x_turned, i * X + s + 1)
                    nc.gpsimd.tensor_copy(ix[s][:, :], k.slot_token[:, bass.ds(i * X + s, 1)]).then_inc(ix_made, 1)
                    pool.wait_ge(ix_made, i * X + s + 1)
                    pool.sem_inc(issuing, 1)
                    pool.indirect_dma_start(out=x[s][:, :], out_offset=None, in_=k.xn_tab,
                                            in_offset=bass.IndirectOffsetOnAxis(ap=ix[s][:, 0:1], axis=0)).then_inc(x_in[s], 16)

        @block.sync
        def _(sp):
            rows = k.y_tab.rearrange("(i p) c -> i p c", p=M)

            def load(i, s):
                sp.dma_start(y[s][:, :], rows[bass.ds(i, 1), :, :].rearrange("a p c -> (a p) c")).then_inc(y_in[s], 16)

            def store(i, s, turn):
                sp.wait_ge(y_kept, i + 3)
                sp.dma_start(rows[bass.ds(i, 1), :, :].rearrange("a p c -> (a p) c"), y[s][:, :]).then_inc(y_out[s], 16)
                sp.wait_ge(y_out[s], 16 * turn + 16)

            if a == 0:
                sp.sem_inc(y_free, 2)
                with sp.Fori(0, NI // 2) as i:
                    for s in range(2):
                        store(i * 2 + s, s, i)
                        sp.sem_inc(y_free, 1)
            else:
                for s in range(2):
                    load(s, s)
                with sp.Fori(0, NI // 2 - 1) as i:
                    for s in range(2):
                        store(i * 2 + s, s, i)
                        load(i * 2 + s + 2, s)
                for s in range(2):
                    store(NI - 2 + s, s, NI // 2 - 1)

        def steps(eng, start, item, finish):
            start()
            item(2, 2, 0, True)
            item(3, 3, 0, True)
            with eng.Fori(1, NI // X - 1) as j:
                for s in range(X):
                    item(j * X + s, s, j, True)
            for s in range(X):
                item(NI - X + s, s, NI // X - 1, s < X - 2)
            finish()

        @block.tensor
        def _(pe):
            pe.sem_inc(x_turned, X)
            pe.sem_inc(h_turned, 2)
            pe.sem_inc(up, 2)
            pe.sem_inc(down, 2)

            def expert(i):
                return pe.value_load(k.item_expert[0:1, bass.ds(i, 1)], min_val=0, max_val=NE - 1)

            experts = [None] * X

            def turn_x(i, s, turn):
                pe.wait_ge(x_in[s], 16 * turn + 16)
                pe.wait_ge(x_kept, i + 1)
                for c in range(2):
                    m = nc.tensor.transpose(TURN[:, c * M:(c + 1) * M], x[s][:, c * 128:(c + 1) * 128], k.ident[:, :])
                m.then_inc(x_turned, 1)

            def go_up(i, s, e):
                pe.wait_ge(x_kept, i + 2)
                pe.wait_ge(h_made, i + 1)
                for bank, w in ((UP[s], k.w1), (GATE[s], k.w3)):
                    n = 0
                    for c in range(2):
                        for px, pw in PRODUCTS:
                            m = nc.tensor.matmul(bank[:, 0:HH], xt[s][px][:, c, :], w[pw][:, c, bass.ds(e, 1), 0:HH].rearrange("p a h -> p (a h)"),
                                                 start=(n == 0), stop=(n == 5))
                            n += 1
                m.then_inc(up, 1)

            def turn_h(i, s):
                pe.wait_ge(h_made, i + 3)
                pe.wait_ge(h_kept, i + 1)
                for b, n in BLOCKS:
                    m = nc.tensor.transpose(TH[0:n, b * M:(b + 1) * M], h[s][:, b * 128:b * 128 + n], k.ident[:, :])
                m.then_inc(h_turned, 1)

            def go_down(i, s, e):
                pe.wait_ge(h_kept, i + 2)
                pe.wait_ge(y_kept, i + 1)
                j = 0
                for b, n in BLOCKS:
                    for ph, pw in PRODUCTS:
                        m = nc.tensor.matmul(DOWN[s][:, 0:C], ht[s][ph][0:n, b, :], k.w2[pw][0:n, b, bass.ds(e, 1), :].rearrange("p a c -> p (a c)"),
                                             start=(j == 0), stop=(j == 8))
                        j += 1
                m.then_inc(down, 1)

            def start():
                turn_x(0, 0, 0)
                turn_x(1, 1, 0)
                experts[0], experts[1] = expert(0), expert(1)
                go_up(0, 0, experts[0])
                turn_x(2, 2, 0)
                go_up(1, 1, experts[1])
                turn_x(3, 3, 0)
                turn_h(0, 0)

            def item(i, x_slot, turn, more):
                s = x_slot % 2
                before = experts[x_slot - 2] if x_slot >= 2 else expert(i - 2)
                experts[x_slot] = expert(i)
                go_up(i, s, experts[x_slot])
                if more:
                    turn_x(i + 2, (x_slot + 2) % X, turn + (x_slot + 2) // X)
                turn_h(i - 1, 1 - s)
                go_down(i - 2, s, before)

            def finish():
                turn_h(NI - 1, 1)
                go_down(NI - 2, 0, experts[X - 2])
                go_down(NI - 1, 1, experts[X - 1])

            steps(pe, start, item, finish)

        def keep_y(eng, i, s, pair):
            eng.wait_ge(down, i + 3)
            if a == 0:
                eng.wait_ge(y_free, i + 1)
                nc.scalar.copy(y[s][:, :], DOWN[s][:, 0:C]).then_inc(y_kept, 1)
            else:
                eng.wait_ge(y_in[s], 16 * pair)
                nc.vector.tensor_tensor(y[s][:, :], y[s][:, :], DOWN[s][:, 0:C], ALU.add).then_inc(y_kept, 1)

        @block.scalar
        def _(act):
            if a == 0:
                act.sem_inc(y_kept, 2)

            def keep_x(i, s):
                act.wait_ge(x_turned, i + 1 + X)
                act.wait_ge(up, i + 1)
                nc.scalar.copy(xt[s][0][:, :, :].rearrange("p a m -> p (a m)"), TURN[:, 0:2 * M]).then_inc(x_high, 1)

            def silu(i, s):
                act.wait_ge(up, i + 3)
                act.wait_ge(h_made, i + 1)
                nc.scalar.activation(gated[s][:, :], UP[s][:, 0:HH], ACT.Silu).then_inc(silued, 1)

            def keep_h(i, s):
                act.wait_ge(h_turned, i + 3)
                act.wait_ge(down, i + 1)
                nc.scalar.copy(ht[s][0][:, 0:2, :].rearrange("p b m -> p (b m)"), TH[:, 0:FULL])
                nc.scalar.copy(ht[s][0][0:TAIL, 2, :], TH[0:TAIL, FULL:FULL + M]).then_inc(h_high, 1)

            def start():
                keep_x(0, 0)
                keep_x(1, 1)
                silu(0, 0)
                keep_x(2, 0)
                silu(1, 1)
                keep_x(3, 1)
                keep_h(0, 0)

            def item(i, x_slot, turn, more):
                s = x_slot % 2
                silu(i, s)
                if more:
                    keep_x(i + 2, s)
                keep_h(i - 1, 1 - s)
                if a == 0:
                    keep_y(act, i - 2, s, turn * (X // 2) + x_slot // 2)

            def finish():
                keep_h(NI - 1, 1)
                if a == 0:
                    keep_y(act, NI - 2, 0, NI // 2)
                    keep_y(act, NI - 1, 1, NI // 2)

            steps(act, start, item, finish)

        @block.vector
        def _(dve):
            v = nc.vector
            dve.sem_inc(h_made, 2)
            dve.sem_inc(x_kept, 1)
            dve.sem_inc(h_kept, 1)
            if a == 1:
                dve.sem_inc(y_kept, 2)

            def low_x(i, s):
                dve.wait_ge(x_high, i + 1)
                v.tensor_tensor(xt[s][1][:, :, :].rearrange("p a m -> p (a m)"), TURN[:, 0:2 * M], xt[s][0][:, :, :].rearrange("p a m -> p (a m)"), ALU.subtract).then_inc(x_kept, 1)

            def gate(i, s):
                dve.wait_ge(silued, i + 1)
                dve.wait_ge(h_turned, i + 1)
                v.tensor_tensor(h[s][:, :], gated[s][:, :], GATE[s][:, 0:HH], ALU.mult).then_inc(h_made, 1)

            def low_h(i, s):
                dve.wait_ge(h_high, i + 1)
                v.tensor_tensor(ht[s][1][:, 0:2, :].rearrange("p b m -> p (b m)"), TH[:, 0:FULL], ht[s][0][:, 0:2, :].rearrange("p b m -> p (b m)"), ALU.subtract)
                v.tensor_tensor(ht[s][1][0:TAIL, 2, :], TH[0:TAIL, FULL:FULL + M], ht[s][0][0:TAIL, 2, :], ALU.subtract).then_inc(h_kept, 1)

            def start():
                low_x(0, 0)
                low_x(1, 1)
                gate(0, 0)
                low_x(2, 0)
                gate(1, 1)
                low_x(3, 1)
                low_h(0, 0)

            def item(i, x_slot, turn, more):
                s = x_slot % 2
                gate(i, s)
                if more:
                    low_x(i + 2, s)
                low_h(i - 1, 1 - s)
                if a == 1:
                    keep_y(dve, i - 2, s, turn * (X // 2) + x_slot // 2)

            def finish():
                low_h(NI - 1, 1)
                if a == 1:
                    keep_y(dve, NI - 2, 0, NI // 2)
                    keep_y(dve, NI - 1, 1, NI // 2)

            steps(dve, start, item, finish)


def combine_phase(k):
    nc, st = k.nc, k.steps
    ctx = ExitStack()
    GROUPS = NT // TB
    with ctx:
        sb = lambda n, s, d=F32: k.sb(f"c_{n}", s, d, ctx)
        sem = lambda n: k.sem(f"c_{n}")
        ys = sb("ys", [P, 2, NT, C])
        xn = sb("xn", [P, NT, C])
        x1_in, deviations, roots, normed_s, out_done = (sem(n) for n in ("x1_in", "deviations", "roots", "normed", "out_done"))
        squares0 = sem("squares0")
        ys_in = [k.gather_sem(f"c_ys_in{g}") for g in range(GROUPS)]
        block = ctx.enter_context(nc.Block())

        @block.sync
        def _(sp):
            sp.dma_start(k.res[:, :, :], k.x1_tab.rearrange("(p t) c -> p t c", p=P)).then_inc(x1_in, 16)
            att = k.att
            squares_in, wx_in, small_in, bout_in = k.att_in
            for t, name in ((att["w_x"], "L1_ffn_W_x"), (att["w_fx"], "L1_ffn_W_fx"), (att["w_out"], "L1_ffn_W_out")):
                sp.dma_start(t[:, :, :], k.a[name].rearrange("(a p) c -> p a c", p=128)).then_inc(wx_in, 16)
            sp.dma_start(att["b_fx"][:, :], k.a["L1_ffn_b_fx"].rearrange("(a c) -> a c", a=1)).then_inc(small_in, 16)
            with nc.allow_non_contiguous_dma(reason="512 single values"):
                sp.dma_start(att["b_x"][:, :], k.a["L1_ffn_b_x"].rearrange("(a p) -> p a", p=128)).then_inc(small_in, 16)
            sp.dma_start(att["b_slice"][:, :, :], k.a["L1_ffn_b_slice"].rearrange("(a b c) -> a b c", a=1, b=1).to_broadcast([1, H, HD])).then_inc(small_in, 16)
            sp.dma_start(att["temp"][:, :], k.a["L1_ffn_temperature"].rearrange("a h b c -> a (h b c)")).then_inc(small_in, 16)
            sp.dma_start(att["temp_b"][:, :], k.a["L1_ffn_temperature"].rearrange("a h b c -> a (h b c)").to_broadcast([128, H])).then_inc(small_in, 16)
            sp.dma_start(att["b_out"][:, :], k.a["L1_ffn_b_out"].rearrange("(a c) -> a c", a=1).to_broadcast([P, C])).then_inc(bout_in, 16)
            sp.wait_ge(squares0, 1)
            for i, name in enumerate(("L1_ffn_W_slice", "L1_ffn_W_q", "L1_ffn_W_k", "L1_ffn_W_v")):
                for d in range(2):
                    sp.dma_start(att["square"][64 * d:64 * d + 64, i, 64 * d:64 * d + 64], k.a[name]).then_inc(squares_in, 16)
            table = k.xn_tab.rearrange("(p t) c -> p t c", p=P)
            for g in range(GROUPS):
                sp.wait_ge(normed_s, (g + 1) * TB)
                sp.dma_start(table[:, g * TB:(g + 1) * TB, :], xn[:, g * TB:(g + 1) * TB, :]).then_inc(out_done, 16)
            sp.wait_ge(out_done, 16 * GROUPS)

        @block.gpsimd
        def _(pool):
            nc.gpsimd.memset(k.att["square"][:, :, :], 0.0).then_inc(squares0, 1)
            for t in range(NT):
                for j in range(2):
                    pool.indirect_dma_start(out=ys[:, j, t, :], out_offset=None, in_=k.y_tab,
                                            in_offset=bass.IndirectOffsetOnAxis(ap=k.place[:, j, t:t + 1], axis=0)).then_inc(ys_in[t // TB], 16)

        @block.scalar
        def _(act):
            norm_roots(k, act, deviations, roots)

        @block.vector
        def _(dve):
            v, me = nc.vector, st["dve"]
            dve.wait_ge(x1_in, 16)
            for g in range(GROUPS):
                dve.wait_ge(ys_in[g], 16 * 2 * TB)
                for j in range(2):
                    for t in range(g * TB, (g + 1) * TB):
                        m = v.scalar_tensor_tensor(out=k.res[:, t, :], in0=ys[:, j, t, :], scalar=k.gate[:, j, t:t + 1], in1=k.res[:, t, :], op0=ALU.mult, op1=ALU.add)
                    me(dve, m)
                for t in range(g * TB, (g + 1) * TB):
                    v.bn_stats(k.stats[:, t, :], k.res[:, t, :])
            norm_factors(k, dve, deviations, roots)
            with dve.Fori(0, NT) as t:
                normed(k, tile_of(xn, t), t).then_inc(normed_s, 1)


HD = 64
NP = H * HD // 128
HG = H * HD


def gnn_node_phase(k):
    nc, st = k.nc, k.steps
    ctx = ExitStack()
    with ctx:
        sb = lambda n, s, d=F32: k.sb(f"n_{n}", s, d, ctx)
        sem = lambda n: k.sem(f"n_{n}")
        q = Turning(k, "n", ctx)
        square, diag, w_comb, bias_x = (k.att[n] for n in ("square", "diag", "w_comb", "bias"))
        w_x, b_x, b_slice, temp, temp_b = (k.att[n] for n in ("w_x", "b_x", "b_slice", "temp", "temp_b"))
        w_xt = sb("w_xt", [128, NP, C])
        bias_row = sb("bias_row", [1, HG])
        squares_in, wx_in, small_in, bout_in = k.att_in
        prep, prep_pe = sem("prep"), sem("prep_pe")
        w, wt = sb("w", [128, 2, C]), sb("wt", [128, 2, C])
        bias = sb("bias", [P, C])
        inv, part = sb("inv", [P, NT]), sb("part", [P, NT])
        chain = sb("chain", [P, NT, RW])
        w_in, bias_in, w_turned, w_ready = sem("w_in"), sem("bias_in"), sem("w_turned"), sem("w_ready")
        chains_in = k.gather_sem("n_chains_in")
        block = ctx.enter_context(nc.Block())

        @block.sync
        def _(sp):
            sp.dma_start(w[:, :, :], k.a["L1_gnn_W"].rearrange("(a p) c -> p a c", p=128)).then_inc(w_in, 16)
            sp.dma_start(bias[:, :], k.a["L1_gnn_b"].rearrange("(a c) -> a c", a=1).to_broadcast([P, C])).then_inc(bias_in, 16)

        @block.gpsimd
        def _(pool):
            g, me = nc.gpsimd, st["pool"]
            me(pool, g.memset(diag[:, :], 0.0))
            g.memset(diag[0:64, 0:64], 1.0)
            me(pool, g.memset(diag[64:128, 64:128], 1.0))
            gather_rows(pool, chain, k.chains[:, :], k.chain_row, chains_in)

        @block.tensor
        def _(pe):
            pe.wait_ge(w_in, 16)
            for c in range(2):
                for a in range(2):
                    m = nc.tensor.transpose(k.ps[c][:, a * 128:(a + 1) * 128], w[:, a, c * 128:(c + 1) * 128], k.ident[:, :])
                m.then_inc(w_turned, 1)
            pe.wait_ge(w_ready, 2)
            t_ = nc.tensor
            pe.wait_ge(wx_in, 48)
            for a in range(NP):
                for c in range(2):
                    m = t_.transpose(k.ps[a][:, c * 128:(c + 1) * 128], w_x[:, c, a * 128:(a + 1) * 128], k.ident[:, :])
                m.then_inc(prep_pe, 1)
            pe.wait_ge(squares_in, 128)
            pe.wait_ge(small_in, 80)
            pe.wait_ge(prep, NP)
            for c in range(2):
                for a in range(NP):
                    m = t_.matmul(k.ps[4 + c][:, a * 128:(a + 1) * 128], w_xt[:, a, c * 128:(c + 1) * 128], square[:, 0, :], start=True, stop=True)
                m.then_inc(prep_pe, 1)
            for a in range(NP):
                m = t_.matmul(k.ps[6][0:1, a * 128:(a + 1) * 128], b_x[:, a:a + 1], square[:, 0, :], start=True, stop=True)
            m.then_inc(prep_pe, 1)
            pe.wait_ge(prep, NP + 1)
            t_.matmul(k.ps[7][0:P, :], k.ones[0:1, 0:P], bias_row[:, :], start=True, stop=True).then_inc(prep_pe, 1)
            pe.wait_ge(prep, NP + 4)

            def multiply(s):
                for c in range(2):
                    m = nc.tensor.matmul(k.ps[3 + s][0:P, 0:C], q.xt[:, s, c, :], wt[:, c, :], start=(c == 0), stop=(c == 1))
                return m

            q.on_tensor(pe, multiply)

        @block.scalar
        def _(act):
            q.on_scalar(act)

        @block.vector
        def _(dve):
            v, me = nc.vector, st["dve"]
            me(dve, v.tensor_scalar(inv[:, :], k.deg[:, :], 1.0, None, ALU.add))
            me(dve, v.reciprocal(inv[:, :], inv[:, :]))
            me(dve, v.tensor_tensor(part[:, :], inv[:, :], k.deg[:, :], ALU.mult))
            dve.wait_ge(bias_in, 16)
            with dve.Fori(0, NT) as t:
                v.scalar_tensor_tensor(out=tile_of(k.res, t), in0=bias[:, :], scalar=part[:, bass.ds(t, 1)], in1=tile_of(k.res, t), op0=ALU.mult, op1=ALU.add)
            for c in range(2):
                dve.wait_ge(w_turned, c + 1)
                v.tensor_copy(wt[:, c, :], k.ps[c][:, 0:C]).then_inc(w_ready, 1)
            for a in range(NP):
                dve.wait_ge(prep_pe, a + 1)
                v.tensor_copy(w_xt[:, a, :], k.ps[a][:, 0:C]).then_inc(prep, 1)
            dve.wait_ge(small_in, 80)
            for t in (temp, temp_b):
                me(dve, v.tensor_scalar(t[:, :], t[:, :], 0.1, 5.0, ALU.max, ALU.min))
                me(dve, v.reciprocal(t[:, :], t[:, :]))
            dve.wait_ge(prep_pe, NP + 3)
            me(dve, v.tensor_tensor(bias_row[:, :], k.ps[6][0:1, :], b_slice[:, :, :].rearrange("p h g -> p (h g)"), ALU.add))
            r = bias_row[:, :].rearrange("p (h g) -> p h g", h=H)
            v.tensor_tensor(r, r, temp[:, :].rearrange("p (h a) -> p h a", a=1).to_broadcast([1, H, HD]), ALU.mult).then_inc(prep, 1)
            for c in range(2):
                v.tensor_tensor(w_comb[:, c, :].rearrange("p (h g) -> p h g", h=H), k.ps[4 + c][:, :].rearrange("p (h g) -> p h g", h=H),
                                temp_b[:, :].rearrange("p (h a) -> p h a", a=1).to_broadcast([128, H, HD]), ALU.mult).then_inc(prep, 1)
            dve.wait_ge(prep_pe, NP + 4)
            v.tensor_copy(bias_x[:, :], k.ps[7][0:P, :]).then_inc(prep, 1)
            dve.wait_ge(bout_in, 16)

            dve.wait_ge(k.mains_in, 16 * NT)
            dve.wait_ge(chains_in, 16 * NT)

            def fill(t, s):
                return v.tensor_tensor(q.xn[:, s, :], tile_of(k.mains, t)[:, 0:C], tile_of(chain, t)[:, 0:C], ALU.add)

            def take(t, s):
                return v.scalar_tensor_tensor(out=tile_of(k.res, t), in0=k.ps[3 + s][0:P, 0:C], scalar=inv[:, bass.ds(t, 1)], in1=tile_of(k.res, t), op0=ALU.mult, op1=ALU.add)

            def stats(t):
                return v.bn_stats(tile_of(k.stats, t), tile_of(k.res, t))

            q.on_vector(dve, fill, take, after=stats)


def attention_phase(k):
    nc, st = k.nc, k.steps
    ctx = ExitStack()
    with ctx:
        sb = lambda n, s, d=F32: k.sb(f"t_{n}", s, d, ctx)
        sem = lambda n: k.sem(f"t_{n}")
        w_fx, w_out, square, diag, w_comb, b_fx, bias, b_out = (
            k.att[n] for n in ("w_fx", "w_out", "square", "diag", "w_comb", "b_fx", "bias", "b_out"))
        xn = sb("xn", [P, TB, C + 1])
        xt = sb("xt", [128, TB, 2, P])
        logit = sb("logit", [P, TB, H, HD])
        peak, total = sb("peak", [P, TB, H]), sb("total", [P, TB, H])
        wt = sb("wt", [128, NT, NP, P])
        u, inv = sb("u", [128, NP, C + 1]), sb("inv", [128, NP])
        ut, share = sb("ut", [128, 2, HG]), sb("share", [1, HG])
        token, qt, kt, val = (sb(n, [128, NP, 128]) for n in ("token", "qt", "kt", "val"))
        score, attn, attn_t, mixed = sb("score", [128, NP, HD]), sb("attn", [128, NP, 128]), sb("attn_t", [128, NP, 128]), sb("mixed", [128, NP, 128])
        apeak, asum = sb("apeak", [128, NP]), sb("asum", [128, NP])
        v2 = sb("v2", [128, NP, C])
        xones, deviations, roots = sem("xones"), sem("deviations"), sem("roots")
        made, turned, kept, logits, biased, peaked, less, exped, summed, weighed, w_turned, w_kept, added = (
            sem(n) for n in ("made", "turned", "kept", "logits", "biased", "peaked", "less", "exped", "summed", "weighed", "w_turned", "w_kept", "added"))
        mid, mid_pe, mid_act = sem("mid"), sem("mid_pe"), sem("mid_act")
        result, joined, stored = sem("result"), sem("joined"), sem("stored")
        block = ctx.enter_context(nc.Block())
        T, L, X, U = k.ps[0], (k.ps[1], k.ps[2]), k.ps[3], k.ps[4:8]

        def bodies(eng, body):
            body(0, first=True)
            with eng.Fori(1, NT // TB - 1) as i:
                body(i)
            body(NT // TB - 1, last=True)

        @block.sync
        def _(sp):
            rows = k.out.rearrange("(p t) c -> p t c", p=P)
            with sp.Fori(0, NT // TB) as i:
                sp.wait_ge(joined, i * TB + TB)
                sp.dma_start(rows[:, bass.ds(i * TB, TB), :], k.res[:, bass.ds(i * TB, TB), :]).then_inc(stored, 16)
            sp.wait_ge(stored, 16 * (NT // TB))

        @block.gpsimd
        def _(pool):
            g, me = nc.gpsimd, st["pool"]
            g.memset(attn[:, :, :], 0.0).then_inc(xones, 1)
            pool.wait_ge(xones, 1)
            g.memset(xn[:, :, C:C + 1], 1.0).then_inc(xones, 1)

            def less_peak(t, s):
                pool.wait_ge(peaked, t + 1)
                g.tensor_tensor(logit[:, s, :, :], logit[:, s, :, :], peak[:, s, :].rearrange("p (h a) -> p h a", a=1).to_broadcast([P, H, HD]), ALU.subtract).then_inc(less, 1)

            def weigh(t, s):
                pool.wait_ge(summed, t + 1)
                g.tensor_tensor(logit[:, s, :, :], logit[:, s, :, :], total[:, s, :].rearrange("p (h a) -> p h a", a=1).to_broadcast([P, H, HD]), ALU.mult).then_inc(weighed, 1)

            def body(i, first=False, last=False):
                for s in range(TB):
                    less_peak(i * TB + s, s)
                    if s or not first:
                        weigh(i * TB + s - 1, (s - 1) % TB)

            bodies(pool, body)
            weigh(NT - 1, TB - 1)

        @block.tensor
        def _(pe):
            t_ = nc.tensor
            pe.wait_ge(xones, 2)

            def turn(t, s):
                pe.wait_ge(made, t + 1)
                pe.wait_ge(kept, t + 1)
                for c in range(2):
                    m = t_.transpose(T[:, c * P:(c + 1) * P], xn[:, s, c * 128:(c + 1) * 128], k.ident[0:P, 0:P])
                m.then_inc(turned, 1)

            def score_nodes(t, s, bank, biased_at):
                pe.wait_ge(kept, t + 2)
                pe.wait_ge(biased, biased_at)
                for c in range(2):
                    m = t_.matmul(bank[0:P, :], xt[:, s, c, :], w_comb[:, c, :], start=(c == 0), stop=(c == 1))
                m.then_inc(logits, 1)

            def slices(t, s, first=False, last=False):
                pe.wait_ge(weighed, t + 1)
                pe.wait_ge(w_kept, t + 1)
                w = logit[:, s, :, :].rearrange("p h g -> p (h g)")
                for a in range(NP):
                    m = t_.transpose(X[:, a * P:(a + 1) * P], w[:, a * 128:(a + 1) * 128], k.ident[0:P, 0:P])
                m.then_inc(w_turned, 1)
                for a in range(NP):
                    m = t_.matmul(U[a][:, 0:C + 1], w[:, a * 128:(a + 1) * 128], xn[:, s, :], start=first, stop=last, skip_group_check=True)
                m.then_inc(added, 1)

            def body(i, first=False, last=False):
                for s in range(TB):
                    t = i * TB + s
                    if s < TB - 1 or not last:
                        turn(t + 1, (s + 1) % TB)
                    score_nodes(t, s, L[s % 2], t + 1 if s == 0 else t)
                    if s >= 2 or not first:
                        slices(t - 2, (s - 2) % TB, first=first and s == 2)

            turn(0, 0)
            bodies(pe, body)
            slices(NT - 2, TB - 2)
            slices(NT - 1, TB - 1, last=True)

            pe.wait_ge(w_kept, NT + 1)
            pe.wait_ge(mid, 1)
            for c in range(2):
                for a in range(NP):
                    m = t_.transpose(k.ps[c][:, a * 128:(a + 1) * 128], u[:, a, c * 128:(c + 1) * 128], k.ident[:, :])
                m.then_inc(mid_pe, 1)
            for a in range(NP):
                m = t_.transpose(k.ps[2][0:1, a * 128:(a + 1) * 128], u[:, a, C:C + 1], k.ident[:, :])
            m.then_inc(mid_pe, 1)
            pe.wait_ge(mid, 4)
            for a in range(NP):
                cols = slice(a * 128, (a + 1) * 128)
                for c in range(2):
                    t_.matmul(k.ps[3][:, cols], w_fx[:, c, cols], ut[:, c, cols], start=(c == 0), stop=False)
                m = t_.matmul(k.ps[3][:, cols], b_fx[:, cols], share[:, cols], start=False, stop=True)
            m.then_inc(mid_pe, 1)
            pe.wait_ge(mid, 5)
            for a in range(NP):
                cols = slice(a * 128, (a + 1) * 128)
                t_.matmul(k.ps[4][:, cols], square[:, 1, :], token[:, a, :], start=True, stop=True)
                t_.matmul(k.ps[5][:, cols], square[:, 2, :], token[:, a, :], start=True, stop=True)
                m = t_.matmul(k.ps[6][:, cols], token[:, a, :], square[:, 3, :], start=True, stop=True)
            m.then_inc(mid_pe, 1)
            pe.wait_ge(mid, 8)
            for a in range(NP):
                m = t_.matmul(k.ps[7][:, a * 128:(a + 1) * 128], qt[:, a, :], kt[:, a, :], start=True, stop=True)
            m.then_inc(mid_pe, 1)
            pe.wait_ge(mid, 9)
            for a in range(NP):
                m = t_.transpose(k.ps[0][:, a * 128:(a + 1) * 128], attn[:, a, :], k.ident[:, :])
            m.then_inc(mid_pe, 1)
            pe.wait_ge(mid, 10)
            for a in range(NP):
                m = t_.matmul(k.ps[1][:, a * 128:(a + 1) * 128], val[:, a, :], attn_t[:, a, :], start=True, stop=True)
            m.then_inc(mid_pe, 1)
            pe.wait_ge(mid, 11)
            for a in range(NP):
                m = t_.matmul(k.ps[2 + a // 2][:, (a % 2) * C:(a % 2 + 1) * C], mixed[:, a, :], w_out[:, a, :], start=True, stop=True)
            m.then_inc(mid_pe, 1)
            pe.wait_ge(mid, 13)

            for t in range(NT):
                if t >= 8:
                    pe.wait_ge(joined, t - 7)
                for a in range(NP):
                    m = t_.matmul(k.ps[t % 8][0:P, 0:C], wt[:, t, a, :], v2[:, a, :], start=(a == 0), stop=(a == NP - 1))
                m.then_inc(result, 1)

        @block.scalar
        def _(act):
            a_ = nc.scalar
            norm_roots(k, act, deviations, roots)
            act.sem_inc(kept, 1)
            act.sem_inc(w_kept, 1)

            def keep(t, s):
                act.wait_ge(turned, t + 1)
                a_.copy(xt[:, s, :, :].rearrange("p a n -> p (a n)"), T[:, 0:2 * P]).then_inc(kept, 1)

            def exp(t, s):
                act.wait_ge(less, t + 1)
                a_.activation(logit[:, s, :, :], logit[:, s, :, :], ACT.Exp).then_inc(exped, 1)

            def keep_w(t, s):
                act.wait_ge(w_turned, t + 1)
                a_.copy(wt[:, bass.ds(t, 1), :, :].rearrange("p b a n -> p (b a n)"), X[:, 0:NP * P]).then_inc(w_kept, 1)

            def body(i, first=False, last=False):
                for s in range(TB):
                    t = i * TB + s
                    if s < TB - 1 or not last:
                        keep(t + 1, (s + 1) % TB)
                    if s or not first:
                        exp(t - 1, (s - 1) % TB)
                    if s >= 2 or not first:
                        keep_w(t - 2, (s - 2) % TB)

            keep(0, 0)
            bodies(act, body)
            exp(NT - 1, TB - 1)
            keep_w(NT - 2, TB - 2)
            keep_w(NT - 1, TB - 1)
            act.wait_ge(mid_act, 1)
            a_.activation(score[:, :, :], score[:, :, :], ACT.Exp, scale=float(HD) ** -0.5).then_inc(mid_act, 1)

        @block.vector
        def _(dve):
            v, me = nc.vector, st["dve"]
            norm_factors(k, dve, deviations, roots)
            dve.wait_ge(xones, 2)
            dve.sem_inc(biased, 1)

            def fill(t, s):
                normed(k, xn[:, s, 0:C], t).then_inc(made, 1)

            def add_bias(t, s):
                dve.wait_ge(logits, t + 1)
                v.tensor_tensor(logit[:, s, :, :].rearrange("p h g -> p (h g)"), L[s % 2][0:P, :], bias[:, :], ALU.add).then_inc(biased, 1)
                dve.wait_ge(biased, t + 2)
                v.tensor_reduce(peak[:, s, :], logit[:, s, :, :], AX, ALU.max).then_inc(peaked, 1)

            def add_up(t, s):
                dve.wait_ge(exped, t + 1)
                me(dve, v.tensor_reduce(total[:, s, :], logit[:, s, :, :], AX, ALU.add))
                v.reciprocal(total[:, s, :], total[:, s, :]).then_inc(summed, 1)

            def body(i, first=False, last=False):
                if not first and not last:
                    me.loop(i - 1, TB)
                for s in range(TB):
                    if s == TB - 1 and not last or s < TB - 1 and not first:
                        dve.wait_ge(added, i * TB + s - TB + 2)
                    if s < TB - 1 or not last:
                        fill(i * TB + s + 1, (s + 1) % TB)
                    add_bias(i * TB + s, s)
                    if s or not first:
                        add_up(i * TB + s - 1, (s - 1) % TB)
                if not first and not last:
                    me.end(NT // TB - 2)

            fill(0, 0)
            bodies(dve, body)
            add_up(NT - 1, TB - 1)

            dve.wait_ge(added, NT)
            for a in range(NP):
                m = v.tensor_scalar(inv[:, a:a + 1], U[a][:, C:C + 1], 1e-5, None, ALU.add)
            me(dve, m)
            me(dve, v.reciprocal(inv[:, :], inv[:, :]))
            for a in range(NP):
                m = v.tensor_scalar(u[:, a, :], U[a][:, 0:C + 1], inv[:, a:a + 1], None, ALU.mult)
            m.then_inc(mid, 1)
            for c in range(2):
                dve.wait_ge(mid_pe, c + 1)
                v.tensor_copy(ut[:, c, :], k.ps[c][:, :]).then_inc(mid, 1)
            dve.wait_ge(mid_pe, 3)
            v.tensor_copy(share[:, :], k.ps[2][0:1, :]).then_inc(mid, 1)
            dve.wait_ge(mid_pe, 4)
            v.tensor_tensor(token[:, :, :], k.ps[3][:, :].rearrange("p (a g) -> p a g", a=NP),
                            diag[:, :].rearrange("p (b g) -> p b g", b=1).to_broadcast([128, NP, 128]), ALU.mult).then_inc(mid, 1)
            dve.wait_ge(mid_pe, 5)
            for t, b in ((qt, 4), (kt, 5), (val, 6)):
                v.tensor_copy(t[:, :, :].rearrange("p a g -> p (a g)"), k.ps[b][:, :]).then_inc(mid, 1)
            dve.wait_ge(mid_pe, 6)
            for d in range(2):
                rows = slice(64 * d, 64 * d + 64)
                m = v.tensor_copy(score[rows, :, :], k.ps[7][rows, :].rearrange("p (a g) -> p a g", a=NP)[:, :, 64 * d:64 * d + 64])
            me(dve, m)
            me(dve, v.tensor_reduce(apeak[:, :], score[:, :, :], AX, ALU.max))
            v.tensor_tensor(score[:, :, :], score[:, :, :], apeak[:, :].rearrange("p (a b) -> p a b", b=1).to_broadcast([128, NP, HD]), ALU.subtract).then_inc(mid_act, 1)
            dve.wait_ge(mid_act, 2)
            me(dve, v.tensor_reduce(asum[:, :], score[:, :, :], AX, ALU.add))
            me(dve, v.reciprocal(asum[:, :], asum[:, :]))
            for d in range(2):
                rows = slice(64 * d, 64 * d + 64)
                m = v.tensor_tensor(attn[rows, :, 64 * d:64 * d + 64], score[rows, :, :],
                                    asum[rows, :].rearrange("p (a b) -> p a b", b=1).to_broadcast([64, NP, HD]), ALU.mult)
            m.then_inc(mid, 1)
            dve.wait_ge(mid_pe, 7)
            v.tensor_copy(attn_t[:, :, :].rearrange("p a g -> p (a g)"), k.ps[0][:, :]).then_inc(mid, 1)
            dve.wait_ge(mid_pe, 8)
            v.tensor_copy(mixed[:, :, :].rearrange("p a g -> p (a g)"), k.ps[1][:, :]).then_inc(mid, 1)
            dve.wait_ge(mid_pe, 9)
            for a in range(2):
                v.tensor_copy(v2[:, 2 * a:2 * a + 2, :].rearrange("p a c -> p (a c)"), k.ps[2 + a][:, :]).then_inc(mid, 1)
            me(dve, v.tensor_tensor(k.res[:, :, :], k.res[:, :, :], b_out[:, :].rearrange("p (a c) -> p a c", a=1).to_broadcast([P, NT, C]), ALU.add))
            for t in range(NT):
                dve.wait_ge(result, t + 1)
                v.tensor_tensor(k.res[:, t, :], k.res[:, t, :], k.ps[t % 8][0:P, 0:C], ALU.add).then_inc(joined, 1)


def build(nc, out, **arrays):
    ctx = ExitStack()
    with ctx:
        k = Kernel(nc, ctx, out, arrays)
        setup(k)
        k.open_layer()
        with ExitStack() as gat:
            k.adst_e = k.sb("adst_e", [EP, ET, H], F32, gat)
            k.slots = rows_slots(k, "gat", XW, range(1), gat)
            with ExitStack() as projecting:
                k.xh = k.sb("xh", [P, NT, RW], F32, projecting)
                first_phase(k)
                spread_phase(k)
            k.slots += rows_slots(k, "gat", XW, range(1, R), gat)
            edge_phase(k, "gat", k.xh_tab, True, here=1)
        with ExitStack() as gat:
            k.xh = k.sb("xh_back", [P, NT, RW], F32, gat)
            k.mains, k.mains_in = k.sb("gat_mains", [P, NT, RW], F32, gat), k.gather_sem("gat_mains_in")
            chain_phase(k, "gat", True)
            gat_node_phase(k)
        k.close_layer()
        k.open_layer()
        router_phase(k)
        with ExitStack() as moe:
            k.w1, k.w3 = ([k.sb(f"{n}_{part}", [128, 2, NE, HW], F32R, moe) for part in ("high", "low")] for n in ("w1", "w3"))
            k.w2 = [k.sb(f"w2_{part}", [128, -(-HW // 128), NE, C], F32R, moe) for part in ("high", "low")]
            for a in range(2):
                weights_phase(k, a)
                experts_phase(k, a)
        k.att = {n: k.sb(f"att_{n}", s) for n, s in (
            ("w_fx", [128, 2, HG]), ("w_out", [128, NP, C]), ("w_comb", [128, 2, HG]), ("diag", [128, 128]),
            ("square", [128, 4, 128]),
            ("b_fx", [1, HG]), ("bias", [P, HG]), ("b_out", [P, C]), ("w_x", [128, 2, HG]), ("b_x", [128, NP]),
            ("b_slice", [1, H, HD]), ("temp", [1, H]), ("temp_b", [128, H]))}
        k.att_in = [ctx.enter_context(nc.semaphore(f"att_{n}_in")) for n in ("squares", "w", "small", "b_out")]
        combine_phase(k)
        k.close_layer()
        k.open_layer()
        with ExitStack() as gnn:
            k.slots = rows_slots(k, "gnn", C, range(R), gnn)
            edge_phase(k, "gnn", k.xn_tab, False, here=0)
        with ExitStack() as gnn:
            k.mains, k.mains_in = k.sb("gnn_mains", [P, NT, RW], F32, gnn), k.gather_sem("gnn_mains_in")
            chain_phase(k, "gnn", False)
            gnn_node_phase(k)
        attention_phase(k)
        k.close_layer()


_INS = ['x','src','dst','L0_gnn_W','L0_gnn_att_src','L0_gnn_att_dst','L0_gnn_bias','L0_gnn_gamma','L0_gnn_beta','L0_ffn_router_w','L0_ffn_w1','L0_ffn_w2','L0_ffn_w3','L1_gnn_W','L1_gnn_b','L1_ffn_W_fx','L1_ffn_b_fx','L1_ffn_W_x','L1_ffn_b_x','L1_ffn_W_slice','L1_ffn_b_slice','L1_ffn_W_q','L1_ffn_W_k','L1_ffn_W_v','L1_ffn_W_out','L1_ffn_b_out','L1_ffn_temperature']


def kernel(**inputs):
    import numpy as _np
    import concourse.bacc as _bacc
    from concourse import mybir as _mybir
    from concourse.bass_utils import run_bass_kernel_spmd as _run

    nc = _bacc.Bacc("TRN2", target_bir_lowering=False, num_devices=1)
    arrays, args = {}, {}
    for name in _INS:
        a = _np.ascontiguousarray(inputs[name])
        arrays[f"in_{name}_dram"] = a
        args[name] = nc.dram_tensor(f"in_{name}_dram", a.shape, _mybir.dt.from_np(a.dtype), kind="ExternalInput").ap()
    out = nc.dram_tensor("out_0_dram", (3125, 256), _mybir.dt.float32, kind="ExternalOutput").ap()
    build(nc, out, **args)
    r = _run(nc, [arrays], core_ids=[0])
    return r.results[0]["out_0_dram"]
```
